# Optimizing a Trainium2 kernel written in Bass

```python
import numpy as np
import jax
import jax.numpy as jnp

def _softmax(x, axis=-1):
    return jax.nn.softmax(x, axis=axis)
def _gelu(x):
    return jax.nn.gelu(x, approximate=True)
def _silu(x):
    return jax.nn.silu(x)
def _sigmoid(x):
    return jax.nn.sigmoid(x)
def _layernorm(x, axis=-1, eps=1e-5):
    m = jnp.mean(x, axis=axis, keepdims=True)
    v = jnp.var(x, axis=axis, keepdims=True)
    return (x - m) / jnp.sqrt(v + eps)
def _scatter_add(tgt, idx, src, axis=0):
    return tgt.at[idx].add(src)
def _segment_sum(src, seg, n):
    return jax.ops.segment_sum(src, seg, n)

kernel_name = 'mk_conv_preact_d4_conv_nhwc64_7087e1'

def setup_inputs(seed: int = 0):
    np.random.seed(seed)
    _w = jnp.asarray
    def _rec_inputs():
        import jax
        import jax.numpy as jnp
        _gk = jax.random.key(seed)
        x = -0.000125 + 0.9999 * jax.random.normal(jax.random.fold_in(_gk, 1), (8, 256, 256, 64), jnp.float32)
        return x
    x = _rec_inputs()
    def _L0_conv_setup():
        import jax, jax.numpy as jnp
        import numpy as np
        LEVEL = 2

        def cdf53_fwd_1d(x, axis):
            N = x.shape[axis]
            even = jnp.take(x, jnp.arange(0, N, 2), axis=axis)
            odd = jnp.take(x, jnp.arange(1, N, 2), axis=axis)
            e_next = jnp.roll(even, -1, axis=axis)
            d = odd - 0.5 * (even + e_next)
            d_prev = jnp.roll(d, 1, axis=axis)
            s = even + 0.25 * (d + d_prev)
            return (s, d)

        def cdf53_inv_1d(s, d, axis):
            d_prev = jnp.roll(d, 1, axis=axis)
            e = s - 0.25 * (d + d_prev)
            e_next = jnp.roll(e, -1, axis=axis)
            o = d + 0.5 * (e + e_next)
            shape = list(s.shape)
            shape[axis] *= 2
            out = jnp.zeros(shape, dtype=s.dtype)
            sl_e = [slice(None)] * len(shape)
            sl_e[axis] = slice(0, shape[axis], 2)
            sl_o = [slice(None)] * len(shape)
            sl_o[axis] = slice(1, shape[axis], 2)
            out = out.at[tuple(sl_e)].set(e)
            out = out.at[tuple(sl_o)].set(o)
            return out

        def lifting_step_fwd(x):
            l_row, h_row = cdf53_fwd_1d(x, axis=2)
            ll, lh = cdf53_fwd_1d(l_row, axis=1)
            hl, hh = cdf53_fwd_1d(h_row, axis=1)
            return (ll, lh, hl, hh)

        def lifting_step_inv(ll, lh, hl, hh):
            l_row = cdf53_inv_1d(ll, lh, axis=1)
            h_row = cdf53_inv_1d(hl, hh, axis=1)
            return cdf53_inv_1d(l_row, h_row, axis=2)
        key = jax.random.key(seed)
        kx, ka, kd, kk = jax.random.split(key, 4)
        B, H, W, Cin, Cout = (8, 256, 256, 64, 64)
        x = jax.random.normal(kx, (B, H, W, Cin), dtype=jnp.float32)
        w_approx = jax.random.normal(ka, (Cin, Cout, 1, 1), dtype=jnp.float32) / np.sqrt(Cin)
        w_detail = jax.random.normal(kd, (Cin, Cout, 3), dtype=jnp.float32) / np.sqrt(Cin * 3)
        dense_kernel = jax.random.normal(kk, (Cin, Cout), dtype=jnp.float32) / np.sqrt(Cin)
        dense_bias = jnp.zeros((Cout,), dtype=jnp.float32)
        return {'x': x, 'w_approx': w_approx, 'w_detail': w_detail, 'dense_kernel': dense_kernel, 'dense_bias': dense_bias}
    _L0_conv_all = _L0_conv_setup()
    _L0_conv_in = {k: v for k, v in _L0_conv_all.items() if k in ('w_approx', 'w_detail', 'dense_kernel', 'dense_bias', )}
    del _L0_conv_all

    def _L1_conv_setup():
        import jax, jax.numpy as jnp
        import numpy as np
        IN_CH = 64
        OUT_CH = 64
        MODES = 16
        BATCH, H, W = (16, 128, 128)
        key = jax.random.key(seed)
        k1, k2, k3 = jax.random.split(key, 3)
        scale = 1.0 / (IN_CH * OUT_CH)
        x = jax.random.normal(k1, (BATCH, H, W, IN_CH), dtype=jnp.float32)
        weights_real = (scale * jax.random.normal(k2, (IN_CH, OUT_CH, MODES, MODES))).astype(jnp.float32)
        weights_imag = (scale * jax.random.normal(k3, (IN_CH, OUT_CH, MODES, MODES))).astype(jnp.float32)
        return {'x': x, 'weights_real': weights_real, 'weights_imag': weights_imag}
    _L1_conv_all = _L1_conv_setup()
    _L1_conv_in = {k: v for k, v in _L1_conv_all.items() if k in ('weights_real', 'weights_imag', )}
    del _L1_conv_all

    def _L2_conv_setup():
        import jax, jax.numpy as jnp
        import numpy as np
        K_TOKENS = 512
        LATENT_DIM = 64

        def _nearest_indices(xf, codebook):
            d = jnp.sum(xf * xf, axis=-1, keepdims=True) - 2.0 * (xf @ codebook.T) + jnp.sum(codebook * codebook, axis=-1)
            return jnp.argmin(d, axis=-1)
        key = jax.random.key(seed)
        k1, k2 = jax.random.split(key)
        x = jax.random.normal(k1, (32, 64, 64, 64), dtype=jnp.float32)
        limit = float(np.sqrt(6.0 / (K_TOKENS + LATENT_DIM)))
        codebook = jax.random.uniform(k2, (K_TOKENS, LATENT_DIM), minval=-limit, maxval=limit, dtype=jnp.float32)
        return {'x': x, 'codebook': codebook}
    _L2_conv_all = _L2_conv_setup()
    _L2_conv_in = {k: v for k, v in _L2_conv_all.items() if k in ('codebook', )}
    del _L2_conv_all

    def _L3_conv_setup():
        import jax, jax.numpy as jnp
        import numpy as np
        key = jax.random.key(seed)
        k1, k2, k3 = jax.random.split(key, 3)
        B, H, W, C = (8, 256, 256, 64)
        O, KH, KW = (64, 3, 3)
        x = jax.random.normal(k1, (B, H, W, C), dtype=jnp.float32)
        kernel = jax.random.uniform(k2, (O, C, KH, KW), dtype=jnp.float32, minval=-0.05, maxval=0.05)
        bias = jax.random.normal(k3, (O, 1, 1), dtype=jnp.float32) * 0.01
        return {'x': x, 'kernel': kernel, 'bias': bias}
    _L3_conv_all = _L3_conv_setup()
    _L3_conv_in = {k: v for k, v in _L3_conv_all.items() if k in ('kernel', 'bias', )}
    del _L3_conv_all

    return {
        "x": x,
        "L0_conv_w_approx": _L0_conv_in["w_approx"],
        "L0_conv_w_detail": _L0_conv_in["w_detail"],
        "L0_conv_dense_kernel": _L0_conv_in["dense_kernel"],
        "L0_conv_dense_bias": _L0_conv_in["dense_bias"],
        "L1_conv_weights_real": _L1_conv_in["weights_real"],
        "L1_conv_weights_imag": _L1_conv_in["weights_imag"],
        "L2_conv_codebook": _L2_conv_in["codebook"],
        "L3_conv_kernel": _L3_conv_in["kernel"],
        "L3_conv_bias": _L3_conv_in["bias"],
    }

def reference(x, L0_conv_w_approx, L0_conv_w_detail, L0_conv_dense_kernel, L0_conv_dense_bias, L1_conv_weights_real, L1_conv_weights_imag, L2_conv_codebook, L3_conv_kernel, L3_conv_bias):
    import jax
    import jax.numpy as jnp
    def _L0_conv_ref(x, w_approx, w_detail, dense_kernel, dense_bias):
        import jax, jax.numpy as jnp
        import numpy as np
        LEVEL = 2

        def cdf53_fwd_1d(x, axis):
            N = x.shape[axis]
            even = jnp.take(x, jnp.arange(0, N, 2), axis=axis)
            odd = jnp.take(x, jnp.arange(1, N, 2), axis=axis)
            e_next = jnp.roll(even, -1, axis=axis)
            d = odd - 0.5 * (even + e_next)
            d_prev = jnp.roll(d, 1, axis=axis)
            s = even + 0.25 * (d + d_prev)
            return (s, d)

        def cdf53_inv_1d(s, d, axis):
            d_prev = jnp.roll(d, 1, axis=axis)
            e = s - 0.25 * (d + d_prev)
            e_next = jnp.roll(e, -1, axis=axis)
            o = d + 0.5 * (e + e_next)
            shape = list(s.shape)
            shape[axis] *= 2
            out = jnp.zeros(shape, dtype=s.dtype)
            sl_e = [slice(None)] * len(shape)
            sl_e[axis] = slice(0, shape[axis], 2)
            sl_o = [slice(None)] * len(shape)
            sl_o[axis] = slice(1, shape[axis], 2)
            out = out.at[tuple(sl_e)].set(e)
            out = out.at[tuple(sl_o)].set(o)
            return out

        def lifting_step_fwd(x):
            l_row, h_row = cdf53_fwd_1d(x, axis=2)
            ll, lh = cdf53_fwd_1d(l_row, axis=1)
            hl, hh = cdf53_fwd_1d(h_row, axis=1)
            return (ll, lh, hl, hh)

        def lifting_step_inv(ll, lh, hl, hh):
            l_row = cdf53_inv_1d(ll, lh, axis=1)
            h_row = cdf53_inv_1d(hl, hh, axis=1)
            return cdf53_inv_1d(l_row, h_row, axis=2)
        out_ch = w_approx.shape[1]
        details = []
        curr = x
        for _ in range(LEVEL):
            ll, lh, hl, hh = lifting_step_fwd(curr)
            details.append((lh, hl, hh))
            curr = ll
        ll_out = jnp.einsum('bhwi,ioxy->bhwo', curr, w_approx)
        lh_deep, hl_deep, hh_deep = details[-1]
        lh_out = jnp.einsum('bhwc,co->bhwo', lh_deep, w_detail[..., 0])
        hl_out = jnp.einsum('bhwc,co->bhwo', hl_deep, w_detail[..., 1])
        hh_out = jnp.einsum('bhwc,co->bhwo', hh_deep, w_detail[..., 2])
        new_details = []
        for i in range(LEVEL - 1):
            B, Hh, Ww, _ = details[i][0].shape
            z = jnp.zeros((B, Hh, Ww, out_ch), dtype=ll_out.dtype)
            new_details.append((z, z, z))
        new_details.append((lh_out, hl_out, hh_out))
        curr = ll_out
        for i in reversed(range(LEVEL)):
            lh, hl, hh = new_details[i]
            curr = lifting_step_inv(curr, lh, hl, hh)
        res = jnp.einsum('bhwi,io->bhwo', x, dense_kernel) + dense_bias
        return jax.nn.gelu(curr + res)

    def _L1_conv_ref(x, weights_real, weights_imag):
        import jax, jax.numpy as jnp
        import numpy as np
        IN_CH = 64
        OUT_CH = 64
        MODES = 16
        BATCH, H, W = (16, 128, 128)
        b, h, w, _ = x.shape
        modes = weights_real.shape[-1]
        out_ch = weights_real.shape[1]
        xc = jnp.transpose(x, (0, 3, 1, 2))
        x_ft = jnp.fft.rfft2(xc, norm='ortho')
        Wc = (weights_real + 1j * weights_imag).astype(jnp.complex64)
        out_modes = jnp.einsum('bixy,ioxy->boxy', x_ft[:, :, :modes, :modes], Wc)
        out_ft = jnp.zeros((b, out_ch, h, w // 2 + 1), dtype=jnp.complex64)
        out_ft = out_ft.at[:, :, :modes, :modes].set(out_modes)
        y = jnp.fft.irfft2(out_ft, s=(h, w), norm='ortho')
        return jnp.transpose(y, (0, 2, 3, 1))

    def _L2_conv_ref(x, codebook):
        import jax, jax.numpy as jnp
        import numpy as np
        K_TOKENS = 512
        LATENT_DIM = 64

        def _nearest_indices(xf, codebook):
            d = jnp.sum(xf * xf, axis=-1, keepdims=True) - 2.0 * (xf @ codebook.T) + jnp.sum(codebook * codebook, axis=-1)
            return jnp.argmin(d, axis=-1)
        xf = x.reshape(-1, x.shape[-1])
        idx = _nearest_indices(xf, codebook)
        codes = codebook[idx].reshape(x.shape)
        return codes

    def _L3_conv_ref(x, kernel, bias):
        import jax, jax.numpy as jnp
        import numpy as np
        B, H, W, C = x.shape
        O, I, kh, kw = kernel.shape
        p = (kh - 1) // 2
        Hp, Wp = (H + 2 * p, W + 2 * p)
        xi = jnp.transpose(x, (0, 3, 1, 2))
        xf = jnp.fft.rfft2(xi, s=(Hp, Wp))
        kf = jnp.fft.rfft2(kernel, s=(Hp, Wp))
        of = jnp.einsum('bihw,oihw->bohw', xf, kf)
        out = jnp.fft.irfft2(of, s=(Hp, Wp))
        out = jnp.roll(out, shift=(2 * p, 2 * p), axis=(-2, -1))
        out = out[:, :, p:p + H, p:p + W]
        out = out + bias
        return jnp.transpose(out, (0, 2, 3, 1))

    def _gn(v, G=32, eps=1e-5):
        B_, H_, W_, C_ = v.shape
        g = v.reshape(B_, H_, W_, G, C_ // G)
        m = jnp.mean(g, axis=(1, 2, 4), keepdims=True)
        s = jnp.var(g, axis=(1, 2, 4), keepdims=True)
        return ((g - m) / jnp.sqrt(s + eps)).reshape(v.shape)

    def _ln_c(v, eps=1e-6):
        m = jnp.mean(v, axis=-1, keepdims=True)
        s = jnp.var(v, axis=-1, keepdims=True)
        return (v - m) / jnp.sqrt(s + eps)

    def _ln_t(v, eps=1e-5):
        m = jnp.mean(v, axis=-1, keepdims=True)
        s = jnp.var(v, axis=-1, keepdims=True)
        return (v - m) / jnp.sqrt(s + eps)

    def _to_tokens(v):
        B_, H_, W_, C_ = v.shape
        return v.reshape(B_, H_ * W_, C_)
    def _from_tokens(t, like):
        return t.reshape(like.shape)

    x = x + _L0_conv_ref(_gn(x), L0_conv_w_approx, L0_conv_w_detail, L0_conv_dense_kernel, L0_conv_dense_bias)
    x = x + _L1_conv_ref(_gn(x), L1_conv_weights_real, L1_conv_weights_imag)
    x = x + _L2_conv_ref(_gn(x), L2_conv_codebook)
    x = x + _L3_conv_ref(_gn(x), L3_conv_kernel, L3_conv_bias)
    return x


_drawn_inputs = setup_inputs


def setup_inputs(seed=0):
    import zlib

    import numpy as np

    out = dict(_drawn_inputs(seed))
    spreads = {'L0_conv_dense_bias': (0.0, 0.1)}
    factors = {'L1_conv_weights_real': 200.0, 'L1_conv_weights_imag': 200.0, 'L3_conv_bias': 8.0}
    for name, (base, spread) in spreads.items():
        noise = np.random.default_rng([zlib.crc32(name.encode()), seed]).standard_normal(out[name].shape)
        drawn = base * np.exp(spread * noise) if base else spread * noise
        out[name] = jnp.asarray(drawn.astype(out[name].dtype))
    for name, factor in factors.items():
        out[name] = (out[name] * factor).astype(out[name].dtype)
    return out
```

```python
from contextlib import ExitStack

import concourse.bass as bass
import numpy as np
from concourse import mybir

F32 = mybir.dt.float32
F16 = mybir.dt.float16
ALU = mybir.AluOpType
ACT = mybir.ActivationFunctionType
AX = mybir.AxisListType
ds = bass.ds

C = 64
W = 256
P = 128
PAIR = 2 * P
MODES = 16
NCODE = 512
CSCALE = 64.0
SHARP = 2.0 ** 50
EPS = 1e-5
ENGINES = 5
PHASES = 7


def fused_layers(nc, x, dense, dense_bias, mix_low, mix_high, modes, codes, codes_t, conv, conv_bias,
                 ident, group, w_analysis, w_synthesis, dft_w, dft_h, idft_h, idft_w, out):
    B = x.shape[0]
    NPX = P * PAIR
    ctx = ExitStack()
    with ctx:
        def sb(name, shape, dt=F32):
            return ctx.enter_context(nc.sbuf_tensor(name, shape, dt))

        def sem(name):
            return ctx.enter_context(nc.semaphore(name))

        X = sb("X", [P, NPX + PAIR])
        R1 = sb("R1", [P, 129 * C])
        SCR = sb("SCR", [P, 7680])
        id32 = sb("id32", [P, P])
        id16 = sb("id16", [P, P], F16)
        grp = sb("grp", [P, P])
        wan = sb("wan", [P, 2, P])
        wsy = sb("wsy", [P, 2 * P])
        dn = sb("dn", [P, P])
        dnf = sb("dnf", [P, P])
        mixw = sb("mixw", [P, 2, P])
        dfw = sb("dfw", [P, 2, 32])
        dfh = sb("dfh", [P, 4, 32])
        idh = sb("idh", [32, W])
        idw = sb("idw", [32, 2 * P])
        dbias = sb("dbias", [P, 1])
        cbias = sb("cbias", [P, 1])
        code_top = sb("code_top", [P, NCODE], F16)
        code_low = sb("code_low", [P, NCODE], F16)
        code_hi = sb("code_hi", [P, 4, C], F16)
        code_lo = sb("code_lo", [P, 4, C], F16)
        conv_hi = sb("conv_hi", [P, 6, P], F16)
        conv_lo = sb("conv_lo", [P, 6, P], F16)
        bnst = sb("bnst", [P, 64 * 6])
        agg = sb("agg", [P, 2])
        tiny = sb("tiny", [P, 12])
        negmax = sb("negmax", [P, 2, 2])
        negsharp = sb("negsharp", [P, 2, 2])
        dev, e2, var, sd, y0, y2, y3, rs, nb, fb = (tiny[:, i:i + 1] for i in range(10))
        nbl = sb("nbl", [P, 1])
        nbd = sb("nbd", [P, 1])

        PS = ctx.enter_context(nc.psum_tensor("PS", [P, 8 * 512], F32))

        def bank(i, n=1):
            return PS[:, i * 512:(i + n) * 512]

        mg = bank(7)[:, 0:1]

        T = [SCR[:, u * 2432:(u + 1) * 2432].rearrange("p (j r c) -> p j r c", j=2, c=C) for u in range(2)]
        ta = SCR[:, 4864:5888].rearrange("p (j k c) -> p j k c", j=2, c=C)
        tb = SCR[:, 5888:6912].rearrange("p (j k c) -> p j k c", j=2, c=C)
        Bc = R1[:, 0:P * C]
        Bv = Bc.rearrange("p (k t c) -> p k t c", t=2, c=C)
        lift = SCR[:, 0:4096].rearrange("p (k c) -> p k c", c=C)
        mst = [SCR[:, 4096 + 512 * u:4608 + 512 * u] for u in range(2)]
        mbt = [SCR[:, 5120 + 512 * u:5632 + 512 * u].rearrange("p (m n) -> p m n", n=P) for u in range(2)]
        AF = SCR[:, 0:4096].rearrange("p (k s) -> p k s", s=32)
        syn = [SCR[:, 4096 + 512 * u:4608 + 512 * u].rearrange("p (k q o) -> p k q o", q=2, o=C) for u in range(2)]
        x1b = [SCR[:, 5120 + 512 * u:5632 + 512 * u] for u in range(2)]
        x1t = [SCR[:, 6656 + 512 * u:7168 + 512 * u].rearrange("p (n m) -> p n m", m=P) for u in range(2)]
        aft = [SCR[:, 4096 + 512 * u:4608 + 512 * u].rearrange("p (n m) -> p n m", m=P) for u in range(2)]
        DV = SCR[:, 5120:5632].rearrange("p (t n) -> p t n", t=2)
        om = SCR[0:C, 5632:6144].rearrange("p (y n t) -> p y n t", n=16, t=2)
        om2 = SCR[0:C, 6144:6656].rearrange("p (y n t) -> p y n t", n=16, t=2)
        OT = SCR[0:32, 0:2048].rearrange("p (o s y) -> p o s y", s=2, y=MODES)
        WM = [R1[:, 2048 * u:2048 * (u + 1)].rearrange("p (n o) -> p n o", o=C) for u in range(2)]
        Z = [R1[0:32, 4096 * u:4096 * (u + 1)].rearrange("p (h o) -> p h o", o=C) for u in range(2)]
        R1h = R1[:, 0:8192].bitcast(F16)
        SCRh = SCR[:, :].bitcast(F16)
        XH = [R1h[:, 1024 * u:1024 * (u + 1)] for u in range(2)]
        XL = [R1h[:, 2048 + 1024 * u:3072 + 1024 * u] for u in range(2)]
        XN = [R1[:, 2048 + 1024 * u:3072 + 1024 * u] for u in range(2)]
        HQ = [[R1h[:, 8192 + 2048 * u + 1024 * q:9216 + 2048 * u + 1024 * q] for q in range(2)] for u in range(2)]
        LQ = [[SCRh[:, 2048 * u + 1024 * q:2048 * u + 1024 * q + 1024] for q in range(2)] for u in range(2)]
        OH = [SCRh[:, 4096 + 512 * i:4608 + 512 * i] for i in range(4)]
        OTs = [SCRh[:, 6144 + 2048 * i:8192 + 2048 * i].rearrange("p (k n) -> p k n", k=4) for i in range(2)]
        NH = [R1h[:, 2340 * u:2340 * (u + 1)].rearrange("p (k j n) -> p k j n", j=2, n=130) for u in range(2)]
        NL = [R1h[:, 4680 + 2340 * u:7020 + 2340 * u].rearrange("p (k j n) -> p k j n", j=2, n=130) for u in range(2)]
        XM = R1[:, 4680:6728].rearrange("p (k n) -> p k n", n=P)
        res = [SCR[:, 512 * i:512 * (i + 1)] for i in range(4)]
        ost = [SCR[:, 2048 + 2048 * u:4096 + 2048 * u].rearrange("p (r j o) -> p r j o", j=2, o=C) for u in range(2)]
        edge = SCR[:, 6144:6400]
        edge_t = SCR[:, 6400:6528]

        s_const = sem("constants_loaded")
        s_prep = sem("weights_prepared")
        s_bar = sem("phase_barrier")
        s_past = sem("waits_taken")
        s_st = sem("statistics_step")
        s_tile = [sem(f"tile_loaded{u}") for u in range(2)]
        s_tp = sem("tile_transposed")
        s_xin = sem("x_written")
        s_padd = sem("row_sums_added")
        s_dl = sem("row_filter_link")
        s_s1 = sem("low_rows_ready")
        s_wa = sem("columns_analysed")
        s_wb = sem("coefficients_stored")
        s_lf = sem("lifting_link")
        s_mc = sem("mix_staged")
        s_mt = sem("mix_transposed")
        s_mb = sem("mix_normalised")
        s_mm = sem("mix_multiplied")
        s_mo = sem("mix_stored")
        s_fold = sem("dense_bias_product_ready")
        s_folded = sem("dense_folded")
        s_sy = sem("synthesis_rows_ready")
        s_l0 = sem("layer0_product_ready")
        s_g = sem("gelu_ready")
        s_x1 = sem("x1_ready")
        s_x1n = sem("x1_measured")
        s_xt = sem("x1_transposed")
        s_xtc = sem("x1_transpose_copied")
        s_fa = sem("row_dft_ready")
        s_fac = sem("row_dft_stored")
        s_at = sem("row_dft_transposed")
        s_atc = sem("row_dft_transpose_copied")
        s_fg = sem("image_dft_ready")
        s_dv = sem("mode_vectors_ready")
        s_wm = [sem(f"mode_weights_loaded{u}") for u in range(2)]
        s_om = sem("modes_mixed")
        s_oms = sem("mixed_modes_copied")
        s_ot = sem("mixed_modes_transposed")
        s_zp = sem("column_synthesis_ready")
        s_zc = sem("column_synthesis_stored")
        s_yp = sem("layer1_output_ready")
        s_x2 = sem("x2_written")
        s_xh = sem("x_high_ready")
        s_xn = sem("x_normalised")
        s_xl = sem("x_low_ready")
        s_hl = [sem(f"halves_placed{u}") for u in range(2)]
        s_sc = sem("scores_ready")
        s_mx = sem("maximum_ready")
        s_mxs = sem("maximum_scaled")
        s_oh = sem("one_hots_ready")
        s_oht = sem("one_hots_transposed")
        s_ocd = sem("even_one_hots_copied")
        s_oca = sem("odd_one_hots_copied")
        s_cd = sem("codes_looked_up")
        s_x3 = sem("x3_written")
        s_nh = sem("conv_high_ready")
        s_nn = sem("conv_normalised")
        s_nl = sem("conv_low_ready")
        s_cp = sem("conv_edges_ready")
        s_pad = sem("conv_padding_cleared")
        s_cv = sem("conv_ready")
        s_rs = sem("conv_residual_added")
        s_ct = sem("output_transposed")
        s_oc = sem("output_copied")
        s_out = [sem(f"output_stored{u}") for u in range(2)]
        s_e = sem("row0_step")
        s_eout = sem("row0_stored")

        block = ctx.enter_context(nc.Block())

        x_cols = x.rearrange("b h (p j) c -> b j p h c", j=2)
        o_rows = out.rearrange("b h (p j) c -> b p h (j c)", j=2)

        ct32 = SCR[:, 0:NCODE]
        c32 = SCR[:, 512:768].rearrange("p (k c) -> p k c", c=C)
        cv32 = SCR[:, 1024:1792].rearrange("p (k n) -> p k n", n=P)
        sq = SCR[0:C, 2048:2560]
        hi16 = SCR[:, 2560:2816].bitcast(F16)
        neghalf = SCR[0:C, 3072:3073]
        bias_row = SCR[0:1, 3200:3712]
        row16 = SCR[0:1, 3712:4224].bitcast(F16)
        CONSTS = [(id32[:], ident), (grp[:], group), (wan[:], w_analysis), (wsy[:], w_synthesis),
                  (dn[:], dense), (mixw[:, 0, :], mix_low), (mixw[:, 1, :], mix_high), (dfw[:], dft_w),
                  (dfh[:], dft_h), (idh[:], idft_h), (idw[:], idft_w), (dbias[:], dense_bias),
                  (cbias[:], conv_bias), (ct32, codes_t), (c32, codes), (cv32, conv)]
        CHUNKS = 16
        NST = 12

        def st_base(b, layer):
            return (b * 4 + layer) * NST

        def past(eng):
            eng.sem_inc(s_past, 1)

        def barrier(eng, b, n):
            past(eng)
            eng.drain().then_inc(s_bar, 1)
            eng.wait_ge(s_bar, (b * PHASES + n + 1) * ENGINES)
            past(eng)

        @block.sync
        def _(sp):
            for u in range(2):
                sp.sem_inc(s_out[u], 32)
            for dst, src in CONSTS:
                sp.dma_start(dst, src).then_inc(s_const, 16)
            sp.wait_ge(s_prep, 13)
            sp.dma_start(code_top[C:C + 1, :], row16[:, 0:NCODE]).then_inc(s_const, 16)
            sp.dma_start(code_top[C + 1:C + 2, :], row16[:, NCODE:2 * NCODE]).then_inc(s_const, 16)
            sp.wait_ge(s_const, 16 * (len(CONSTS) + 2))
            with sp.Fori(0, B) as b:
                def around(ci):
                    if isinstance(ci, int):
                        return 16 * ci, (16 * ci + 254) % 256, (16 * ci + 16) % 256
                    return sp.snap(16 * ci), sp.snap((16 * ci + 254) % 256), sp.snap((16 * ci + 16) % 256)

                def load(rows, u):
                    main, above, below = rows
                    for j in range(2):
                        src = x_cols[b, j]
                        sp.dma_start(T[u][:, j, 2:18, :], src[:, ds(main, 16), :]).then_inc(s_tile[u], 16)
                        sp.dma_start(T[u][:, j, 0:2, :], src[:, ds(above, 2), :]).then_inc(s_tile[u], 16)
                        sp.dma_start(T[u][:, j, 18:19, :], src[:, ds(below, 1), :]).then_inc(s_tile[u], 16)

                load(around(0), 0)
                load(around(1), 1)
                with sp.Fori(0, 7) as c2:
                    for u in range(2):
                        n = b * CHUNKS + 2 * c2 + u
                        rows = around(2 * c2 + u + 2)
                        sp.wait_ge(s_wa, n + 2)
                        load(rows, u)
                barrier(sp, b, 0)
                barrier(sp, b, 1)
                barrier(sp, b, 2)
                sp.dma_start(WM[0], modes[:, 0:32, :]).then_inc(s_wm[0], 16)
                sp.dma_start(WM[1], modes[:, 32:64, :]).then_inc(s_wm[1], 16)
                with sp.Fori(0, 3) as i:
                    for u in range(2):
                        sp.wait_ge(s_om, b * 8 + 2 * i + u + 1)
                        sp.dma_start(WM[u], modes[:, ds((2 * i + u + 2) * 32, 32), :]).then_inc(s_wm[u], 16)
                barrier(sp, b, 3)
                barrier(sp, b, 4)

                def place(n, u):
                    sp.wait_ge(s_xl, n + 1)
                    for q in range(2):
                        rows = slice(C * q, C * q + C)
                        sp.dma_start(HQ[u][q][0:C, :], XH[u][rows, :]).then_inc(s_hl[u], 16)
                        sp.dma_start(LQ[u][q][C:P, :], XH[u][rows, :]).then_inc(s_hl[u], 16)
                        sp.dma_start(LQ[u][q][0:C, :], XL[u][rows, :]).then_inc(s_hl[u], 16)

                sp.wait_ge(s_pad, 2 * b + 1)
                place(b * 32, 0)
                place(b * 32 + 1, 1)
                with sp.Fori(0, 15) as i:
                    for u in range(2):
                        n = b * 32 + 2 * i + u
                        place(n + 2, u)
                barrier(sp, b, 5)

                def store(ci, u, halves):
                    sp.wait_ge(s_oc, 2 + (b * CHUNKS + ci + 1) * 4)
                    for r0, nr in halves:
                        sp.dma_start(o_rows[b][:, ds(16 * ci + 1 + r0, nr), :],
                                     ost[u][:, r0:r0 + nr, :, :].rearrange("p r j o -> p r (j o)")
                                     ).then_inc(s_out[u], 16)

                with sp.Fori(0, 7) as i:
                    for u in range(2):
                        store(2 * i + u, u, ((0, 8), (8, 8)))
                store(14, 0, ((0, 8), (8, 8)))
                store(15, 1, ((0, 8), (8, 7)))
                sp.wait_ge(s_e, b * 5 + 5)
                sp.dma_start(o_rows[b][:, 0:1, :], edge_t[:, :].rearrange("p (r n) -> p r n", r=1)).then_inc(s_eout, 16)
                sp.wait_ge(s_eout, 16 * (b + 1))
                for u in range(2):
                    sp.wait_ge(s_out[u], 32 + 256 * (b + 1))
                barrier(sp, b, 6)

        @block.tensor
        def _(pe):
            for free, count in ((s_wa, 1), (s_fg, 2), (s_xt, 2), (s_fa, 1), (s_yp, 1), (s_oht, 2), (s_cd, 2), (s_ct, 4), (s_cv, 4)):
                pe.sem_inc(free, count)
            pe.wait_ge(s_prep, 10)
            pe.matmul(bank(0)[0:1, :], neghalf, sq, start=True, stop=True).then_inc(s_prep, 1)
            pe.wait_ge(s_prep, 13)
            pe.wait_ge(s_const, 16 * (len(CONSTS) + 2))
            with pe.Fori(0, B) as b:
                def stats(layer):
                    base = st_base(b, layer)
                    pe.wait_ge(s_st, base + 1)
                    pe.matmul(bank(7)[:, 0:1], grp[:], agg[:, 0:1], start=True, stop=True).then_inc(s_st, 1)
                    pe.wait_ge(s_st, base + 4)
                    pe.matmul(bank(7)[:, 1:2], grp[:], e2, start=True, stop=True).then_inc(s_st, 1)

                with pe.Fori(0, 8) as c2:
                    for u in range(2):
                        c = b * CHUNKS + 2 * c2 + u
                        pe.wait_ge(s_tile[u], 96 * (b * 8 + c2 + 1))
                        for m in range(4):
                            pe.wait_ge(s_xin, c * 4 + m + 1)
                            for kk in range(2):
                                for j in range(2):
                                    r = 2 + 2 * (2 * m + kk)
                                    t = pe.transpose(bank(m % 2)[:, (2 * kk + j) * P:(2 * kk + j + 1) * P],
                                                     T[u][:, j, r:r + 2, :], id32[:])
                            t.then_inc(s_tp, 1)
                        pe.wait_ge(s_wb, c + 1)
                        for j in range(2):
                            pe.wait_ge(s_s1, c * 2 + j + 1)
                            t = pe.matmul(bank(2 + u), wan[:, j, :], tb[:, j, :, :], start=j == 0, stop=j == 1)
                        t.then_inc(s_wa, 1)
                barrier(pe, b, 0)
                stats(0)
                with pe.Fori(0, 8) as g:
                    for u in range(2):
                        n = b * 16 + 2 * g + u
                        pe.wait_ge(s_mc, n + 1)
                        pe.wait_ge(s_mo, n + 1)
                        for m in range(4):
                            t = pe.transpose(bank(u)[:, m * P:(m + 1) * P], mst[u][:, m * P:(m + 1) * P], id32[:])
                        t.then_inc(s_mt, 1)
                    for u in range(2):
                        n = b * 16 + 2 * g + u
                        pe.wait_ge(s_mb, n + 1)
                        for half in range(2):
                            for m in range(4):
                                t = pe.matmul(bank(2 + u)[half * C:(half + 1) * C, m * P:(m + 1) * P],
                                              mbt[u][:, m, half * C:(half + 1) * C], mixw[:, half, :],
                                              start=True, stop=True)
                        t.then_inc(s_mm, 1)
                pe.matmul(bank(7)[:, 2:3], dn[:], nb, start=True, stop=True).then_inc(s_fold, 1)
                barrier(pe, b, 1)

                def product(n, m, at):
                    if m % 2 == 0:
                        pe.wait_ge(s_sy, at[1] + 1)
                    pe.wait_ge(s_g, n + 1)
                    pe.matmul(bank(m), dnf[:], X[:, ds(at[0], 512)], start=True, stop=False, skip_group_check=True)
                    for i in range(2):
                        t = pe.matmul(bank(m)[:, i * 256:(i + 1) * 256], syn[m // 2][:, 2 * (m % 2) + i, :, :],
                                      wsy[:], start=False, stop=True, skip_group_check=True)
                    t.then_inc(s_l0, 1)

                def layer0_steps(c, last):
                    for m in range(4):
                        n = (b * CHUNKS + c) * 4 + m
                        pe.wait_ge(s_x1, n + 1)
                        pe.wait_ge(s_xtc, n + 1)
                        for i in range(4):
                            t = pe.transpose(bank(4 + m % 2)[:, i * P:(i + 1) * P],
                                             x1b[m % 2][:, i * P:(i + 1) * P], id32[:])
                        t.then_inc(s_xt, 1)
                        if not (last and m >= 2):
                            product(n + 2, (m + 2) % 4, (c * 2048 + (m + 2) * 512, (b * CHUNKS + c) * 2 + (m + 2) // 2))
                        pe.wait_ge(s_xtc, n + 3)
                        if m == 0:
                            pe.wait_ge(s_fac, b * CHUNKS + c + 1)
                        for kk in range(2):
                            for j in range(2):
                                t = pe.matmul(bank(6)[:, (2 * m + kk) * 32:(2 * m + kk + 1) * 32],
                                              x1t[m % 2][:, 2 * kk + j, :], dfw[:, j, :], start=j == 0, stop=j == 1)
                        t.then_inc(s_fa, 1)

                pe.wait_ge(s_folded, 2 * b + 2)
                for m in range(2):
                    product(b * 64 + m, m, (m * 512, b * 32))
                with pe.Fori(0, CHUNKS - 1) as c:
                    layer0_steps(c, False)
                layer0_steps(CHUNKS - 1, True)
                barrier(pe, b, 2)

                stats(1)
                for g in range(9):
                    if g < 8:
                        pe.wait_ge(s_atc, b * 8 + g + 1)
                        for i in range(4):
                            t = pe.transpose(bank(g % 2)[:, i * P:(i + 1) * P], AF[:, :, 4 * g + i], id32[:])
                        t.then_inc(s_at, 1)
                    if g == 0:
                        continue
                    pe.wait_ge(s_atc, b * 8 + g + 2)
                    for yy in range(2):
                        y = 2 * (g - 1) + yy
                        for half in range(2):
                            for q in range(2):
                                for part in range(2):
                                    t = pe.matmul(bank(2)[half * C:(half + 1) * C, y * 32:(y + 1) * 32],
                                                  aft[(g - 1) % 2][:, 2 * yy + part, q * C:(q + 1) * C],
                                                  dfh[:, 2 * q + part, :], start=q == 0 and part == 0,
                                                  stop=q == 1 and part == 1)
                    t.then_inc(s_fg, 1)
                pe.wait_ge(s_dv, b * 6 + 6)
                past(pe)
                for i in range(4):
                    for u in range(2):
                        pe.wait_ge(s_wm[u], 16 * (b * 4 + i + 1))
                        for md in range(32):
                            k = (2 * i + u) * 32 + md
                            t = pe.matmul(bank(3)[0:C, 2 * k:2 * k + 2], WM[u][:, md, :],
                                          DV[:, :, k:k + 1], start=True, stop=True)
                        t.then_inc(s_om, 1)
                pe.wait_ge(s_oms, b * 3 + 3)
                past(pe)
                for s, src in enumerate((om, om2)):
                    for y in range(MODES):
                        t = pe.transpose(bank(4 + 2 * s + y // 8)[0:32, (y % 8) * C:(y % 8 + 1) * C],
                                         src[:, y, :, :], id32[0:C, 0:C])
                t.then_inc(s_ot, 1)
                barrier(pe, b, 3)

                for zz in range(2):
                    for u in range(2):
                        z = b * 4 + 2 * zz + u
                        for g in range(8):
                            pe.wait_ge(s_zc, z * 8 + g + 1)
                            past(pe)
                            for o in range(8):
                                t = pe.matmul(bank(g % 2)[0:32, o * 64:(o + 1) * 64], OT[:, 8 * g + o, :, :],
                                              idh[:, 128 * zz + 64 * u:128 * zz + 64 * u + 64], start=True, stop=True)
                            t.then_inc(s_zp, 1)
                        pe.wait_ge(s_zc, z * 8 + 10)
                        for m in range(16):
                            pe.wait_ge(s_x2, z * 16 + m + 1)
                            for i in range(2):
                                r = 2 * (2 * m + i)
                                t = pe.matmul(bank(2 + m % 2)[:, i * 256:(i + 1) * 256], Z[u][:, r:r + 2, :],
                                              idw[:], start=True, stop=True)
                            t.then_inc(s_yp, 1)
                barrier(pe, b, 4)

                stats(2)

                def scores(n, u, h):
                    px, q, hh = h // 4, h // 2 % 2, h % 2
                    for t2 in range(2):
                        pix = slice(px * 512 + (2 * hh + t2) * P, px * 512 + (2 * hh + t2 + 1) * P)
                        dst = bank(2 * hh + t2)
                        pe.matmul(dst, LQ[u][q][:, pix], code_low[:], start=True, stop=False)
                        t = pe.matmul(dst, HQ[u][q][0:C + 2, pix], code_top[0:C + 2, :], start=False, stop=True)
                    t.then_inc(s_sc, 1)

                def layer2_chunks(i, last):
                    first, half_first, quarter_first = (b * 16 + i) * 16, (b * 16 + i) * 8, (b * 16 + i) * 4

                    def look_up(k):
                        q, px = k // 2 % 2, k // 4 % 2
                        pe.wait_ge(s_oca, half_first + k // 2 + 2)
                        pe.wait_ge(s_ocd, half_first + k // 2 + 2)
                        if q == 0:
                            pe.wait_ge(s_x3, quarter_first + k // 4 + 1)
                        dst = bank(6 + px)[q * C:(q + 1) * C, :]
                        for blk in range(4):
                            pe.matmul(dst, code_hi[:, blk, :], OTs[q][:, blk, :], start=blk == 0, stop=False)
                            t = pe.matmul(dst, code_lo[:, blk, :], OTs[q][:, blk, :], start=False, stop=blk == 3)
                        t.then_inc(s_cd, 1)

                    for k in range(16):
                        n, u, h, hh = first + k, k // 8, k % 8, k % 2
                        pe.wait_ge(s_oh, n + 1)
                        if not (last and k >= 14):
                            if h == 6:
                                pe.wait_ge(s_hl[1 - u], 96 * (b * 16 + i + 1 + u))
                            scores(n + 2, (k + 2) // 8 % 2, (h + 2) % 8)
                        pe.wait_ge(s_oca if hh else s_ocd, half_first + k // 2 + 1)
                        dst = bank(4 + hh).bitcast(F16).rearrange("p (k n) -> p k n", k=4)
                        for t2 in range(2):
                            for blk in range(4):
                                t = pe.transpose(dst[:, blk, t2 * P:(t2 + 1) * P],
                                                 OH[2 * hh + t2][:, blk * P:(blk + 1) * P], id16[:])
                        t.then_inc(s_oht, 1)
                        if k % 2 == 0 and k >= 2:
                            look_up(k - 2)
                    look_up(14)

                pe.wait_ge(s_hl[0], 96 * (b * 16 + 1))
                scores(b * 256, 0, 0)
                scores(b * 256 + 1, 0, 1)
                with pe.Fori(0, 15) as i:
                    layer2_chunks(i, False)
                layer2_chunks(15, True)
                barrier(pe, b, 5)

                stats(3)

                def conv_group(dst, u, kk0, count, j):
                    taps = [(tap, pr, w3, src) for tap in range(3) for pr in range(2)
                            for w3, src in ((conv_hi, NH), (conv_lo, NH), (conv_hi, NL))]
                    for i, (tap, pr, w3, src) in enumerate(taps):
                        col = j - (tap + 1)
                        jj = col % 2
                        p0 = 2 + (col - jj) // 2
                        t = pe.matmul(dst, w3[:, pr * 3 + tap, :], src[u][:, kk0 + pr:kk0 + pr + count, jj, p0:p0 + P],
                                      start=i == 0, stop=i == len(taps) - 1)
                    return t

                def turn(n, m):
                    pe.wait_ge(s_rs, n + 5)
                    pe.wait_ge(s_oc, n + 1)
                    for i in range(4):
                        t = pe.transpose(bank(4 + m % 2)[:, i * P:(i + 1) * P], res[m][:, i * P:(i + 1) * P], id32[:])
                    t.then_inc(s_ct, 1)

                with pe.Fori(0, 8) as i:
                    for u in range(2):
                        c = b * CHUNKS + 2 * i + u
                        pe.wait_ge(s_cp, b * 17 + 2 * i + u + 2)
                        for m in range(4):
                            pe.wait_ge(s_rs, c * 4 + m + 1)
                            conv_group(bank(m), u, 4 * (m // 2), 4, m % 2).then_inc(s_cv, 1)
                            if u or m:
                                turn(c * 4 + m - 1, (m - 1) % 4)
                    turn(c * 4 + 3, 3)
                pe.wait_ge(s_cp, b * 17 + 18)
                conv_group(bank(6)[:, 0:P], 0, 0, 1, 0)
                conv_group(bank(6)[:, P:2 * P], 0, 0, 1, 1).then_inc(s_e, 1)
                pe.wait_ge(s_e, b * 5 + 3)
                for j in range(2):
                    t = pe.transpose(bank(7)[:, j * P:(j + 1) * P], edge[:, j * P:(j + 1) * P], id32[:])
                t.then_inc(s_e, 1)
                barrier(pe, b, 6)

        @block.scalar
        def _(act):
            for free, count in ((s_xin, 2), (s_wb, 2), (s_mo, 2), (s_g, 4), (s_xtc, 2), (s_atc, 2), (s_zc, 2),
                                (s_oc, 2), (s_oca, 1)):
                act.sem_inc(free, count)
            act.wait_ge(s_const, 16 * len(CONSTS))
            with act.Fori(0, B) as b:
                def stats(layer):
                    base = st_base(b, layer)
                    act.wait_ge(s_st, base + 6)
                    act.activation(sd, var, ACT.Sqrt).then_inc(s_st, 1)

                with act.Fori(0, 8) as c2:
                    for u in range(2):
                        c = b * CHUNKS + 2 * c2 + u
                        for m in range(4):
                            act.wait_ge(s_tp, c * 4 + m + 1)
                            act.activation(X[:, ds((2 * c2 + u) * 2048 + m * 512, 512)], bank(m % 2),
                                           ACT.Copy).then_inc(s_xin, 1)
                        act.wait_ge(s_wa, c + 2)
                        act.activation(R1[:, ds((2 * c2 + u) * 512, 512)], bank(2 + u), ACT.Copy).then_inc(s_wb, 1)
                barrier(act, b, 0)
                stats(0)
                act.wait_ge(s_st, st_base(b, 0) + NST)
                act.wait_ge(s_folded, 2 * b + 1)
                with act.Fori(0, 8) as g:
                    for u in range(2):
                        n = b * 16 + 2 * g + u
                        act.wait_ge(s_mt, n + 1)
                        src = bank(u).rearrange("p (m n) -> p m n", n=P)
                        act.activation(mbt[u][:, :, 0:C], src[:, :, 0:C], ACT.Identity, bias=nbl[:], scale=rs)
                        act.activation(mbt[u][:, :, C:P], src[:, :, C:P], ACT.Copy, scale=rs).then_inc(s_mb, 1)
                    for u in range(2):
                        n = b * 16 + 2 * g + u
                        act.wait_ge(s_mm, n + 1)
                        act.activation(R1[:, ds((2 * g + u) * 512, 512)], bank(2 + u), ACT.Copy).then_inc(s_mo, 1)
                barrier(act, b, 1)

                def gelu(n, m):
                    act.wait_ge(s_l0, n + 1)
                    act.wait_ge(s_xt, n + 1)
                    act.wait_ge(s_x1n, n + 1)
                    act.activation(x1b[m % 2], bank(m), ACT.Gelu_apprx_tanh, bias=fb).then_inc(s_g, 1)

                def copies(c, last):
                    for m in range(4):
                        n = (b * CHUNKS + c) * 4 + m
                        if not (last and m == 3):
                            gelu(n + 1, (m + 1) % 4)
                        act.wait_ge(s_xt, n + 3)
                        act.wait_ge(s_fa, n + 1)
                        act.activation(x1t[m % 2], bank(4 + m % 2).rearrange("p (n m) -> p n m", m=P),
                                       ACT.Copy).then_inc(s_xtc, 1)

                act.wait_ge(s_folded, 2 * b + 2)
                gelu(b * 64, 0)
                with act.Fori(0, CHUNKS - 1) as c:
                    copies(c, False)
                copies(CHUNKS - 1, True)
                barrier(act, b, 2)

                stats(1)
                for g in range(8):
                    act.wait_ge(s_at, b * 8 + g + 1)
                    act.wait_ge(s_fg, b * 8 + g + 1)
                    act.activation(aft[g % 2], bank(g % 2).rearrange("p (n m) -> p n m", m=P),
                                   ACT.Copy).then_inc(s_atc, 1)
                mixed = bank(3)[0:C, :].rearrange("p (y n t) -> p y n t", n=MODES, t=2)
                act.wait_ge(s_om, b * 8 + 8)
                act.activation(om, mixed, ACT.Copy).then_inc(s_oms, 1)
                act.activation(om2[:, :, :, 0], mixed[:, :, :, 1], ACT.Copy).then_inc(s_oms, 1)
                act.activation(om2[:, :, :, 1], mixed[:, :, :, 0], ACT.Copy, scale=-1.0).then_inc(s_oms, 1)
                act.wait_ge(s_ot, b + 1)
                for s in range(2):
                    for yh in range(2):
                        act.activation(OT[:, :, s, 8 * yh:8 * yh + 8].rearrange("p o y -> p y o"),
                                       bank(4 + 2 * s + yh)[0:32, :].rearrange("p (y o) -> p y o", o=C), ACT.Copy)
                barrier(act, b, 3)
                with act.Fori(0, 2) as zz:
                    for u in range(2):
                        z = b * 4 + 2 * zz + u
                        for g in range(8):
                            act.wait_ge(s_zp, z * 8 + g + 1)
                            if g == 0:
                                act.wait_ge(s_yp, (b * 4 + 2 * zz) * 16 + 1)
                            act.activation(Z[u][:, :, 8 * g:8 * g + 8].rearrange("p h o -> p o h"),
                                           bank(g % 2)[0:32, :].rearrange("p (o h) -> p o h", h=64),
                                           ACT.Copy).then_inc(s_zc, 1)
                barrier(act, b, 4)
                stats(2)
                act.wait_ge(s_st, st_base(b, 2) + NST)

                def high(n, at, u):
                    act.activation(XH[u], X[:, ds(at, 1024)], ACT.Identity, bias=nb, scale=rs).then_inc(s_xh, 1)

                def one_hots(i, last):
                    first, half_first, quarter_first = (b * 16 + i) * 16, (b * 16 + i) * 8, (b * 16 + i) * 4

                    def copy_odd(k):
                        q = k // 2 % 2
                        act.wait_ge(s_oht, 2 + first + k + 1)
                        act.wait_ge(s_cd, half_first + k // 2 + 1)
                        act.activation(OTs[q][:, :, 256:512], bank(5).bitcast(F16).rearrange(
                            "p (k n) -> p k n", k=4), ACT.Copy).then_inc(s_oca, 1)

                    for k in range(16):
                        n, u, hh = first + k, k // 8, k % 2
                        c = b * 32 + 2 * i + u
                        act.wait_ge(s_mxs, n + 1)
                        act.wait_ge(s_oht, n + 1)
                        for t2 in range(2):
                            t = act.activation(OH[2 * hh + t2], bank(2 * hh + t2), ACT.Exp,
                                               bias=negsharp[:, hh, t2:t2 + 1], scale=SHARP)
                        t.then_inc(s_oh, 1)
                        if k % 2 == 0 and k >= 2:
                            copy_odd(k - 1)
                        if k % 8 == 3 and not last:
                            act.wait_ge(s_hl[u], 96 * (b * 16 + i + 1))
                            act.wait_ge(s_xl, c + 1)
                            high(c + 2, (2 * i + u + 2) * 1024, u)
                    copy_odd(15)

                high(b * 32, 0, 0)
                high(b * 32 + 1, 1024, 1)
                with act.Fori(0, 15) as i:
                    one_hots(i, False)
                one_hots(15, True)
                barrier(act, b, 5)
                stats(3)
                act.wait_ge(s_st, st_base(b, 3) + NST)

                def conv_high(at, u):
                    act.activation(NH[u][:, 1:9, :, 2:130], X[:, ds(at, 2048)].rearrange(
                        "p (k j n) -> p k j n", j=2, n=P), ACT.Identity, bias=nb, scale=rs).then_inc(s_nh, 1)

                def out_copies(i, last):
                    for u in range(2):
                        c = b * CHUNKS + 2 * i + u
                        for m in range(4):
                            n = c * 4 + m
                            if m == 0:
                                act.wait_ge(s_out[u], 32 * (b * 8 + i + 1))
                            act.wait_ge(s_ct, n + 5)
                            src = bank(4 + m % 2).rearrange("p (k r o) -> p k r o", r=2, o=C)
                            dst = ost[u].rearrange("p (k r) j o -> p k r j o", r=2)[:, 4 * (m // 2):4 * (m // 2) + 4]
                            act.activation(dst[:, :, 1, m % 2, :], src[:, :, 0, :], ACT.Copy)
                            act.activation(dst[:, :, 0, m % 2, :], src[:, :, 1, :], ACT.Copy).then_inc(s_oc, 1)
                            if m == 0 and not (last and u == 1):
                                act.wait_ge(s_cv, c * 4 + 4)
                                act.wait_ge(s_cp, b * 17 + 2 * i + u + 2)
                                conv_high((2 * i + u + 1) * 2048, 1 - u)

                act.wait_ge(s_pad, 2 * b + 2)
                conv_high(0, 0)
                with act.Fori(0, 7) as i:
                    out_copies(i, False)
                out_copies(7, True)
                act.wait_ge(s_e, b * 5 + 4)
                act.activation(edge_t.rearrange("p (j o) -> p j o", o=C),
                               bank(7)[:, 0:2 * P].rearrange("p (j r o) -> p j r o", r=2, o=C)[:, :, 0, :],
                               ACT.Copy).then_inc(s_e, 1)
                barrier(act, b, 6)

        @block.vector
        def _(dve):
            for free, count in ((s_x1n, 2), (s_fac, 1), (s_x2, 2), (s_ocd, 1), (s_x3, 2), (s_rs, 4), (s_cp, 1)):
                dve.sem_inc(free, count)
            dve.memset(neghalf, -0.5 / CSCALE).then_inc(s_prep, 1)
            dve.wait_ge(s_const, 16 * len(CONSTS))
            dve.tensor_scalar(ct32, ct32, CSCALE, None, ALU.mult).then_inc(s_prep, 1)
            dve.tensor_scalar(c32, c32, CSCALE, None, ALU.mult).then_inc(s_prep, 1)
            dve.wait_ge(s_prep, 3)
            dve.tensor_copy(code_top[0:C, :], ct32[0:C, :])
            dve.tensor_copy(code_low[0:C, :], ct32[0:C, :]).then_inc(s_prep, 1)
            dve.tensor_copy(hi16, ct32).then_inc(s_prep, 1)
            dve.tensor_copy(code_hi[:], c32).then_inc(s_prep, 1)
            dve.tensor_copy(conv_hi[:], cv32).then_inc(s_prep, 1)
            dve.wait_ge(s_prep, 7)
            dve.tensor_tensor(code_low[C:P, :], ct32[C:P, :], hi16[C:P, :], ALU.subtract)
            dve.tensor_tensor(code_lo[:], c32, code_hi[:], ALU.subtract).then_inc(s_prep, 1)
            dve.tensor_tensor(conv_lo[:], cv32, conv_hi[:], ALU.subtract).then_inc(s_prep, 1)
            dve.tensor_tensor(sq, ct32[0:C, :], ct32[0:C, :], ALU.mult).then_inc(s_prep, 1)
            dve.wait_ge(s_prep, 11)
            dve.tensor_copy(bias_row, bank(0)[0:1, :]).then_inc(s_prep, 1)
            dve.wait_ge(s_prep, 12)
            dve.tensor_copy(row16[:, 0:NCODE], bias_row).then_inc(s_lf, 1)
            dve.tensor_copy(id16[:], id32[:])
            dve.memset(X[:, NPX:NPX + PAIR], 0.0)
            dve.memset(nbl[:], 0.0).then_inc(s_lf, 1)
            dve.wait_ge(s_lf, 2)
            dve.tensor_tensor(row16[:, NCODE:2 * NCODE], bias_row, row16[:, 0:NCODE], ALU.subtract).then_inc(s_prep, 1)

            with dve.Fori(0, B) as b:
                def stats(layer):
                    base = st_base(b, layer)
                    dve.bn_aggr(agg[:], bnst[:]).then_inc(s_st, 1)
                    dve.wait_ge(s_st, base + 2)
                    dve.tensor_tensor(dev, agg[:, 0:1], mg, ALU.subtract).then_inc(s_st, 1)
                    dve.wait_ge(s_st, base + 3)
                    dve.scalar_tensor_tensor(e2, dev, dev, agg[:, 1:2], ALU.mult, ALU.add).then_inc(s_st, 1)
                    dve.wait_ge(s_st, base + 5)
                    dve.tensor_scalar(var, bank(7)[:, 1:2], EPS, None, ALU.add).then_inc(s_st, 1)
                    dve.wait_ge(s_st, base + 7)
                    dve.reciprocal(y0, sd).then_inc(s_st, 1)
                    dve.wait_ge(s_st, base + 8)
                    dve.scalar_tensor_tensor(y2, y0, var, y0, ALU.mult, ALU.mult).then_inc(s_st, 1)
                    dve.wait_ge(s_st, base + 9)
                    dve.tensor_scalar(y3, y2, -0.5, 1.5, ALU.mult, ALU.add).then_inc(s_st, 1)
                    dve.wait_ge(s_st, base + 10)
                    dve.tensor_tensor(rs, y0, y3, ALU.mult).then_inc(s_st, 1)
                    dve.wait_ge(s_st, base + 11)
                    dve.scalar_tensor_tensor(nb, mg, -1.0, rs, ALU.mult, ALU.mult).then_inc(s_st, 1)
                    dve.wait_ge(s_st, base + 12)

                def measure(src, at):
                    return dve.bn_stats(bnst[:, ds(at, 6)], src)

                with dve.Fori(0, 8) as c2:
                    for u in range(2):
                        c = b * CHUNKS + 2 * c2 + u
                        for j in range(2):
                            n = c * 2 + j
                            dve.wait_ge(s_padd, (n + 1) * 2)
                            dve.scalar_tensor_tensor(ta[:, j], tb[:, j], -0.5, ta[:, j],
                                                     ALU.mult, ALU.add).then_inc(s_dl, 1)
                            dve.wait_ge(s_dl, n + 1)
                            dve.scalar_tensor_tensor(tb[:, j], T[u][:, j, 2:18:2, :], 3.0,
                                                     ta[:, j], ALU.mult, ALU.add).then_inc(s_s1, 1)
                        for m in range(4):
                            dve.wait_ge(s_xin, 2 + c * 4 + m + 1)
                            measure(X[:, ds((2 * c2 + u) * 2048 + m * 512, 512)], ((2 * c2 + u) * 4 + m) * 6)
                barrier(dve, b, 0)
                even, odd = Bv[:, :, 0, :], Bv[:, :, 1, :]
                def neighbours(i, dst, src, ahead):
                    dve.wait_ge(s_lf, 2 + b * 8 + 2 * i)
                    if ahead:
                        dve.tensor_tensor(dst[:, 0:63, :], src[:, 0:63, :], src[:, 1:64, :], ALU.add)
                        t = dve.tensor_tensor(dst[:, 63, :], src[:, 63, :], src[:, 0, :], ALU.add)
                    else:
                        dve.tensor_tensor(dst[:, 1:64, :], src[:, 1:64, :], src[:, 0:63, :], ALU.add)
                        t = dve.tensor_tensor(dst[:, 0, :], src[:, 0, :], src[:, 63, :], ALU.add)
                    t.then_inc(s_lf, 1)
                    dve.wait_ge(s_lf, 2 + b * 8 + 2 * i + 1)

                def lift_into(dst, factor):
                    dve.scalar_tensor_tensor(dst, lift, factor, dst, ALU.mult, ALU.add).then_inc(s_lf, 1)

                neighbours(0, lift, even, True)
                lift_into(odd, -0.5)
                neighbours(1, lift, odd, False)
                lift_into(even, 0.25)
                stats(0)
                dve.tensor_copy(nbl[0:C, :], nb[0:C, :])
                dve.tensor_scalar(dnf[:], dn[:], rs, None, ALU.mult).then_inc(s_folded, 1)
                dve.wait_ge(s_mo, 2 + b * 16 + 16)
                neighbours(2, lift, odd, False)
                lift_into(even, -0.25)
                neighbours(3, lift, even, True)
                lift_into(odd, 0.5)
                dve.wait_ge(s_lf, 2 + b * 8 + 8)
                dve.tensor_copy(R1[:, P * C:P * C + C], R1[:, 0:C])
                dve.wait_ge(s_fold, b + 1)
                dve.tensor_tensor(fb, bank(7)[:, 2:3], dbias[:], ALU.add).then_inc(s_folded, 1)
                barrier(dve, b, 1)

                with dve.Fori(0, CHUNKS) as c:
                    for m in range(4):
                        n = (b * CHUNKS + c) * 4 + m
                        dve.wait_ge(s_g, 4 + n + 1)
                        dve.tensor_tensor(x1b[m % 2], x1b[m % 2], X[:, ds(c * 2048 + m * 512, 512)],
                                          ALU.add).then_inc(s_x1, 1)
                        dve.wait_ge(s_x1, n + 1)
                        measure(x1b[m % 2], (c * 4 + m) * 6)
                        dve.tensor_copy(X[:, ds(c * 2048 + m * 512, 512)], x1b[m % 2]).then_inc(s_x1n, 1)
                    dve.wait_ge(s_fa, (b * CHUNKS + c) * 4 + 5)
                    dve.tensor_copy(SCR[:, ds(c * 256, 256)], bank(6)[:, 0:256]).then_inc(s_fac, 1)
                barrier(dve, b, 2)

                stats(1)
                dve.wait_ge(s_fg, 2 + b * 8 + 8)
                F = bank(2).rearrange("p (y t n) -> p t y n", t=2, n=MODES)
                V = DV.rearrange("p t (y n) -> p t y n", n=MODES)
                lo, up = slice(0, C), slice(C, P)
                dve.tensor_scalar(V[lo, 0], F[lo, 0], rs[lo, :], None, ALU.mult).then_inc(s_dv, 1)
                dve.tensor_scalar(V[lo, 1], F[lo, 1], rs[lo, :], None, ALU.mult).then_inc(s_dv, 1)
                dve.tensor_scalar(V[up, 0], F[up, 1], rs[up, :], -1.0, ALU.mult, ALU.mult).then_inc(s_dv, 1)
                dve.tensor_scalar(V[up, 1], F[up, 0], rs[up, :], None, ALU.mult).then_inc(s_dv, 1)
                dve.wait_ge(s_dv, b * 6 + 4)
                dve.scalar_tensor_tensor(DV[lo, 0, 0:1], nb[lo, :], float(W), DV[lo, 0, 0:1], ALU.mult, ALU.add).then_inc(s_dv, 1)
                dve.scalar_tensor_tensor(DV[up, 1, 0:1], nb[up, :], float(W), DV[up, 1, 0:1], ALU.mult, ALU.add).then_inc(s_dv, 1)
                barrier(dve, b, 3)
                with dve.Fori(0, 2) as zz:
                    for u in range(2):
                        for m in range(16):
                            n = (b * 4 + 2 * zz + u) * 16 + m
                            at = (2 * zz + u) * 16 + m
                            dve.wait_ge(s_yp, n + 2)
                            dve.tensor_tensor(X[:, ds(at * 512, 512)], bank(2 + m % 2), X[:, ds(at * 512, 512)],
                                              ALU.add).then_inc(s_x2, 1)
                            dve.wait_ge(s_x2, 2 + n + 1)
                            measure(X[:, ds(at * 512, 512)], at * 6)
                barrier(dve, b, 4)

                stats(2)

                def low(n, at, u):
                    dve.tensor_scalar(XN[u], X[:, ds(at, 1024)], rs, nb, ALU.mult, ALU.add).then_inc(s_xn, 1)
                    dve.wait_ge(s_xn, n + 1)
                    dve.wait_ge(s_xh, n + 1)
                    dve.tensor_tensor(XL[u], XN[u], XH[u], ALU.subtract).then_inc(s_xl, 1)

                def maximum(n, hh):
                    dve.wait_ge(s_sc, n + 1)
                    dve.tensor_reduce(negmax[:, hh, :], bank(2 * hh, 2).rearrange("p (t n) -> p t n", t=2), AX.X,
                                      ALU.max, negate=True).then_inc(s_mx, 1)
                    dve.wait_ge(s_mx, n + 1)
                    dve.tensor_scalar(negsharp[:, hh, :], negmax[:, hh, :], SHARP, None, ALU.mult).then_inc(s_mxs, 1)

                def vector_steps(i, last):
                    first, half_first, quarter_first = (b * 16 + i) * 16, (b * 16 + i) * 8, (b * 16 + i) * 4

                    def add_codes(k):
                        px = k // 4 % 2
                        dve.wait_ge(s_cd, 2 + half_first + k // 2 + 1)
                        at = 2 * i * 1024 + (k // 4) * 512
                        dve.scalar_tensor_tensor(X[:, ds(at, 512)], bank(6 + px), 1.0 / CSCALE,
                                                 X[:, ds(at, 512)], ALU.mult, ALU.add).then_inc(s_x3, 1)
                        dve.wait_ge(s_x3, 2 + quarter_first + k // 4 + 1)
                        measure(X[:, ds(at, 512)], (2 * i * 2 + k // 4) * 6)

                    for k in range(16):
                        n, u, hh, q = first + k, k // 8, k % 2, k // 2 % 2
                        c = b * 32 + 2 * i + u
                        if not (last and k >= 14):
                            maximum(n + 2, hh)
                        if hh == 0:
                            dve.wait_ge(s_oht, 2 + n + 1)
                            dve.wait_ge(s_cd, half_first + k // 2 + 1)
                            dve.tensor_copy(OTs[q][:, :, 0:256],
                                            bank(4).bitcast(F16).rearrange("p (k n) -> p k n", k=4)).then_inc(s_ocd, 1)
                        if k % 8 == 5 and not last:
                            dve.wait_ge(s_hl[u], 96 * (b * 16 + i + 1))
                            low(c + 2, (2 * i + u + 2) * 1024, u)
                        if k % 4 == 1 and k >= 5:
                            add_codes(k - 2)
                    add_codes(15)

                low(b * 32, 0, 0)
                low(b * 32 + 1, 1024, 1)
                maximum(b * 256, 0)
                maximum(b * 256 + 1, 1)
                with dve.Fori(0, 15) as i:
                    vector_steps(i, False)
                vector_steps(15, True)
                barrier(dve, b, 5)

                stats(3)

                def conv_low(n, at, u, edges):
                    dve.tensor_scalar(XM, X[:, ds(at, 2048)].rearrange("p (k n) -> p k n", n=P), rs, nb,
                                      ALU.mult, ALU.add).then_inc(s_nn, 1)
                    dve.wait_ge(s_nn, n + 1)
                    dve.wait_ge(s_nh, n + 1)
                    dve.tensor_tensor(NL[u][:, 1:9, :, 2:130], XM.rearrange("p (k j) n -> p k j n", j=2),
                                      NH[u][:, 1:9, :, 2:130], ALU.subtract).then_inc(s_nl, 1)
                    dve.wait_ge(s_nl, n + 1)
                    dve.wait_ge(s_cp, edges)
                    for buf in (NH, NL):
                        dve.tensor_copy(buf[u][:, 0, :, :], buf[1 - u][:, 8, :, :])
                        t = dve.tensor_copy(buf[u][:, 1:9, 1, 0:1], buf[u][:, 1:9, 1, 129:130])
                    t.then_inc(s_cp, 1)

                def residuals(i, last):
                    for u in range(2):
                        c = b * CHUNKS + 2 * i + u
                        for m in range(4):
                            n = c * 4 + m
                            dve.wait_ge(s_cv, n + 5)
                            dve.wait_ge(s_ct, n + 1)
                            k0 = ((2 * i + u) * 8 + 4 * (m // 2)) * 2 + m % 2
                            X4 = X[:, :].rearrange("p (k n) -> p k n", n=P)
                            src = bank(m).rearrange("p (k n) -> p k n", n=P)
                            dst = res[m].rearrange("p (k n) -> p k n", n=P)
                            dve.scalar_tensor_tensor(dst[0:C], src[0:C], cbias[0:C, :],
                                                     X4[0:C, ds(k0 + 2, 4, 2), :], ALU.add, ALU.add)
                            dve.scalar_tensor_tensor(dst[C:P], src[C:P], cbias[C:P, :],
                                                     X4[C:P, ds(k0, 4, 2), :], ALU.add, ALU.add).then_inc(s_rs, 1)
                            if m == 0 and not (last and u == 1):
                                dve.wait_ge(s_cv, c * 4 + 4)
                                dve.wait_ge(s_cp, b * 17 + 2 * i + u + 2)
                                conv_low(c + 1, (2 * i + u + 1) * 2048, 1 - u, b * 17 + 2 * i + u + 2)

                dve.wait_ge(s_pad, 2 * b + 2)
                conv_low(b * CHUNKS, 0, 0, b * 17 + 1)
                with dve.Fori(0, 7) as i:
                    residuals(i, False)
                residuals(7, True)
                dve.wait_ge(s_cv, (b * CHUNKS + 16) * 4 + 4)
                dve.wait_ge(s_cp, b * 17 + 17)
                for buf in (NH, NL):
                    dve.tensor_copy(buf[0][:, 0, :, :], buf[1][:, 8, :, :])
                    t = dve.memset(buf[0][:, 1, :, :], 0.0)
                t.then_inc(s_cp, 1)
                dve.wait_ge(s_e, b * 5 + 1)
                dve.scalar_tensor_tensor(edge[0:C, :], bank(6)[0:C, 0:PAIR], cbias[0:C, :], X[0:C, 0:PAIR],
                                         ALU.add, ALU.add).then_inc(s_e, 1)
                dve.memset(edge[C:P, :], 0.0).then_inc(s_e, 1)
                barrier(dve, b, 6)

        @block.gpsimd
        def _(pool):
            pool.wait_ge(s_prep, 13)
            pool.wait_ge(s_const, 16 * (len(CONSTS) + 2))
            with pool.Fori(0, B) as b:
                with pool.Fori(0, 8) as c2:
                    for u in range(2):
                        c = b * CHUNKS + 2 * c2 + u
                        pool.wait_ge(s_tile[u], 96 * (b * 8 + c2 + 1))
                        pool.wait_ge(s_wa, c + 1)
                        for j in range(2):
                            pool.tensor_tensor(ta[:, j], T[u][:, j, 1:16:2, :], T[u][:, j, 3:18:2, :],
                                               ALU.add).then_inc(s_padd, 1)
                            pool.tensor_tensor(tb[:, j], T[u][:, j, 0:15:2, :], T[u][:, j, 4:19:2, :],
                                               ALU.add).then_inc(s_padd, 1)
                barrier(pool, b, 0)
                pool.wait_ge(s_folded, 2 * b + 1)
                past(pool)
                with pool.Fori(0, 8) as g:
                    for u in range(2):
                        pool.wait_ge(s_mo, b * 16 + 2 * g + u + 1)
                        pool.tensor_copy(mst[u], R1[:, ds((2 * g + u) * 512, 512)]).then_inc(s_mc, 1)
                barrier(pool, b, 1)

                def interpolate(at, u):
                    a = R1[:, ds(at, 256)].rearrange("p (k o) -> p k o", o=C)
                    a1 = R1[:, ds(at + C, 256)].rearrange("p (k o) -> p k o", o=C)
                    pool.tensor_tensor(syn[u][:, :, 0, :], a, a, ALU.add)
                    pool.tensor_tensor(syn[u][:, :, 1, :], a, a1, ALU.add).then_inc(s_sy, 1)

                interpolate(0, 0)
                interpolate(256, 1)
                with pool.Fori(0, CHUNKS - 1) as c:
                    for u in range(2):
                        pool.wait_ge(s_l0, (b * CHUNKS + c) * 4 + 2 * u + 2)
                        interpolate(c * 512 + 512 + 256 * u, u)
                barrier(pool, b, 2)
                barrier(pool, b, 3)
                barrier(pool, b, 4)
                for u in range(2):
                    for q in range(2):
                        t = pool.memset(HQ[u][q][C:C + 32, :], 1.0)
                t.then_inc(s_pad, 1)
                barrier(pool, b, 5)
                for buf in (NH, NL):
                    for u in range(2):
                        pool.memset(buf[u][:, :, :, 0:2], 0.0)
                    t = pool.memset(buf[1][:, 8, :, 2:130], 0.0)
                t.then_inc(s_pad, 1)
                barrier(pool, b, 6)

    return nc


def cdf53(n, level):
    cur = np.eye(n)
    for _ in range(level):
        e, o = cur[0::2], cur[1::2]
        d = o - 0.5 * (e + np.roll(e, -1, 0))
        s = e + 0.25 * (d + np.roll(d, 1, 0))
        cur, high = s, d
    return np.concatenate([cur, high])


def uncdf53(s, d):
    e = s - 0.25 * (d + np.roll(d, 1, 0))
    o = d + 0.5 * (e + np.roll(e, -1, 0))
    return np.stack([e, o], 1).reshape(2 * len(e), -1)


def shape_constants():
    f32 = np.float32
    a = cdf53(W, 2) / 4.0
    w_analysis = a.reshape(P, P, 2).transpose(1, 2, 0)
    low, high = np.eye(P)[:C], np.eye(P)[C:]
    s = uncdf53(low, high)
    s = uncdf53(s, np.zeros_like(s)) / 2.0
    w_synthesis = s.reshape(P, 2, P).transpose(2, 1, 0).reshape(P, 2 * P)
    k, m = np.arange(W), np.arange(MODES)
    ang = 2 * np.pi * np.outer(k, m) / W
    cos, sin = np.cos(ang), np.sin(ang)
    dft_w = np.stack([cos, -sin], 2).reshape(P, 2, 2 * MODES) / W
    c2, s2 = cos.reshape(P, 2, MODES), sin.reshape(P, 2, MODES)
    dft_h = np.stack([np.concatenate([c2, -s2], 2), np.concatenate([s2, c2], 2)], 2).reshape(P, 4, 2 * MODES)
    idft_h = np.stack([cos, -sin], 2).reshape(W, 2 * MODES).T
    twice = np.where(m == 0, 1.0, 2.0)[:, None] / W
    order = k.reshape(P, 2).T.reshape(-1)
    idft_w = np.concatenate([cos.T * twice, -sin.T * twice])[:, order]
    pair = np.arange(P) % C // 2
    group = (pair[:, None] == pair[None, :]) / 4.0
    return {"ident": np.eye(P, dtype=f32), "group": group.astype(f32), "w_analysis": w_analysis.astype(f32),
            "w_synthesis": w_synthesis.astype(f32), "dft_w": dft_w.astype(f32), "dft_h": dft_h.astype(f32),
            "idft_h": idft_h.astype(f32), "idft_w": idft_w.astype(f32)}


def two_blocks(a, b):
    out = np.zeros((2 * C, 2 * C), a.dtype)
    out[:C, :C] = a
    out[C:, C:] = b
    return out


def kernel(x, L0_conv_w_approx, L0_conv_w_detail, L0_conv_dense_kernel, L0_conv_dense_bias,
           L1_conv_weights_real, L1_conv_weights_imag, L2_conv_codebook, L3_conv_kernel, L3_conv_bias):
    import concourse.bacc as bacc
    from concourse.bass_utils import run_bass_kernel_spmd as run

    x = np.ascontiguousarray(x)
    det = np.asarray(L0_conv_w_detail)
    both = np.concatenate([np.asarray(L1_conv_weights_real), np.asarray(L1_conv_weights_imag)])
    modes = both.transpose(0, 3, 2, 1).reshape(P, MODES * MODES, C)
    book = np.asarray(L2_conv_codebook)
    taps = np.asarray(L3_conv_kernel).transpose(2, 3, 1, 0)
    conv = np.zeros((P, 6, P), np.float32)
    for half, row in ((0, 2), (1, 1)):
        for pr in range(2):
            for q in range(2):
                back = row - (2 * (pr - 1) + q)
                if 1 <= back <= 3:
                    for t in range(3):
                        conv[q * C:(q + 1) * C, pr * 3 + t, half * C:(half + 1) * C] = taps[back - 1, t]
    twice = lambda v: np.ascontiguousarray(np.concatenate([np.asarray(v).reshape(C, 1)] * 2))
    arrays = {
        "x": x,
        "dense": two_blocks(np.asarray(L0_conv_dense_kernel), np.asarray(L0_conv_dense_kernel)),
        "dense_bias": twice(L0_conv_dense_bias),
        "mix_low": two_blocks(np.asarray(L0_conv_w_approx)[:, :, 0, 0], det[..., 0]),
        "mix_high": two_blocks(det[..., 1], det[..., 2]),
        "modes": np.ascontiguousarray(modes),
        "codes": np.ascontiguousarray(book.reshape(4, P, C).transpose(1, 0, 2)),
        "codes_t": np.ascontiguousarray(np.concatenate([book.T, book.T])),
        "conv": conv,
        "conv_bias": twice(L3_conv_bias),
        **shape_constants(),
    }
    nc = bacc.Bacc("TRN2", target_bir_lowering=False, num_devices=1)
    args = {}
    for name, a in arrays.items():
        arrays[name] = a = np.ascontiguousarray(a)
        args[name] = nc.dram_tensor(name, a.shape, mybir.dt.from_np(a.dtype), kind="ExternalInput").ap()
    out = nc.dram_tensor("out", x.shape, F32, kind="ExternalOutput").ap()
    fused_layers(nc, out=out, **args)
    r = run(nc, [arrays], core_ids=[0])
    return r.results[0]["out"]
```

```python
from contextlib import ExitStack

import concourse.bass as bass
import numpy as np
from concourse import mybir

F32 = mybir.dt.float32
F16 = mybir.dt.float16
ALU = mybir.AluOpType
ACT = mybir.ActivationFunctionType
AX = mybir.AxisListType
ds = bass.ds

C = 64
W = 256
P = 128
PAIR = 2 * P
MODES = 16
NCODE = 512
CSCALE = 64.0
SHARP = 2.0 ** 50
EPS = 1e-5
ENGINES = 5
PHASES = 7


def fused_layers(nc, x, dense, dense_bias, mix_low, mix_high, modes, codes, codes_t, conv, conv_bias,
                 ident, group, w_analysis, w_synthesis, dft_w, dft_h, idft_h, idft_w, out):
    B = x.shape[0]
    NPX = P * PAIR
    ctx = ExitStack()
    with ctx:
        def sb(name, shape, dt=F32):
            return ctx.enter_context(nc.sbuf_tensor(name, shape, dt))

        def sem(name):
            return ctx.enter_context(nc.semaphore(name))

        X = sb("X", [P, NPX + PAIR])
        R1 = sb("R1", [P, 129 * C])
        SCR = sb("SCR", [P, 7680])
        id32 = sb("id32", [P, P])
        id16 = sb("id16", [P, P], F16)
        grp = sb("grp", [P, P])
        wan = sb("wan", [P, 2, P])
        wsy = sb("wsy", [P, 2 * P])
        dn = sb("dn", [P, P])
        dnf = sb("dnf", [P, P])
        mixw = sb("mixw", [P, 2, P])
        dfw = sb("dfw", [P, 2, 32])
        dfh = sb("dfh", [P, 4, 32])
        idh = sb("idh", [32, W])
        idw = sb("idw", [32, 2 * P])
        dbias = sb("dbias", [P, 1])
        cbias = sb("cbias", [P, 1])
        code_top = sb("code_top", [P, NCODE], F16)
        code_low = sb("code_low", [P, NCODE], F16)
        code_hi = sb("code_hi", [P, 4, C], F16)
        code_lo = sb("code_lo", [P, 4, C], F16)
        conv_hi = sb("conv_hi", [P, 6, P], F16)
        conv_lo = sb("conv_lo", [P, 6, P], F16)
        bnst = sb("bnst", [P, 64 * 6])
        agg = sb("agg", [P, 2])
        tiny = sb("tiny", [P, 12])
        negmax = sb("negmax", [P, 2, 2])
        negsharp = sb("negsharp", [P, 2, 2])
        dev, e2, var, sd, y0, y2, y3, rs, nb, fb = (tiny[:, i:i + 1] for i in range(10))
        nbl = sb("nbl", [P, 1])
        nbd = sb("nbd", [P, 1])

        PS = ctx.enter_context(nc.psum_tensor("PS", [P, 8 * 512], F32))

        def bank(i, n=1):
            return PS[:, i * 512:(i + n) * 512]

        mg = bank(7)[:, 0:1]

        def wide(column, n):
            return bass.AP(column.tensor, column.offset, [column.ap[0], [0, n]])

        T = [SCR[:, u * 2432:(u + 1) * 2432].rearrange("p (j r c) -> p j r c", j=2, c=C) for u in range(2)]
        ta = SCR[:, 4864:5888].rearrange("p (j k c) -> p j k c", j=2, c=C)
        tb = SCR[:, 5888:6912].rearrange("p (j k c) -> p j k c", j=2, c=C)
        Bc = R1[:, 0:P * C]
        Bv = Bc.rearrange("p (k t c) -> p k t c", t=2, c=C)
        lift = SCR[:, 0:4096].rearrange("p (k c) -> p k c", c=C)
        mst = [SCR[:, 4096 + 512 * u:4608 + 512 * u] for u in range(2)]
        mbt = [SCR[:, 5120 + 512 * u:5632 + 512 * u].rearrange("p (m n) -> p m n", n=P) for u in range(2)]
        AF = SCR[:, 0:4096].rearrange("p (k s) -> p k s", s=32)
        syn = [SCR[:, 4096 + 512 * u:4608 + 512 * u].rearrange("p (k q o) -> p k q o", q=2, o=C) for u in range(2)]
        x1b = [SCR[:, 5120 + 512 * u:5632 + 512 * u] for u in range(2)]
        x1t = [SCR[:, 6656 + 512 * u:7168 + 512 * u].rearrange("p (n m) -> p n m", m=P) for u in range(2)]
        aft = [SCR[:, 4096 + 512 * u:4608 + 512 * u].rearrange("p (n m) -> p n m", m=P) for u in range(2)]
        DV = SCR[:, 5120:5632].rearrange("p (t n) -> p t n", t=2)
        om = SCR[0:C, 5632:6144].rearrange("p (y n t) -> p y n t", n=16, t=2)
        om2 = SCR[0:C, 6144:6656].rearrange("p (y n t) -> p y n t", n=16, t=2)
        OT = SCR[0:32, 0:2048].rearrange("p (o s y) -> p o s y", s=2, y=MODES)
        WM = [R1[:, 2048 * u:2048 * (u + 1)].rearrange("p (n o) -> p n o", o=C) for u in range(2)]
        Z = [R1[0:32, 4096 * u:4096 * (u + 1)].rearrange("p (h o) -> p h o", o=C) for u in range(2)]
        R1h = R1[:, 0:8192].bitcast(F16)
        SCRh = SCR[:, :].bitcast(F16)
        XH = [R1h[:, 1024 * u:1024 * (u + 1)] for u in range(2)]
        XL = [R1h[:, 2048 + 1024 * u:3072 + 1024 * u] for u in range(2)]
        XN = [R1[:, 2048 + 1024 * u:3072 + 1024 * u] for u in range(2)]
        HQ = [[R1h[:, 8192 + 2048 * u + 1024 * q:9216 + 2048 * u + 1024 * q] for q in range(2)] for u in range(2)]
        LQ = [[SCRh[:, 2048 * u + 1024 * q:2048 * u + 1024 * q + 1024] for q in range(2)] for u in range(2)]
        OH = [SCRh[:, 4096 + 512 * i:4608 + 512 * i] for i in range(4)]
        OTs = [SCRh[:, 6144 + 2048 * i:8192 + 2048 * i].rearrange("p (k n) -> p k n", k=4) for i in range(2)]
        NH = [R1h[:, 2340 * u:2340 * (u + 1)].rearrange("p (k j n) -> p k j n", j=2, n=130) for u in range(2)]
        NL = [R1h[:, 4680 + 2340 * u:7020 + 2340 * u].rearrange("p (k j n) -> p k j n", j=2, n=130) for u in range(2)]
        XM = R1[:, 4680:6728]
        res = [SCR[:, 512 * i:512 * (i + 1)] for i in range(4)]
        ost = [SCR[:, 2048 + 2048 * u:4096 + 2048 * u].rearrange("p (r j o) -> p r j o", j=2, o=C) for u in range(2)]
        edge = SCR[:, 6144:6400]
        edge_t = SCR[:, 6400:6528]

        s_const = sem("constants_loaded")
        s_prep = sem("weights_prepared")
        s_bar = sem("phase_barrier")
        s_past = sem("waits_taken")
        s_st = sem("statistics_step")
        s_tile = [sem(f"tile_loaded{u}") for u in range(2)]
        s_tp = sem("tile_transposed")
        s_xin = sem("x_written")
        s_padd = sem("row_sums_added")
        s_dl = sem("row_filter_link")
        s_s1 = sem("low_rows_ready")
        s_wa = sem("columns_analysed")
        s_wb = sem("coefficients_stored")
        s_lf = sem("lifting_link")
        s_mc = sem("mix_staged")
        s_mt = sem("mix_transposed")
        s_mb = sem("mix_normalised")
        s_mm = sem("mix_multiplied")
        s_mo = sem("mix_stored")
        s_fold = sem("dense_bias_product_ready")
        s_folded = sem("dense_folded")
        s_sy = sem("synthesis_rows_ready")
        s_l0 = sem("layer0_product_ready")
        s_g = sem("gelu_ready")
        s_x1 = sem("x1_ready")
        s_x1n = sem("x1_measured")
        s_xt = sem("x1_transposed")
        s_xtc = sem("x1_transpose_copied")
        s_fa = sem("row_dft_ready")
        s_fac = sem("row_dft_stored")
        s_at = sem("row_dft_transposed")
        s_atc = sem("row_dft_transpose_copied")
        s_fg = sem("image_dft_ready")
        s_dv = sem("mode_vectors_ready")
        s_wm = [sem(f"mode_weights_loaded{u}") for u in range(2)]
        s_om = sem("modes_mixed")
        s_oms = sem("mixed_modes_copied")
        s_ot = sem("mixed_modes_transposed")
        s_zp = sem("column_synthesis_ready")
        s_zc = sem("column_synthesis_stored")
        s_yp = sem("layer1_output_ready")
        s_x2 = sem("x2_written")
        s_xh = sem("x_high_ready")
        s_xn = sem("x_normalised")
        s_xl = sem("x_low_ready")
        s_hl = [sem(f"halves_placed{u}") for u in range(2)]
        s_sc = sem("scores_ready")
        s_mx = sem("maximum_ready")
        s_mxs = sem("maximum_scaled")
        s_oh = sem("one_hots_ready")
        s_oht = sem("one_hots_transposed")
        s_ocd = sem("even_one_hots_copied")
        s_oca = sem("odd_one_hots_copied")
        s_cd = sem("codes_looked_up")
        s_x3 = sem("x3_written")
        s_nh = sem("conv_high_ready")
        s_nn = sem("conv_normalised")
        s_nl = sem("conv_low_ready")
        s_cp = sem("conv_edges_ready")
        s_pad = sem("conv_padding_cleared")
        s_cv = sem("conv_ready")
        s_rs = sem("conv_residual_added")
        s_ct = sem("output_transposed")
        s_oc = sem("output_copied")
        s_out = [sem(f"output_stored{u}") for u in range(2)]
        s_e = sem("row0_step")
        s_eout = sem("row0_stored")

        block = ctx.enter_context(nc.Block())

        x_cols = x.rearrange("b h (p j) c -> b j p h c", j=2)
        o_rows = out.rearrange("b h (p j) c -> b p h (j c)", j=2)

        ct32 = SCR[:, 0:NCODE]
        c32 = SCR[:, 512:768].rearrange("p (k c) -> p k c", c=C)
        cv32 = SCR[:, 1024:1792].rearrange("p (k n) -> p k n", n=P)
        sq = SCR[0:C, 2048:2560]
        hi16 = SCR[:, 2560:2816].bitcast(F16)
        neghalf = SCR[0:C, 3072:3073]
        bias_row = SCR[0:1, 3200:3712]
        row16 = SCR[0:1, 3712:4224].bitcast(F16)
        CONSTS = [(id32[:], ident), (grp[:], group), (wan[:], w_analysis), (wsy[:], w_synthesis),
                  (dn[:], dense), (mixw[:, 0, :], mix_low), (mixw[:, 1, :], mix_high), (dfw[:], dft_w),
                  (dfh[:], dft_h), (idh[:], idft_h), (idw[:], idft_w), (dbias[:], dense_bias),
                  (cbias[:], conv_bias), (ct32, codes_t), (c32, codes), (cv32, conv)]
        CHUNKS = 16
        NST = 12

        def st_base(b, layer):
            return (b * 4 + layer) * NST

        def past(eng):
            eng.sem_inc(s_past, 1)

        def barrier(eng, b, n):
            past(eng)
            eng.drain().then_inc(s_bar, 1)
            eng.wait_ge(s_bar, (b * PHASES + n + 1) * ENGINES)
            past(eng)

        @block.sync
        def _(sp):
            for u in range(2):
                sp.sem_inc(s_out[u], 32)
            for dst, src in CONSTS:
                sp.dma_start(dst, src).then_inc(s_const, 16)
            sp.wait_ge(s_prep, 13)
            sp.dma_start(code_top[C:C + 1, :], row16[:, 0:NCODE]).then_inc(s_const, 16)
            sp.dma_start(code_top[C + 1:C + 2, :], row16[:, NCODE:2 * NCODE]).then_inc(s_const, 16)
            sp.wait_ge(s_const, 16 * (len(CONSTS) + 2))
            with sp.Fori(0, B) as b:
                def around(ci):
                    if isinstance(ci, int):
                        return 16 * ci, (16 * ci + 254) % 256, (16 * ci + 16) % 256
                    return sp.snap(16 * ci), sp.snap((16 * ci + 254) % 256), sp.snap((16 * ci + 16) % 256)

                def load(rows, u):
                    main, above, below = rows
                    for j in range(2):
                        src = x_cols[b, j]
                        sp.dma_start(T[u][:, j, 2:18, :], src[:, ds(main, 16), :]).then_inc(s_tile[u], 16)
                        sp.dma_start(T[u][:, j, 0:2, :], src[:, ds(above, 2), :]).then_inc(s_tile[u], 16)
                        sp.dma_start(T[u][:, j, 18:19, :], src[:, ds(below, 1), :]).then_inc(s_tile[u], 16)

                load(around(0), 0)
                load(around(1), 1)
                with sp.Fori(0, 7) as c2:
                    for u in range(2):
                        n = b * CHUNKS + 2 * c2 + u
                        rows = around(2 * c2 + u + 2)
                        sp.wait_ge(s_wa, n + 2)
                        load(rows, u)
                barrier(sp, b, 0)
                barrier(sp, b, 1)
                barrier(sp, b, 2)
                sp.dma_start(WM[0], modes[:, 0:32, :]).then_inc(s_wm[0], 16)
                sp.dma_start(WM[1], modes[:, 32:64, :]).then_inc(s_wm[1], 16)
                with sp.Fori(0, 3) as i:
                    for u in range(2):
                        sp.wait_ge(s_om, b * 8 + 2 * i + u + 1)
                        sp.dma_start(WM[u], modes[:, ds((2 * i + u + 2) * 32, 32), :]).then_inc(s_wm[u], 16)
                barrier(sp, b, 3)
                barrier(sp, b, 4)

                def place(n, u, first):
                    sp.wait_ge(s_xl, n + 1)
                    if not first:
                        sp.wait_ge(s_sc, (n - 1) * 16)
                    for q in range(2):
                        rows = slice(C * q, C * q + C)
                        sp.dma_start(HQ[u][q][0:C, :], XH[u][rows, :]).then_inc(s_hl[u], 16)
                        sp.dma_start(LQ[u][q][C:P, :], XH[u][rows, :]).then_inc(s_hl[u], 16)
                        sp.dma_start(LQ[u][q][0:C, :], XL[u][rows, :]).then_inc(s_hl[u], 16)

                sp.wait_ge(s_pad, 2 * b + 1)
                place(b * 32, 0, True)
                place(b * 32 + 1, 1, True)
                with sp.Fori(0, 15) as i:
                    for u in range(2):
                        n = b * 32 + 2 * i + u
                        place(n + 2, u, False)
                barrier(sp, b, 5)

                def store(ci, u, halves):
                    sp.wait_ge(s_oc, 2 + (b * CHUNKS + ci + 1) * 4)
                    for r0, nr in halves:
                        sp.dma_start(o_rows[b][:, ds(16 * ci + 1 + r0, nr), :],
                                     ost[u][:, r0:r0 + nr, :, :].rearrange("p r j o -> p r (j o)")
                                     ).then_inc(s_out[u], 16)

                with sp.Fori(0, 7) as i:
                    for u in range(2):
                        store(2 * i + u, u, ((0, 8), (8, 8)))
                store(14, 0, ((0, 8), (8, 8)))
                store(15, 1, ((0, 8), (8, 7)))
                sp.wait_ge(s_e, b * 5 + 5)
                sp.dma_start(o_rows[b][:, 0:1, :], edge_t[:, :].rearrange("p (r n) -> p r n", r=1)).then_inc(s_eout, 16)
                sp.wait_ge(s_eout, 16 * (b + 1))
                for u in range(2):
                    sp.wait_ge(s_out[u], 32 + 256 * (b + 1))
                barrier(sp, b, 6)

        @block.tensor
        def _(pe):
            for free, count in ((s_wa, 1), (s_fg, 2), (s_xt, 2), (s_fa, 1), (s_yp, 1), (s_oht, 2), (s_cd, 2), (s_ct, 4), (s_cv, 4)):
                pe.sem_inc(free, count)
            pe.wait_ge(s_prep, 10)
            pe.matmul(bank(0)[0:1, :], neghalf, sq, start=True, stop=True).then_inc(s_prep, 1)
            pe.wait_ge(s_prep, 13)
            pe.wait_ge(s_const, 16 * (len(CONSTS) + 2))
            with pe.Fori(0, B) as b:
                def stats(layer):
                    base = st_base(b, layer)
                    pe.wait_ge(s_st, base + 1)
                    pe.matmul(bank(7)[:, 0:1], grp[:], agg[:, 0:1], start=True, stop=True).then_inc(s_st, 1)
                    pe.wait_ge(s_st, base + 4)
                    pe.matmul(bank(7)[:, 1:2], grp[:], e2, start=True, stop=True).then_inc(s_st, 1)

                with pe.Fori(0, 8) as c2:
                    for u in range(2):
                        c = b * CHUNKS + 2 * c2 + u
                        pe.wait_ge(s_tile[u], 96 * (b * 8 + c2 + 1))
                        for m in range(4):
                            pe.wait_ge(s_xin, c * 4 + m + 1)
                            for kk in range(2):
                                for j in range(2):
                                    r = 2 + 2 * (2 * m + kk)
                                    t = pe.transpose(bank(m % 2)[:, (2 * kk + j) * P:(2 * kk + j + 1) * P],
                                                     T[u][:, j, r:r + 2, :], id32[:])
                            t.then_inc(s_tp, 1)
                        pe.wait_ge(s_wb, c + 1)
                        for j in range(2):
                            pe.wait_ge(s_s1, c * 2 + j + 1)
                            t = pe.matmul(bank(2 + u), wan[:, j, :], tb[:, j, :, :], start=j == 0, stop=j == 1)
                        t.then_inc(s_wa, 1)
                barrier(pe, b, 0)
                stats(0)
                with pe.Fori(0, 8) as g:
                    for u in range(2):
                        n = b * 16 + 2 * g + u
                        pe.wait_ge(s_mc, n + 1)
                        pe.wait_ge(s_mo, n + 1)
                        for m in range(4):
                            t = pe.transpose(bank(u)[:, m * P:(m + 1) * P], mst[u][:, m * P:(m + 1) * P], id32[:])
                        t.then_inc(s_mt, 1)
                    for u in range(2):
                        n = b * 16 + 2 * g + u
                        pe.wait_ge(s_mb, n + 1)
                        for half in range(2):
                            for m in range(4):
                                t = pe.matmul(bank(2 + u)[half * C:(half + 1) * C, m * P:(m + 1) * P],
                                              mbt[u][:, m, half * C:(half + 1) * C], mixw[:, half, :],
                                              start=True, stop=True)
                        t.then_inc(s_mm, 1)
                pe.matmul(bank(7)[:, 2:3], dn[:], nb, start=True, stop=True).then_inc(s_fold, 1)
                barrier(pe, b, 1)

                def product(n, m, at):
                    if m % 2 == 0:
                        pe.wait_ge(s_sy, at[1] + 1)
                    pe.wait_ge(s_g, n + 1)
                    pe.matmul(bank(m), dnf[:], X[:, ds(at[0], 512)], start=True, stop=False, skip_group_check=True)
                    for i in range(2):
                        t = pe.matmul(bank(m)[:, i * 256:(i + 1) * 256], syn[m // 2][:, 2 * (m % 2) + i, :, :],
                                      wsy[:], start=False, stop=True, skip_group_check=True)
                    t.then_inc(s_l0, 1)

                def layer0_steps(c, last):
                    for m in range(4):
                        n = (b * CHUNKS + c) * 4 + m
                        pe.wait_ge(s_x1, n + 1)
                        pe.wait_ge(s_xtc, n + 1)
                        for i in range(4):
                            t = pe.transpose(bank(4 + m % 2)[:, i * P:(i + 1) * P],
                                             x1b[m % 2][:, i * P:(i + 1) * P], id32[:])
                        t.then_inc(s_xt, 1)
                        if not (last and m >= 2):
                            product(n + 2, (m + 2) % 4, (c * 2048 + (m + 2) * 512, (b * CHUNKS + c) * 2 + (m + 2) // 2))
                        pe.wait_ge(s_xtc, n + 3)
                        if m == 0:
                            pe.wait_ge(s_fac, b * CHUNKS + c + 1)
                        for kk in range(2):
                            for j in range(2):
                                t = pe.matmul(bank(6)[:, (2 * m + kk) * 32:(2 * m + kk + 1) * 32],
                                              x1t[m % 2][:, 2 * kk + j, :], dfw[:, j, :], start=j == 0, stop=j == 1)
                        t.then_inc(s_fa, 1)

                pe.wait_ge(s_folded, 2 * b + 2)
                for m in range(2):
                    product(b * 64 + m, m, (m * 512, b * 32))
                with pe.Fori(0, CHUNKS - 1) as c:
                    layer0_steps(c, False)
                layer0_steps(CHUNKS - 1, True)
                barrier(pe, b, 2)

                stats(1)
                for g in range(9):
                    if g < 8:
                        pe.wait_ge(s_atc, b * 8 + g + 1)
                        for i in range(4):
                            t = pe.transpose(bank(g % 2)[:, i * P:(i + 1) * P], AF[:, :, 4 * g + i], id32[:])
                        t.then_inc(s_at, 1)
                    if g == 0:
                        continue
                    pe.wait_ge(s_atc, b * 8 + g + 2)
                    for yy in range(2):
                        y = 2 * (g - 1) + yy
                        for half in range(2):
                            for q in range(2):
                                for part in range(2):
                                    t = pe.matmul(bank(2)[half * C:(half + 1) * C, y * 32:(y + 1) * 32],
                                                  aft[(g - 1) % 2][:, 2 * yy + part, q * C:(q + 1) * C],
                                                  dfh[:, 2 * q + part, :], start=q == 0 and part == 0,
                                                  stop=q == 1 and part == 1)
                    t.then_inc(s_fg, 1)
                pe.wait_ge(s_dv, b * 6 + 6)
                past(pe)
                for i in range(4):
                    for u in range(2):
                        pe.wait_ge(s_wm[u], 16 * (b * 4 + i + 1))
                        for md in range(32):
                            k = (2 * i + u) * 32 + md
                            t = pe.matmul(bank(3)[0:C, 2 * k:2 * k + 2], WM[u][:, md, :],
                                          DV[:, :, k:k + 1], start=True, stop=True)
                        t.then_inc(s_om, 1)
                pe.wait_ge(s_oms, b * 3 + 3)
                past(pe)
                for s, src in enumerate((om, om2)):
                    for y in range(MODES):
                        t = pe.transpose(bank(4 + 2 * s + y // 8)[0:32, (y % 8) * C:(y % 8 + 1) * C],
                                         src[:, y, :, :], id32[0:C, 0:C])
                t.then_inc(s_ot, 1)
                barrier(pe, b, 3)

                for zz in range(2):
                    for u in range(2):
                        z = b * 4 + 2 * zz + u
                        for g in range(8):
                            pe.wait_ge(s_zc, z * 8 + g + 1)
                            past(pe)
                            for o in range(8):
                                t = pe.matmul(bank(g % 2)[0:32, o * 64:(o + 1) * 64], OT[:, 8 * g + o, :, :],
                                              idh[:, 128 * zz + 64 * u:128 * zz + 64 * u + 64], start=True, stop=True)
                            t.then_inc(s_zp, 1)
                        pe.wait_ge(s_zc, z * 8 + 10)
                        for m in range(16):
                            pe.wait_ge(s_x2, z * 16 + m + 1)
                            for i in range(2):
                                r = 2 * (2 * m + i)
                                t = pe.matmul(bank(2 + m % 2)[:, i * 256:(i + 1) * 256], Z[u][:, r:r + 2, :],
                                              idw[:], start=True, stop=True)
                            t.then_inc(s_yp, 1)
                barrier(pe, b, 4)

                stats(2)

                def scores(n, u, h, fresh):
                    px, q, hh = h // 4, h // 2 % 2, h % 2
                    for t2 in range(2):
                        pix = slice(px * 512 + (2 * hh + t2) * P, px * 512 + (2 * hh + t2 + 1) * P)
                        dst = bank(2 * hh + t2)
                        if not fresh:
                            pe.wait_ge(s_oh, 2 * n - 4 + t2 + 1)
                        pe.matmul(dst, LQ[u][q][:, pix], code_low[:], start=True, stop=False)
                        pe.matmul(dst, HQ[u][q][0:C + 2, pix], code_top[0:C + 2, :], start=False,
                                  stop=True).then_inc(s_sc, 1)

                def layer2_chunks(i, first, last):
                    k0, unit0, quarter0 = (b * 16 + i) * 16, (b * 16 + i) * 8, (b * 16 + i) * 4

                    def look_up(k):
                        q, px = k // 2 % 2, k // 4 % 2
                        pe.wait_ge(s_oca, unit0 + k // 2 + 2)
                        pe.wait_ge(s_ocd, unit0 + k // 2 + 2)
                        if q == 0:
                            pe.wait_ge(s_x3, quarter0 + k // 4 + 1)
                        dst = bank(6 + px)[q * C:(q + 1) * C, :]
                        for blk in range(4):
                            pe.matmul(dst, code_hi[:, blk, :], OTs[q][:, blk, :], start=blk == 0, stop=False)
                            t = pe.matmul(dst, code_lo[:, blk, :], OTs[q][:, blk, :], start=False, stop=blk == 3)
                        t.then_inc(s_cd, 1)

                    for k in range(16):
                        n, h, hh = k0 + k, k % 8, k % 2
                        if not (last and k >= 14):
                            if h == 6:
                                pe.wait_ge(s_hl[1 - k // 8], 96 * (b * 16 + i + 1 + k // 8))
                            scores(n + 2, (k + 2) // 8 % 2, (h + 2) % 8, False)
                        else:
                            pe.wait_ge(s_oh, 2 * n + 2)
                        pe.wait_ge(s_oca if hh else s_ocd, unit0 + k // 2 + 1)
                        dst = bank(4 + hh).bitcast(F16).rearrange("p (k n) -> p k n", k=4)
                        for t2 in range(2):
                            for blk in range(4):
                                t = pe.transpose(dst[:, blk, t2 * P:(t2 + 1) * P],
                                                 OH[2 * hh + t2][:, blk * P:(blk + 1) * P], id16[:])
                        t.then_inc(s_oht, 1)
                        if hh and not (first and k == 1):
                            look_up(k - 3)
                    if last:
                        look_up(14)

                pe.wait_ge(s_hl[0], 96 * (b * 16 + 1))
                scores(b * 256, 0, 0, True)
                scores(b * 256 + 1, 0, 1, True)
                layer2_chunks(0, True, False)
                with pe.Fori(1, 15) as i:
                    layer2_chunks(i, False, False)
                layer2_chunks(15, False, True)
                barrier(pe, b, 5)

                stats(3)

                def conv_group(dst, u, kk0, count, j):
                    taps = [(tap, pr, w3, src) for tap in range(3) for pr in range(2)
                            for w3, src in ((conv_hi, NH), (conv_lo, NH), (conv_hi, NL))]
                    for i, (tap, pr, w3, src) in enumerate(taps):
                        col = j - (tap + 1)
                        jj = col % 2
                        p0 = 2 + (col - jj) // 2
                        t = pe.matmul(dst, w3[:, pr * 3 + tap, :], src[u][:, kk0 + pr:kk0 + pr + count, jj, p0:p0 + P],
                                      start=i == 0, stop=i == len(taps) - 1)
                    return t

                def turn(n, m):
                    pe.wait_ge(s_rs, n + 5)
                    pe.wait_ge(s_oc, n + 1)
                    for i in range(4):
                        t = pe.transpose(bank(4 + m % 2)[:, i * P:(i + 1) * P], res[m][:, i * P:(i + 1) * P], id32[:])
                    t.then_inc(s_ct, 1)

                with pe.Fori(0, 8) as i:
                    for u in range(2):
                        c = b * CHUNKS + 2 * i + u
                        pe.wait_ge(s_cp, b * 17 + 2 * i + u + 2)
                        for m in range(4):
                            pe.wait_ge(s_rs, c * 4 + m + 1)
                            conv_group(bank(m), u, 4 * (m // 2), 4, m % 2).then_inc(s_cv, 1)
                            if u or m:
                                turn(c * 4 + m - 1, (m - 1) % 4)
                    turn(c * 4 + 3, 3)
                pe.wait_ge(s_cp, b * 17 + 18)
                conv_group(bank(6)[:, 0:P], 0, 0, 1, 0)
                conv_group(bank(6)[:, P:2 * P], 0, 0, 1, 1).then_inc(s_e, 1)
                pe.wait_ge(s_e, b * 5 + 3)
                for j in range(2):
                    t = pe.transpose(bank(7)[:, j * P:(j + 1) * P], edge[:, j * P:(j + 1) * P], id32[:])
                t.then_inc(s_e, 1)
                barrier(pe, b, 6)

        @block.scalar
        def _(act):
            for free, count in ((s_xin, 2), (s_wb, 2), (s_mo, 2), (s_g, 4), (s_xtc, 2), (s_atc, 2), (s_zc, 2),
                                (s_oc, 2), (s_oca, 1)):
                act.sem_inc(free, count)
            act.wait_ge(s_const, 16 * len(CONSTS))
            with act.Fori(0, B) as b:
                def stats(layer):
                    base = st_base(b, layer)
                    act.wait_ge(s_st, base + 6)
                    act.activation(sd, var, ACT.Sqrt).then_inc(s_st, 1)

                with act.Fori(0, 8) as c2:
                    for u in range(2):
                        c = b * CHUNKS + 2 * c2 + u
                        for m in range(4):
                            act.wait_ge(s_tp, c * 4 + m + 1)
                            act.activation(X[:, ds((2 * c2 + u) * 2048 + m * 512, 512)], bank(m % 2),
                                           ACT.Copy).then_inc(s_xin, 1)
                        act.wait_ge(s_wa, c + 2)
                        act.activation(R1[:, ds((2 * c2 + u) * 512, 512)], bank(2 + u), ACT.Copy).then_inc(s_wb, 1)
                barrier(act, b, 0)
                stats(0)
                act.wait_ge(s_st, st_base(b, 0) + NST)
                act.wait_ge(s_folded, 2 * b + 1)
                with act.Fori(0, 8) as g:
                    for u in range(2):
                        n = b * 16 + 2 * g + u
                        act.wait_ge(s_mt, n + 1)
                        src = bank(u).rearrange("p (m n) -> p m n", n=P)
                        act.activation(mbt[u][:, :, 0:C], src[:, :, 0:C], ACT.Identity, bias=nbl[:], scale=rs)
                        act.activation(mbt[u][:, :, C:P], src[:, :, C:P], ACT.Copy, scale=rs).then_inc(s_mb, 1)
                    for u in range(2):
                        n = b * 16 + 2 * g + u
                        act.wait_ge(s_mm, n + 1)
                        act.activation(R1[:, ds((2 * g + u) * 512, 512)], bank(2 + u), ACT.Copy).then_inc(s_mo, 1)
                barrier(act, b, 1)

                def gelu(n, m):
                    act.wait_ge(s_l0, n + 1)
                    act.wait_ge(s_xt, n + 1)
                    act.wait_ge(s_x1n, n + 1)
                    act.activation(x1b[m % 2], bank(m), ACT.Gelu_apprx_tanh, bias=fb).then_inc(s_g, 1)

                def copies(c, last):
                    for m in range(4):
                        n = (b * CHUNKS + c) * 4 + m
                        if not (last and m == 3):
                            gelu(n + 1, (m + 1) % 4)
                        act.wait_ge(s_xt, n + 3)
                        act.wait_ge(s_fa, n + 1)
                        act.activation(x1t[m % 2], bank(4 + m % 2).rearrange("p (n m) -> p n m", m=P),
                                       ACT.Copy).then_inc(s_xtc, 1)

                act.wait_ge(s_folded, 2 * b + 2)
                gelu(b * 64, 0)
                with act.Fori(0, CHUNKS - 1) as c:
                    copies(c, False)
                copies(CHUNKS - 1, True)
                barrier(act, b, 2)

                stats(1)
                for g in range(8):
                    act.wait_ge(s_at, b * 8 + g + 1)
                    act.wait_ge(s_fg, b * 8 + g + 1)
                    act.activation(aft[g % 2], bank(g % 2).rearrange("p (n m) -> p n m", m=P),
                                   ACT.Copy).then_inc(s_atc, 1)
                mixed = bank(3)[0:C, :].rearrange("p (y n t) -> p y n t", n=MODES, t=2)
                act.wait_ge(s_om, b * 8 + 8)
                act.activation(om, mixed, ACT.Copy).then_inc(s_oms, 1)
                act.activation(om2[:, :, :, 0], mixed[:, :, :, 1], ACT.Copy).then_inc(s_oms, 1)
                act.activation(om2[:, :, :, 1], mixed[:, :, :, 0], ACT.Copy, scale=-1.0).then_inc(s_oms, 1)
                act.wait_ge(s_ot, b + 1)
                for s in range(2):
                    for yh in range(2):
                        act.activation(OT[:, :, s, 8 * yh:8 * yh + 8].rearrange("p o y -> p y o"),
                                       bank(4 + 2 * s + yh)[0:32, :].rearrange("p (y o) -> p y o", o=C), ACT.Copy)
                barrier(act, b, 3)
                with act.Fori(0, 2) as zz:
                    for u in range(2):
                        z = b * 4 + 2 * zz + u
                        for g in range(8):
                            act.wait_ge(s_zp, z * 8 + g + 1)
                            if g == 0:
                                act.wait_ge(s_yp, (b * 4 + 2 * zz) * 16 + 1)
                            act.activation(Z[u][:, :, 8 * g:8 * g + 8].rearrange("p h o -> p o h"),
                                           bank(g % 2)[0:32, :].rearrange("p (o h) -> p o h", h=64),
                                           ACT.Copy).then_inc(s_zc, 1)
                barrier(act, b, 4)
                stats(2)
                act.wait_ge(s_st, st_base(b, 2) + NST)

                def high(at, u):
                    act.activation(XH[u], X[:, ds(at, 1024)], ACT.Identity, bias=nb, scale=rs).then_inc(s_xh, 1)

                def one_hots(i, first, last):
                    k0, unit0 = (b * 16 + i) * 16, (b * 16 + i) * 8

                    def copy_odd(k):
                        q = k // 2 % 2
                        act.wait_ge(s_oht, 2 + k0 + k + 1)
                        act.wait_ge(s_cd, unit0 + k // 2 + 1)
                        act.activation(OTs[q][:, :, 256:512], bank(5).bitcast(F16).rearrange(
                            "p (k n) -> p k n", k=4), ACT.Copy).then_inc(s_oca, 1)

                    for k in range(16):
                        n, hh = k0 + k, k % 2
                        act.wait_ge(s_oht, n + 1)
                        for t2 in range(2):
                            act.wait_ge(s_mxs, 2 * n + t2 + 1)
                            act.activation(OH[2 * hh + t2], bank(2 * hh + t2), ACT.Exp,
                                           bias=negsharp[:, hh, t2:t2 + 1], scale=SHARP).then_inc(s_oh, 1)
                        if k % 2 == 0 and not (first and k == 0):
                            copy_odd(k - 1)
                        if k % 8 == 3 and not last:
                            u = k // 8
                            act.wait_ge(s_hl[u], 96 * (b * 16 + i + 1))
                            act.wait_ge(s_xl, b * 32 + 2 * i + u + 1)
                            high((2 * i + u + 2) * 1024, u)
                    if last:
                        copy_odd(15)

                high(0, 0)
                high(1024, 1)
                one_hots(0, True, False)
                with act.Fori(1, 15) as i:
                    one_hots(i, False, False)
                one_hots(15, False, True)
                barrier(act, b, 5)
                stats(3)
                act.wait_ge(s_st, st_base(b, 3) + NST)

                def conv_high(at, u):
                    act.activation(NH[u][:, 1:9, :, 2:130], X[:, ds(at, 2048)].rearrange(
                        "p (k j n) -> p k j n", j=2, n=P), ACT.Identity, bias=nb, scale=rs).then_inc(s_nh, 1)

                def out_copies(i, last):
                    for u in range(2):
                        c = b * CHUNKS + 2 * i + u
                        for m in range(4):
                            n = c * 4 + m
                            if m == 3 and not last:
                                act.wait_ge(s_cv, c * 4 + 8)
                                act.wait_ge(s_cp, b * 17 + 2 * i + u + 3)
                                conv_high((2 * i + u + 2) * 2048, u)
                            if m == 0:
                                act.wait_ge(s_out[u], 32 * (b * 8 + i + 1))
                            act.wait_ge(s_ct, n + 5)
                            src = bank(4 + m % 2).rearrange("p (k r o) -> p k r o", r=2, o=C)
                            dst = ost[u].rearrange("p (k r) j o -> p k r j o", r=2)[:, 4 * (m // 2):4 * (m // 2) + 4]
                            act.activation(dst[:, :, 1, m % 2, :], src[:, :, 0, :], ACT.Copy)
                            act.activation(dst[:, :, 0, m % 2, :], src[:, :, 1, :], ACT.Copy).then_inc(s_oc, 1)

                act.wait_ge(s_pad, 2 * b + 2)
                conv_high(0, 0)
                act.wait_ge(s_cp, b * 17 + 2)
                conv_high(2048, 1)
                with act.Fori(0, 7) as i:
                    out_copies(i, False)
                out_copies(7, True)
                act.wait_ge(s_e, b * 5 + 4)
                act.activation(edge_t.rearrange("p (j o) -> p j o", o=C),
                               bank(7)[:, 0:2 * P].rearrange("p (j r o) -> p j r o", r=2, o=C)[:, :, 0, :],
                               ACT.Copy).then_inc(s_e, 1)
                barrier(act, b, 6)

        @block.vector
        def _(dve):
            for free, count in ((s_x1n, 2), (s_fac, 1), (s_x2, 2), (s_ocd, 1), (s_x3, 2), (s_rs, 4), (s_cp, 1)):
                dve.sem_inc(free, count)
            dve.memset(neghalf, -0.5 / CSCALE).then_inc(s_prep, 1)
            dve.wait_ge(s_const, 16 * len(CONSTS))
            dve.tensor_scalar(ct32, ct32, CSCALE, None, ALU.mult).then_inc(s_prep, 1)
            dve.tensor_scalar(c32, c32, CSCALE, None, ALU.mult).then_inc(s_prep, 1)
            dve.wait_ge(s_prep, 3)
            dve.tensor_copy(code_top[0:C, :], ct32[0:C, :])
            dve.tensor_copy(code_low[0:C, :], ct32[0:C, :]).then_inc(s_prep, 1)
            dve.tensor_copy(hi16, ct32).then_inc(s_prep, 1)
            dve.tensor_copy(code_hi[:], c32).then_inc(s_prep, 1)
            dve.tensor_copy(conv_hi[:], cv32).then_inc(s_prep, 1)
            dve.wait_ge(s_prep, 7)
            dve.tensor_tensor(code_low[C:P, :], ct32[C:P, :], hi16[C:P, :], ALU.subtract)
            dve.tensor_tensor(code_lo[:], c32, code_hi[:], ALU.subtract).then_inc(s_prep, 1)
            dve.tensor_tensor(conv_lo[:], cv32, conv_hi[:], ALU.subtract).then_inc(s_prep, 1)
            dve.tensor_tensor(sq, ct32[0:C, :], ct32[0:C, :], ALU.mult).then_inc(s_prep, 1)
            dve.wait_ge(s_prep, 11)
            dve.tensor_copy(bias_row, bank(0)[0:1, :]).then_inc(s_prep, 1)
            dve.wait_ge(s_prep, 12)
            dve.tensor_copy(row16[:, 0:NCODE], bias_row).then_inc(s_lf, 1)
            dve.tensor_copy(id16[:], id32[:])
            dve.memset(X[:, NPX:NPX + PAIR], 0.0)
            dve.memset(nbl[:], 0.0).then_inc(s_lf, 1)
            dve.wait_ge(s_lf, 2)
            dve.tensor_tensor(row16[:, NCODE:2 * NCODE], bias_row, row16[:, 0:NCODE], ALU.subtract).then_inc(s_prep, 1)

            with dve.Fori(0, B) as b:
                def stats(layer):
                    base = st_base(b, layer)
                    dve.bn_aggr(agg[:], bnst[:]).then_inc(s_st, 1)
                    dve.wait_ge(s_st, base + 2)
                    dve.tensor_tensor(dev, agg[:, 0:1], mg, ALU.subtract).then_inc(s_st, 1)
                    dve.wait_ge(s_st, base + 3)
                    dve.scalar_tensor_tensor(e2, dev, dev, agg[:, 1:2], ALU.mult, ALU.add).then_inc(s_st, 1)
                    dve.wait_ge(s_st, base + 5)
                    dve.tensor_scalar(var, bank(7)[:, 1:2], EPS, None, ALU.add).then_inc(s_st, 1)
                    dve.wait_ge(s_st, base + 7)
                    dve.reciprocal(y0, sd).then_inc(s_st, 1)
                    dve.wait_ge(s_st, base + 8)
                    dve.scalar_tensor_tensor(y2, y0, var, y0, ALU.mult, ALU.mult).then_inc(s_st, 1)
                    dve.wait_ge(s_st, base + 9)
                    dve.tensor_scalar(y3, y2, -0.5, 1.5, ALU.mult, ALU.add).then_inc(s_st, 1)
                    dve.wait_ge(s_st, base + 10)
                    dve.tensor_tensor(rs, y0, y3, ALU.mult).then_inc(s_st, 1)
                    dve.wait_ge(s_st, base + 11)
                    dve.scalar_tensor_tensor(nb, mg, -1.0, rs, ALU.mult, ALU.mult).then_inc(s_st, 1)
                    dve.wait_ge(s_st, base + 12)

                def measure(src, at):
                    return dve.bn_stats(bnst[:, ds(at, 6)], src)

                with dve.Fori(0, 8) as c2:
                    for u in range(2):
                        c = b * CHUNKS + 2 * c2 + u
                        for j in range(2):
                            n = c * 2 + j
                            dve.wait_ge(s_padd, (n + 1) * 2)
                            dve.scalar_tensor_tensor(ta[:, j], tb[:, j], -0.5, ta[:, j],
                                                     ALU.mult, ALU.add).then_inc(s_dl, 1)
                            dve.wait_ge(s_dl, n + 1)
                            dve.scalar_tensor_tensor(tb[:, j], T[u][:, j, 2:18:2, :], 3.0,
                                                     ta[:, j], ALU.mult, ALU.add).then_inc(s_s1, 1)
                        for m in range(4):
                            dve.wait_ge(s_xin, 2 + c * 4 + m + 1)
                            measure(X[:, ds((2 * c2 + u) * 2048 + m * 512, 512)], ((2 * c2 + u) * 4 + m) * 6)
                barrier(dve, b, 0)
                even, odd = Bv[:, :, 0, :], Bv[:, :, 1, :]
                def neighbours(i, dst, src, ahead):
                    dve.wait_ge(s_lf, 2 + b * 8 + 2 * i)
                    if ahead:
                        dve.tensor_tensor(dst[:, 0:63, :], src[:, 0:63, :], src[:, 1:64, :], ALU.add)
                        t = dve.tensor_tensor(dst[:, 63, :], src[:, 63, :], src[:, 0, :], ALU.add)
                    else:
                        dve.tensor_tensor(dst[:, 1:64, :], src[:, 1:64, :], src[:, 0:63, :], ALU.add)
                        t = dve.tensor_tensor(dst[:, 0, :], src[:, 0, :], src[:, 63, :], ALU.add)
                    t.then_inc(s_lf, 1)
                    dve.wait_ge(s_lf, 2 + b * 8 + 2 * i + 1)

                def lift_into(dst, factor):
                    dve.scalar_tensor_tensor(dst, lift, factor, dst, ALU.mult, ALU.add).then_inc(s_lf, 1)

                neighbours(0, lift, even, True)
                lift_into(odd, -0.5)
                neighbours(1, lift, odd, False)
                lift_into(even, 0.25)
                stats(0)
                dve.tensor_copy(nbl[0:C, :], nb[0:C, :])
                dve.tensor_scalar(dnf[:], dn[:], rs, None, ALU.mult).then_inc(s_folded, 1)
                dve.wait_ge(s_mo, 2 + b * 16 + 16)
                neighbours(2, lift, odd, False)
                lift_into(even, -0.25)
                neighbours(3, lift, even, True)
                lift_into(odd, 0.5)
                dve.wait_ge(s_lf, 2 + b * 8 + 8)
                dve.tensor_copy(R1[:, P * C:P * C + C], R1[:, 0:C])
                dve.wait_ge(s_fold, b + 1)
                dve.tensor_tensor(fb, bank(7)[:, 2:3], dbias[:], ALU.add).then_inc(s_folded, 1)
                barrier(dve, b, 1)

                with dve.Fori(0, CHUNKS) as c:
                    for m in range(4):
                        n = (b * CHUNKS + c) * 4 + m
                        dve.wait_ge(s_g, 4 + n + 1)
                        dve.tensor_tensor(x1b[m % 2], x1b[m % 2], X[:, ds(c * 2048 + m * 512, 512)],
                                          ALU.add).then_inc(s_x1, 1)
                        dve.wait_ge(s_x1, n + 1)
                        measure(x1b[m % 2], (c * 4 + m) * 6)
                        dve.tensor_copy(X[:, ds(c * 2048 + m * 512, 512)], x1b[m % 2]).then_inc(s_x1n, 1)
                    dve.wait_ge(s_fa, (b * CHUNKS + c) * 4 + 5)
                    dve.tensor_copy(SCR[:, ds(c * 256, 256)], bank(6)[:, 0:256]).then_inc(s_fac, 1)
                barrier(dve, b, 2)

                stats(1)
                dve.wait_ge(s_fg, 2 + b * 8 + 8)
                F = bank(2).rearrange("p (y t n) -> p t y n", t=2, n=MODES)
                V = DV.rearrange("p t (y n) -> p t y n", n=MODES)
                lo, up = slice(0, C), slice(C, P)
                dve.tensor_scalar(V[lo, 0], F[lo, 0], rs[lo, :], None, ALU.mult).then_inc(s_dv, 1)
                dve.tensor_scalar(V[lo, 1], F[lo, 1], rs[lo, :], None, ALU.mult).then_inc(s_dv, 1)
                dve.tensor_scalar(V[up, 0], F[up, 1], rs[up, :], -1.0, ALU.mult, ALU.mult).then_inc(s_dv, 1)
                dve.tensor_scalar(V[up, 1], F[up, 0], rs[up, :], None, ALU.mult).then_inc(s_dv, 1)
                dve.wait_ge(s_dv, b * 6 + 4)
                dve.scalar_tensor_tensor(DV[lo, 0, 0:1], nb[lo, :], float(W), DV[lo, 0, 0:1], ALU.mult, ALU.add).then_inc(s_dv, 1)
                dve.scalar_tensor_tensor(DV[up, 1, 0:1], nb[up, :], float(W), DV[up, 1, 0:1], ALU.mult, ALU.add).then_inc(s_dv, 1)
                barrier(dve, b, 3)
                with dve.Fori(0, 2) as zz:
                    for u in range(2):
                        for m in range(16):
                            n = (b * 4 + 2 * zz + u) * 16 + m
                            at = (2 * zz + u) * 16 + m
                            dve.wait_ge(s_yp, n + 2)
                            dve.tensor_tensor(X[:, ds(at * 512, 512)], bank(2 + m % 2), X[:, ds(at * 512, 512)],
                                              ALU.add).then_inc(s_x2, 1)
                            dve.wait_ge(s_x2, 2 + n + 1)
                            measure(X[:, ds(at * 512, 512)], at * 6)
                barrier(dve, b, 4)

                stats(2)

                def maximum(n, hh, t2):
                    dve.wait_ge(s_sc, 2 * n + t2 + 1)
                    dve.tensor_reduce(negmax[:, hh, t2:t2 + 1], bank(2 * hh + t2), AX.X,
                                      ALU.max, negate=True).then_inc(s_mx, 1)

                def scale_maximum(n, hh, t2):
                    dve.wait_ge(s_mx, 2 * n + t2 + 1)
                    dve.tensor_scalar(negsharp[:, hh, t2:t2 + 1], negmax[:, hh, t2:t2 + 1], SHARP, None,
                                      ALU.mult).then_inc(s_mxs, 1)

                def vector_steps(i, first, last):
                    k0, unit0, quarter0 = (b * 16 + i) * 16, (b * 16 + i) * 8, (b * 16 + i) * 4

                    def add_codes(k):
                        dve.wait_ge(s_cd, 2 + unit0 + k // 2 + 1)
                        at = 2 * i * 1024 + (k // 4) * 512
                        dve.scalar_tensor_tensor(X[:, ds(at, 512)], bank(6 + k // 4 % 2), 1.0 / CSCALE,
                                                 X[:, ds(at, 512)], ALU.mult, ALU.add).then_inc(s_x3, 1)

                    def measure_codes(k):
                        dve.wait_ge(s_x3, 2 + quarter0 + k // 4 + 1)
                        measure(X[:, ds(2 * i * 1024 + (k // 4) * 512, 512)], (2 * i * 2 + k // 4) * 6)

                    for k in range(16):
                        hh, q = k % 2, k // 2 % 2
                        ahead = not (last and k >= 14)
                        if ahead:
                            maximum(k0 + k + 2, hh, 0)
                            maximum(k0 + k + 2, hh, 1)
                            scale_maximum(k0 + k + 2, hh, 0)
                        if hh == 0:
                            dve.wait_ge(s_oht, 2 + k0 + k + 1)
                            dve.wait_ge(s_cd, unit0 + k // 2 + 1)
                            dve.tensor_copy(OTs[q][:, :, 0:256],
                                            bank(4).bitcast(F16).rearrange("p (k n) -> p k n", k=4)).then_inc(s_ocd, 1)
                        elif k % 4 == 3 and not (first and k == 3):
                            add_codes(k - 4)
                        elif k % 4 == 1 and not (first and k <= 5):
                            measure_codes(k - 6)
                        if ahead:
                            scale_maximum(k0 + k + 2, hh, 1)
                    if last:
                        measure_codes(11)
                        add_codes(15)
                        measure_codes(15)

                for k in range(2):
                    for t2 in range(2):
                        maximum(b * 256 + k, k, t2)
                        scale_maximum(b * 256 + k, k, t2)
                vector_steps(0, True, False)
                with dve.Fori(1, 15) as i:
                    vector_steps(i, False, False)
                vector_steps(15, False, True)
                barrier(dve, b, 5)

                stats(3)

                def residuals(i):
                    for u in range(2):
                        c = b * CHUNKS + 2 * i + u
                        for m in range(4):
                            n = c * 4 + m
                            dve.wait_ge(s_cv, n + 5)
                            dve.wait_ge(s_ct, n + 1)
                            k0 = ((2 * i + u) * 8 + 4 * (m // 2)) * 2 + m % 2
                            X4 = X[:, :].rearrange("p (k n) -> p k n", n=P)
                            src = bank(m).rearrange("p (k n) -> p k n", n=P)
                            dst = res[m].rearrange("p (k n) -> p k n", n=P)
                            dve.scalar_tensor_tensor(dst[0:C], src[0:C], cbias[0:C, :],
                                                     X4[0:C, ds(k0 + 2, 4, 2), :], ALU.add, ALU.add)
                            dve.scalar_tensor_tensor(dst[C:P], src[C:P], cbias[C:P, :],
                                                     X4[C:P, ds(k0, 4, 2), :], ALU.add, ALU.add).then_inc(s_rs, 1)

                past(dve)
                with dve.Fori(0, 8) as i:
                    residuals(i)
                dve.wait_ge(s_cv, (b * CHUNKS + 16) * 4 + 4)
                dve.wait_ge(s_cp, b * 17 + 17)
                for buf in (NH, NL):
                    dve.tensor_copy(buf[0][:, 0, :, :], buf[1][:, 8, :, :])
                    t = dve.memset(buf[0][:, 1, :, :], 0.0)
                t.then_inc(s_cp, 1)
                dve.wait_ge(s_e, b * 5 + 1)
                dve.scalar_tensor_tensor(edge[0:C, :], bank(6)[0:C, 0:PAIR], cbias[0:C, :], X[0:C, 0:PAIR],
                                         ALU.add, ALU.add).then_inc(s_e, 1)
                dve.memset(edge[C:P, :], 0.0).then_inc(s_e, 1)
                barrier(dve, b, 6)

        @block.gpsimd
        def _(pool):
            pool.wait_ge(s_prep, 13)
            pool.wait_ge(s_const, 16 * (len(CONSTS) + 2))
            with pool.Fori(0, B) as b:
                with pool.Fori(0, 8) as c2:
                    for u in range(2):
                        c = b * CHUNKS + 2 * c2 + u
                        pool.wait_ge(s_tile[u], 96 * (b * 8 + c2 + 1))
                        pool.wait_ge(s_wa, c + 1)
                        for j in range(2):
                            pool.tensor_tensor(ta[:, j], T[u][:, j, 1:16:2, :], T[u][:, j, 3:18:2, :],
                                               ALU.add).then_inc(s_padd, 1)
                            pool.tensor_tensor(tb[:, j], T[u][:, j, 0:15:2, :], T[u][:, j, 4:19:2, :],
                                               ALU.add).then_inc(s_padd, 1)
                barrier(pool, b, 0)
                pool.wait_ge(s_folded, 2 * b + 1)
                past(pool)
                with pool.Fori(0, 8) as g:
                    for u in range(2):
                        pool.wait_ge(s_mo, b * 16 + 2 * g + u + 1)
                        pool.tensor_copy(mst[u], R1[:, ds((2 * g + u) * 512, 512)]).then_inc(s_mc, 1)
                barrier(pool, b, 1)

                def interpolate(at, u):
                    a = R1[:, ds(at, 256)].rearrange("p (k o) -> p k o", o=C)
                    a1 = R1[:, ds(at + C, 256)].rearrange("p (k o) -> p k o", o=C)
                    pool.tensor_tensor(syn[u][:, :, 0, :], a, a, ALU.add)
                    pool.tensor_tensor(syn[u][:, :, 1, :], a, a1, ALU.add).then_inc(s_sy, 1)

                interpolate(0, 0)
                interpolate(256, 1)
                with pool.Fori(0, CHUNKS - 1) as c:
                    for u in range(2):
                        pool.wait_ge(s_l0, (b * CHUNKS + c) * 4 + 2 * u + 2)
                        interpolate(c * 512 + 512 + 256 * u, u)
                barrier(pool, b, 2)
                barrier(pool, b, 3)
                barrier(pool, b, 4)
                for u in range(2):
                    for q in range(2):
                        t = pool.memset(HQ[u][q][C:C + 32, :], 1.0)
                t.then_inc(s_pad, 1)
                pool.wait_ge(s_pad, 2 * b + 1)
                pool.wait_ge(s_st, st_base(b, 2) + NST)
                past(pool)

                def low(n, at, u):
                    pool.tensor_tensor(XN[u], X[:, ds(at, 1024)], wide(rs, 1024), ALU.mult).then_inc(s_xn, 1)
                    pool.wait_ge(s_xn, 2 * n + 1)
                    past(pool)
                    pool.tensor_scalar(XN[u], XN[u], nb, None, ALU.add).then_inc(s_xn, 1)
                    pool.wait_ge(s_xn, 2 * n + 2)
                    pool.wait_ge(s_xh, n + 1)
                    pool.tensor_tensor(XL[u], XN[u], XH[u], ALU.subtract).then_inc(s_xl, 1)

                low(b * 32, 0, 0)
                low(b * 32 + 1, 1024, 1)
                with pool.Fori(0, 15) as i:
                    for u in range(2):
                        pool.wait_ge(s_hl[u], 96 * (b * 16 + i + 1))
                        past(pool)
                        low(b * 32 + 2 * i + u + 2, (2 * i + u + 2) * 1024, u)
                barrier(pool, b, 5)
                for buf in (NH, NL):
                    for u in range(2):
                        pool.memset(buf[u][:, :, :, 0:2], 0.0)
                    t = pool.memset(buf[1][:, 8, :, 2:130], 0.0)
                t.then_inc(s_pad, 1)
                pool.wait_ge(s_pad, 2 * b + 2)
                pool.wait_ge(s_st, st_base(b, 3) + NST)
                past(pool)

                def conv_low(n, at, u, edges):
                    pool.tensor_tensor(XM, X[:, ds(at, 2048)], wide(rs, 2048), ALU.mult).then_inc(s_nn, 1)
                    pool.wait_ge(s_nn, 2 * n + 1)
                    past(pool)
                    pool.tensor_scalar(XM, XM, nb, None, ALU.add).then_inc(s_nn, 1)
                    pool.wait_ge(s_nn, 2 * n + 2)
                    pool.wait_ge(s_nh, n + 1)
                    pool.tensor_tensor(NL[u][:, 1:9, :, 2:130], XM.rearrange("p (k j n) -> p k j n", j=2, n=P),
                                       NH[u][:, 1:9, :, 2:130], ALU.subtract).then_inc(s_nl, 1)
                    pool.wait_ge(s_nl, n + 1)
                    pool.wait_ge(s_cp, edges)
                    past(pool)
                    for buf in (NH, NL):
                        pool.tensor_copy(buf[u][:, 0, :, :], buf[1 - u][:, 8, :, :])
                        t = pool.tensor_copy(buf[u][:, 1:9, 1, 0:1], buf[u][:, 1:9, 1, 129:130])
                    t.then_inc(s_cp, 1)

                conv_low(b * CHUNKS, 0, 0, b * 17 + 1)
                conv_low(b * CHUNKS + 1, 2048, 1, b * 17 + 2)
                with pool.Fori(0, 7) as i:
                    for u in range(2):
                        conv_low(b * CHUNKS + 2 * i + u + 2, (2 * i + u + 2) * 2048, u, b * 17 + 2 * i + u + 3)
                barrier(pool, b, 6)

    return nc


def cdf53(n, level):
    cur = np.eye(n)
    for _ in range(level):
        e, o = cur[0::2], cur[1::2]
        d = o - 0.5 * (e + np.roll(e, -1, 0))
        s = e + 0.25 * (d + np.roll(d, 1, 0))
        cur, high = s, d
    return np.concatenate([cur, high])


def uncdf53(s, d):
    e = s - 0.25 * (d + np.roll(d, 1, 0))
    o = d + 0.5 * (e + np.roll(e, -1, 0))
    return np.stack([e, o], 1).reshape(2 * len(e), -1)


def shape_constants():
    f32 = np.float32
    a = cdf53(W, 2) / 4.0
    w_analysis = a.reshape(P, P, 2).transpose(1, 2, 0)
    low, high = np.eye(P)[:C], np.eye(P)[C:]
    s = uncdf53(low, high)
    s = uncdf53(s, np.zeros_like(s)) / 2.0
    w_synthesis = s.reshape(P, 2, P).transpose(2, 1, 0).reshape(P, 2 * P)
    k, m = np.arange(W), np.arange(MODES)
    ang = 2 * np.pi * np.outer(k, m) / W
    cos, sin = np.cos(ang), np.sin(ang)
    dft_w = np.stack([cos, -sin], 2).reshape(P, 2, 2 * MODES) / W
    c2, s2 = cos.reshape(P, 2, MODES), sin.reshape(P, 2, MODES)
    dft_h = np.stack([np.concatenate([c2, -s2], 2), np.concatenate([s2, c2], 2)], 2).reshape(P, 4, 2 * MODES)
    idft_h = np.stack([cos, -sin], 2).reshape(W, 2 * MODES).T
    twice = np.where(m == 0, 1.0, 2.0)[:, None] / W
    order = k.reshape(P, 2).T.reshape(-1)
    idft_w = np.concatenate([cos.T * twice, -sin.T * twice])[:, order]
    pair = np.arange(P) % C // 2
    group = (pair[:, None] == pair[None, :]) / 4.0
    return {"ident": np.eye(P, dtype=f32), "group": group.astype(f32), "w_analysis": w_analysis.astype(f32),
            "w_synthesis": w_synthesis.astype(f32), "dft_w": dft_w.astype(f32), "dft_h": dft_h.astype(f32),
            "idft_h": idft_h.astype(f32), "idft_w": idft_w.astype(f32)}


def two_blocks(a, b):
    out = np.zeros((2 * C, 2 * C), a.dtype)
    out[:C, :C] = a
    out[C:, C:] = b
    return out


def kernel(x, L0_conv_w_approx, L0_conv_w_detail, L0_conv_dense_kernel, L0_conv_dense_bias,
           L1_conv_weights_real, L1_conv_weights_imag, L2_conv_codebook, L3_conv_kernel, L3_conv_bias):
    import concourse.bacc as bacc
    from concourse.bass_utils import run_bass_kernel_spmd as run

    x = np.ascontiguousarray(x)
    det = np.asarray(L0_conv_w_detail)
    both = np.concatenate([np.asarray(L1_conv_weights_real), np.asarray(L1_conv_weights_imag)])
    modes = both.transpose(0, 3, 2, 1).reshape(P, MODES * MODES, C)
    book = np.asarray(L2_conv_codebook)
    taps = np.asarray(L3_conv_kernel).transpose(2, 3, 1, 0)
    conv = np.zeros((P, 6, P), np.float32)
    for half, row in ((0, 2), (1, 1)):
        for pr in range(2):
            for q in range(2):
                back = row - (2 * (pr - 1) + q)
                if 1 <= back <= 3:
                    for t in range(3):
                        conv[q * C:(q + 1) * C, pr * 3 + t, half * C:(half + 1) * C] = taps[back - 1, t]
    twice = lambda v: np.ascontiguousarray(np.concatenate([np.asarray(v).reshape(C, 1)] * 2))
    arrays = {
        "x": x,
        "dense": two_blocks(np.asarray(L0_conv_dense_kernel), np.asarray(L0_conv_dense_kernel)),
        "dense_bias": twice(L0_conv_dense_bias),
        "mix_low": two_blocks(np.asarray(L0_conv_w_approx)[:, :, 0, 0], det[..., 0]),
        "mix_high": two_blocks(det[..., 1], det[..., 2]),
        "modes": np.ascontiguousarray(modes),
        "codes": np.ascontiguousarray(book.reshape(4, P, C).transpose(1, 0, 2)),
        "codes_t": np.ascontiguousarray(np.concatenate([book.T, book.T])),
        "conv": conv,
        "conv_bias": twice(L3_conv_bias),
        **shape_constants(),
    }
    nc = bacc.Bacc("TRN2", target_bir_lowering=False, num_devices=1)
    args = {}
    for name, a in arrays.items():
        arrays[name] = a = np.ascontiguousarray(a)
        args[name] = nc.dram_tensor(name, a.shape, mybir.dt.from_np(a.dtype), kind="ExternalInput").ap()
    out = nc.dram_tensor("out", x.shape, F32, kind="ExternalOutput").ap()
    fused_layers(nc, out=out, **args)
    r = run(nc, [arrays], core_ids=[0])
    return r.results[0]["out"]
```

```python
from contextlib import ExitStack

import concourse.bass as bass
import numpy as np
from concourse import mybir

F32 = mybir.dt.float32
F16 = mybir.dt.float16
ALU = mybir.AluOpType
ACT = mybir.ActivationFunctionType
AX = mybir.AxisListType
ds = bass.ds

C = 64
W = 256
P = 128
PAIR = 2 * P
MODES = 16
NCODE = 512
CSCALE = 64.0
YSCALE = 256.0
WSCALE = 64.0
SHARP = 2.0 ** 50
EPS = 1e-5
ENGINES = 5
PHASES = 7


def fused_layers(nc, x, dense, dense_bias, mix_low, mix_high, modes, codes, codes_t, conv, conv_bias,
                 ident, group, fold, w_analysis, w_synthesis, dft_w, dft_h, idft_h, idft_w, out):
    B = x.shape[0]
    NPX = P * PAIR
    ctx = ExitStack()
    with ctx:
        def sb(name, shape, dt=F32):
            return ctx.enter_context(nc.sbuf_tensor(name, shape, dt))

        def sem(name):
            return ctx.enter_context(nc.semaphore(name))

        X = sb("X", [P, NPX + PAIR])
        R1 = sb("R1", [P, 129 * C])
        SCR = sb("SCR", [P, 7680])
        id32 = sb("id32", [P, P])
        id16 = sb("id16", [P, P], F16)
        grp = sb("grp", [P, P])
        fld = sb("fld", [P, 5, C])
        wan = sb("wan", [P, 2, P])
        wsy = sb("wsy", [P, 2 * P], F16)
        dn = sb("dn", [P, P])
        dnf = sb("dnf", [P, P])
        mixw = sb("mixw", [P, 2, P])
        dfw = sb("dfw", [P, 2, 64], F16)
        dfh = sb("dfh", [P, 4, 32])
        idh = sb("idh", [96, W], F16)
        idw = sb("idw", [96, 2 * P], F16)
        dbias = sb("dbias", [P, 1])
        cbias = sb("cbias", [P, 1])
        code_top = sb("code_top", [P, NCODE], F16)
        code_low = sb("code_low", [P, NCODE], F16)
        code_hi = sb("code_hi", [P, 4, C], F16)
        code_lo = sb("code_lo", [P, 4, C], F16)
        conv_hi = sb("conv_hi", [P, 6, P], F16)
        conv_lo = sb("conv_lo", [P, 6, P], F16)
        bnst = sb("bnst", [P, 64 * 6])
        agg = sb("agg", [P, 2])
        tiny = sb("tiny", [P, 12])
        negmax = sb("negmax", [P, 2, 2])
        negsharp = sb("negsharp", [P, 2, 2])
        dev, e2, var, sd, y0, y2, y3, rs, nb, fb = (tiny[:, i:i + 1] for i in range(10))
        nbl = sb("nbl", [P, 1])

        PS = ctx.enter_context(nc.psum_tensor("PS", [P, 8 * 512], F32))

        def bank(i, n=1):
            return PS[:, i * 512:(i + n) * 512]

        mg = bank(7)[:, 0:1]

        def mixed(half):
            return bank(2 + half).rearrange("p (y n t) -> p y n t", n=MODES, t=4)

        def modes_out(k, s, yh):
            return OT[32 * k:32 * k + 32, :, s, 8 * yh:8 * yh + 8].rearrange("p o y -> p y o")

        def modes_in(s, yh):
            return bank(4 + 2 * s + yh)[0:32, :].rearrange("p (y o) -> p y o", o=C)

        def block_out(z, k, g):
            return Z[z % 2][32 * k:32 * k + 32, :, 8 * g:8 * g + 8].rearrange("p h o -> p o h")

        def block_in(g):
            return bank(g % 2)[0:32, :].rearrange("p (o h) -> p o h", h=64)

        def wide(column, n):
            return bass.AP(column.tensor, column.offset, [column.ap[0], [0, n]])

        T = [SCR[:, u * 2432:(u + 1) * 2432].rearrange("p (j r c) -> p j r c", j=2, c=C) for u in range(2)]
        ta = SCR[:, 4864:5888].rearrange("p (j k c) -> p j k c", j=2, c=C)
        tb = SCR[:, 5888:6912].rearrange("p (j k c) -> p j k c", j=2, c=C)
        lift = SCR[:, 6912:7168].rearrange("p (k c) -> p k c", c=C)
        mbt = [SCR[:, 5120 + 512 * u:5632 + 512 * u].rearrange("p (m n) -> p m n", n=P) for u in range(2)]
        AF = SCR[:, 0:4096].rearrange("p (k s) -> p k s", s=32)
        syn = SCR[:, 6144:6656].rearrange("p (k q o) -> p k q o", q=2, o=C)
        syn_hi, syn_lo = ([SCR[:, at + 512 * u:at + 256 + 512 * u].bitcast(F16).rearrange(
            "p (k q o) -> p k q o", q=2, o=C) for u in range(2)] for at in (4096, 4352))
        x1b = [SCR[:, 5120 + 512 * u:5632 + 512 * u] for u in range(2)]
        x1t_hi, x1t_lo = ([SCR[:, at + 512 * u:at + 256 + 512 * u].bitcast(F16).rearrange(
            "p (n m) -> p n m", m=P) for u in range(2)] for at in (6656, 6912))
        aft = [SCR[:, 4096 + 512 * u:4608 + 512 * u].rearrange("p (n m) -> p n m", m=P) for u in range(2)]
        DV = SCR[:, 5120:5632].rearrange("p (t n) -> p t n", t=2)
        om = SCR[:, 5632:6144].rearrange("p (y n t) -> p y n t", n=16, t=2)
        om2 = SCR[:, 6144:6656].rearrange("p (y n t) -> p y n t", n=16, t=2)
        both_dft = SCR[:, 6656:7680]
        om_low = SCR[:, 6656:7168].rearrange("p (y n t) -> p y n t", n=16, t=2)
        DV16 = SCR[:, 7168:7680].bitcast(F16).rearrange("p (t n) -> p t n", t=4)
        OT = SCR[0:96, 0:1024].bitcast(F16).rearrange("p (o s y) -> p o s y", s=2, y=MODES)
        WM = [R1[:, 2048 * u:2048 * (u + 1)].rearrange("p (n o) -> p n o", o=C) for u in range(2)]
        W16 = [R1[:, 4096 + 2048 * u:6144 + 2048 * u].bitcast(F16).rearrange(
            "p (n s o) -> p n s o", s=2, o=C) for u in range(2)]
        Z = [R1[0:96, 2048 * u:2048 * (u + 1)].bitcast(F16).rearrange("p (h o) -> p h o", o=C) for u in range(2)]
        R1h = R1[:, 0:8192].bitcast(F16)
        SCRh = SCR[:, :].bitcast(F16)
        XH = [R1h[:, 1024 * u:1024 * (u + 1)] for u in range(2)]
        XL = [R1h[:, 2048 + 1024 * u:3072 + 1024 * u] for u in range(2)]
        XN = [R1[:, 2048 + 1024 * u:3072 + 1024 * u] for u in range(2)]
        HQ = [[R1h[:, 8192 + 2048 * u + 1024 * q:9216 + 2048 * u + 1024 * q] for q in range(2)] for u in range(2)]
        LQ = [[SCRh[:, 2048 * u + 1024 * q:2048 * u + 1024 * q + 1024] for q in range(2)] for u in range(2)]
        OH = [SCRh[:, 4096 + 512 * i:4608 + 512 * i] for i in range(4)]
        OTs = [SCRh[:, 6144 + 2048 * i:8192 + 2048 * i].rearrange("p (k n) -> p k n", k=4) for i in range(2)]
        NH = [R1h[:, 2340 * u:2340 * (u + 1)].rearrange("p (k j n) -> p k j n", j=2, n=130) for u in range(2)]
        NL = [R1h[:, 4680 + 2340 * u:7020 + 2340 * u].rearrange("p (k j n) -> p k j n", j=2, n=130) for u in range(2)]
        XM = R1[:, 4680:6728]
        res = [SCR[:, 512 * i:512 * (i + 1)] for i in range(4)]
        ost = [SCR[:, 2048 + 2048 * u:4096 + 2048 * u].rearrange("p (r j o) -> p r j o", j=2, o=C) for u in range(2)]
        edge = SCR[:, 6144:6400]
        edge_t = SCR[:, 6400:6528]

        s_const = sem("constants_loaded")
        s_prep = sem("weights_prepared")
        s_bar = sem("phase_barrier")
        s_past = sem("waits_taken")
        s_st = sem("statistics_step")
        s_tile = [sem(f"tile_loaded{u}") for u in range(2)]
        s_tp = sem("tile_transposed")
        s_xin = sem("x_written")
        s_padd = sem("row_sums_added")
        s_dl = sem("row_filter_link")
        s_s1 = sem("low_rows_ready")
        s_wa = sem("columns_analysed")
        s_wb = sem("coefficients_stored")
        s_lf = sem("lifting_link")
        s_mt = sem("mix_transposed")
        s_mb = sem("mix_normalised")
        s_mm = sem("mix_multiplied")
        s_mo = sem("mix_stored")
        s_fold = sem("dense_bias_product_ready")
        s_folded = sem("dense_folded")
        s_si = sem("synthesis_rows_interpolated")
        s_sh = sem("synthesis_rows_high_ready")
        s_sy = sem("synthesis_rows_ready")
        s_l0 = sem("layer0_product_ready")
        s_g = sem("gelu_ready")
        s_x1 = sem("x1_ready")
        s_xst = sem("x1_stored")
        s_x1n = sem("x1_measured")
        s_xt = sem("x1_transposed")
        s_xth = sem("x1_transpose_high_copied")
        s_xtl = sem("x1_transpose_low_copied")
        s_fa = sem("row_dft_ready")
        s_fah = sem("row_dft_half_stored")
        s_fac = sem("row_dft_stored")
        s_at = sem("row_dft_transposed")
        s_atc = sem("row_dft_transpose_copied")
        s_fg = sem("image_dft_ready")
        s_bd = sem("image_dft_stored")
        s_ff = sem("image_dft_folded")
        s_wh = sem("mode_weights_high_ready")
        s_wl = sem("mode_weights_low_ready")
        s_ol = sem("modes_mixed_low_copied")
        s_dv = sem("mode_vectors_ready")
        s_wm = [sem(f"mode_weights_loaded{u}") for u in range(2)]
        s_om = sem("modes_mixed")
        s_oms = sem("mixed_modes_copied")
        s_ot = sem("mixed_modes_transposed")
        s_oth = sem("transposed_modes_high_ready")
        s_zp = sem("column_synthesis_ready")
        s_zc = sem("column_synthesis_high_stored")
        s_zl = sem("column_synthesis_low_stored")
        s_yp = sem("layer1_output_ready")
        s_x2 = sem("x2_written")
        s_xh = sem("x_high_ready")
        s_xn = sem("x_normalised")
        s_xl = sem("x_low_ready")
        s_hl = [sem(f"halves_placed{u}") for u in range(2)]
        s_sc = sem("scores_ready")
        s_mx = sem("maximum_ready")
        s_mxs = sem("maximum_scaled")
        s_oh = sem("one_hots_ready")
        s_oht = sem("one_hots_transposed")
        s_ocd = sem("even_one_hots_copied")
        s_oca = sem("odd_one_hots_copied")
        s_cd = sem("codes_looked_up")
        s_x3 = sem("x3_written")
        s_nh = sem("conv_high_ready")
        s_nn = sem("conv_normalised")
        s_nl = sem("conv_low_ready")
        s_cp = sem("conv_edges_ready")
        s_pad = sem("conv_padding_cleared")
        s_cv = sem("conv_ready")
        s_rs = sem("conv_residual_added")
        s_ct = sem("output_transposed")
        s_oc = sem("output_copied")
        s_out = [sem(f"output_stored{u}") for u in range(2)]
        s_e = sem("row0_step")
        s_eout = sem("row0_stored")

        block = ctx.enter_context(nc.Block())

        x_cols = x.rearrange("b h (p j) c -> b j p h c", j=2)
        o_rows = out.rearrange("b h (p j) c -> b p h (j c)", j=2)

        ct32 = SCR[:, 0:NCODE]
        c32 = SCR[:, 512:768].rearrange("p (k c) -> p k c", c=C)
        cv32 = SCR[:, 1024:1792].rearrange("p (k n) -> p k n", n=P)
        sq = SCR[0:C, 2048:2560]
        hi16 = SCR[:, 2560:2816].bitcast(F16)
        neghalf = SCR[0:C, 3072:3073]
        bias_row = SCR[0:1, 3200:3712]
        row16 = SCR[0:1, 3712:4224].bitcast(F16)
        CONSTS = [(id32[:], ident), (grp[:], group), (fld[:], fold), (wan[:], w_analysis), (wsy[:], w_synthesis),
                  (dn[:], dense), (mixw[:, 0, :], mix_low), (mixw[:, 1, :], mix_high), (dfw[:], dft_w),
                  (dfh[:], dft_h), (idh[:], idft_h), (idw[:], idft_w), (dbias[:], dense_bias),
                  (cbias[:], conv_bias), (ct32, codes_t), (c32, codes), (cv32, conv)]
        CHUNKS = 16
        NST = 12
        LIFTS = 140

        def st_base(b, layer):
            return (b * 4 + layer) * NST

        def past(eng):
            eng.sem_inc(s_past, 1)

        def barrier(eng, b, n):
            past(eng)
            eng.drain().then_inc(s_bar, 1)
            eng.wait_ge(s_bar, (b * PHASES + n + 1) * ENGINES)
            past(eng)

        @block.sync
        def _(sp):
            for u in range(2):
                sp.sem_inc(s_out[u], 32)
            for dst, src in CONSTS:
                sp.dma_start(dst, src).then_inc(s_const, 16)
            sp.wait_ge(s_prep, 13)
            sp.dma_start(code_top[C:C + 1, :], row16[:, 0:NCODE]).then_inc(s_const, 16)
            sp.dma_start(code_top[C + 1:C + 2, :], row16[:, NCODE:2 * NCODE]).then_inc(s_const, 16)
            sp.wait_ge(s_const, 16 * (len(CONSTS) + 2))
            with sp.Fori(0, B) as b:
                def around(ci):
                    if isinstance(ci, int):
                        return 16 * ci, (16 * ci + 254) % 256, (16 * ci + 16) % 256
                    return sp.snap(16 * ci), sp.snap((16 * ci + 254) % 256), sp.snap((16 * ci + 16) % 256)

                def load(rows, u):
                    main, above, below = rows
                    for j in range(2):
                        src = x_cols[b, j]
                        sp.dma_start(T[u][:, j, 2:18, :], src[:, ds(main, 16), :]).then_inc(s_tile[u], 16)
                        sp.dma_start(T[u][:, j, 0:2, :], src[:, ds(above, 2), :]).then_inc(s_tile[u], 16)
                        sp.dma_start(T[u][:, j, 18:19, :], src[:, ds(below, 1), :]).then_inc(s_tile[u], 16)

                load(around(0), 0)
                load(around(1), 1)
                with sp.Fori(0, 7) as c2:
                    for u in range(2):
                        n = b * CHUNKS + 2 * c2 + u
                        rows = around(2 * c2 + u + 2)
                        sp.wait_ge(s_tp, n * 4 + 4)
                        sp.wait_ge(s_s1, n * 2 + 2)
                        load(rows, u)
                barrier(sp, b, 0)
                barrier(sp, b, 1)
                barrier(sp, b, 2)
                sp.dma_start(WM[0], modes[:, 0:32, :]).then_inc(s_wm[0], 16)
                sp.dma_start(WM[1], modes[:, 32:64, :]).then_inc(s_wm[1], 16)
                with sp.Fori(0, 3) as i:
                    for u in range(2):
                        sp.wait_ge(s_wl, b * 8 + 2 * i + u + 1)
                        sp.dma_start(WM[u], modes[:, ds((2 * i + u + 2) * 32, 32), :]).then_inc(s_wm[u], 16)
                barrier(sp, b, 3)
                barrier(sp, b, 4)

                def place(n, u, first):
                    if not first:
                        sp.wait_ge(s_sc, (n - 1) * 16)
                        past(sp)
                    sp.wait_ge(s_xh, n + 1)
                    for q in range(2):
                        rows = slice(C * q, C * q + C)
                        sp.dma_start(HQ[u][q][0:C, :], XH[u][rows, :]).then_inc(s_hl[u], 16)
                        sp.dma_start(LQ[u][q][C:P, :], XH[u][rows, :]).then_inc(s_hl[u], 16)
                    sp.wait_ge(s_xl, n + 1)
                    for q in range(2):
                        rows = slice(C * q, C * q + C)
                        sp.dma_start(LQ[u][q][0:C, :], XL[u][rows, :]).then_inc(s_hl[u], 16)

                sp.wait_ge(s_pad, 2 * b + 1)
                place(b * 32, 0, True)
                place(b * 32 + 1, 1, True)
                with sp.Fori(0, 15) as i:
                    for u in range(2):
                        n = b * 32 + 2 * i + u
                        place(n + 2, u, False)
                barrier(sp, b, 5)

                def store(ci, u, halves):
                    sp.wait_ge(s_oc, 2 + (b * CHUNKS + ci + 1) * 4)
                    for r0, nr in halves:
                        sp.dma_start(o_rows[b][:, ds(16 * ci + 1 + r0, nr), :],
                                     ost[u][:, r0:r0 + nr, :, :].rearrange("p r j o -> p r (j o)")
                                     ).then_inc(s_out[u], 16)

                with sp.Fori(0, 7) as i:
                    for u in range(2):
                        store(2 * i + u, u, ((0, 8), (8, 8)))
                store(14, 0, ((0, 8), (8, 8)))
                store(15, 1, ((0, 8), (8, 7)))
                sp.wait_ge(s_e, b * 5 + 5)
                sp.dma_start(o_rows[b][:, 0:1, :], edge_t[:, :].rearrange("p (r n) -> p r n", r=1)).then_inc(s_eout, 16)
                sp.wait_ge(s_eout, 16 * (b + 1))
                for u in range(2):
                    sp.wait_ge(s_out[u], 32 + 256 * (b + 1))
                barrier(sp, b, 6)

        @block.tensor
        def _(pe):
            for free, count in ((s_wa, 2), (s_fg, 2), (s_xt, 2), (s_fa, 2), (s_yp, 1), (s_oht, 2), (s_cd, 2), (s_ct, 4), (s_cv, 4)):
                pe.sem_inc(free, count)
            pe.wait_ge(s_prep, 10)
            pe.matmul(bank(0)[0:1, :], neghalf, sq, start=True, stop=True).then_inc(s_prep, 1)
            pe.wait_ge(s_prep, 13)
            pe.wait_ge(s_const, 16 * (len(CONSTS) + 2))
            with pe.Fori(0, B) as b:
                def stats(layer):
                    base = st_base(b, layer)
                    pe.wait_ge(s_st, base + 1)
                    pe.matmul(bank(7)[:, 0:1], grp[:], agg[:, 0:1], start=True, stop=True).then_inc(s_st, 1)
                    pe.wait_ge(s_st, base + 4)
                    pe.matmul(bank(7)[:, 1:2], grp[:], e2, start=True, stop=True).then_inc(s_st, 1)

                with pe.Fori(0, 8) as c2:
                    for u in range(2):
                        c = b * CHUNKS + 2 * c2 + u
                        pe.wait_ge(s_tile[u], 96 * (b * 8 + c2 + 1))
                        for m in range(4):
                            pe.wait_ge(s_xin, c * 4 + m + 1)
                            for kk in range(2):
                                for j in range(2):
                                    r = 2 + 2 * (2 * m + kk)
                                    t = pe.transpose(bank(m % 2)[:, (2 * kk + j) * P:(2 * kk + j + 1) * P],
                                                     T[u][:, j, r:r + 2, :], id32[:])
                            t.then_inc(s_tp, 1)
                        pe.wait_ge(s_wb, c + 1)
                        for j in range(2):
                            pe.wait_ge(s_s1, c * 2 + j + 1)
                            pe.matmul(bank(2 + u), wan[:, j, :], tb[:, j, :, :], start=j == 0,
                                      stop=j == 1).then_inc(s_wa, 1)
                barrier(pe, b, 0)
                def turn_bands(g):
                    for m in range(4):
                        at = g * 512 + m * P
                        t = pe.transpose(bank(g % 2)[:, m * P:(m + 1) * P], R1[:, at:at + P], id32[:])
                    t.then_inc(s_mt, 1)

                turn_bands(0)
                turn_bands(1)
                stats(0)
                for g in range(16):
                    pe.wait_ge(s_mb, b * 16 + g + 1)
                    pe.wait_ge(s_mo, b * 16 + g + 1)
                    past(pe)
                    for half in range(2):
                        for m in range(4):
                            t = pe.matmul(bank(2 + g % 2)[half * C:(half + 1) * C, m * P:(m + 1) * P],
                                          mbt[g % 2][:, m, half * C:(half + 1) * C], mixw[:, half, :],
                                          start=True, stop=True)
                    t.then_inc(s_mm, 1)
                    if g < 14:
                        turn_bands(g + 2)
                pe.matmul(bank(7)[:, 2:3], dn[:], nb, start=True, stop=True).then_inc(s_fold, 1)
                barrier(pe, b, 1)

                def product(n, m, at):
                    if m % 2 == 0:
                        pe.wait_ge(s_sy, at[1] + 1)
                    pe.wait_ge(s_g, n + 1)
                    pe.matmul(bank(m), dnf[:], X[:, ds(at[0], 512)], start=True, stop=False, skip_group_check=True)
                    for i in range(2):
                        dst = bank(m)[:, i * 256:(i + 1) * 256]
                        pe.matmul(dst, syn_hi[m // 2][:, 2 * (m % 2) + i], wsy[:], start=False, stop=False,
                                  skip_group_check=True)
                        t = pe.matmul(dst, syn_lo[m // 2][:, 2 * (m % 2) + i], wsy[:], start=False, stop=True,
                                      skip_group_check=True)
                    t.then_inc(s_l0, 1)

                def row_dft(c, m, u):
                    n = (b * CHUNKS + c) * 4 + m
                    pe.wait_ge(s_xtl, n + 3)
                    if m == 0:
                        pe.wait_ge(s_fac, b * CHUNKS + c + 1)
                    for kk in range(2):
                        at = (2 * m + kk) * 64
                        for j in range(2):
                            pe.matmul(bank(6 + u)[:, at:at + 64], x1t_hi[m % 2][:, 2 * kk + j, :], dfw[:, j, :],
                                      start=j == 0, stop=False, skip_group_check=True)
                            t = pe.matmul(bank(6 + u)[:, at:at + 32], x1t_lo[m % 2][:, 2 * kk + j, :],
                                          dfw[:, j, 0:32], start=False, stop=j == 1, skip_group_check=True)
                    t.then_inc(s_fa, 1)

                def layer0_steps(c, u, first, last):
                    for m in range(4):
                        n = (b * CHUNKS + c) * 4 + m
                        pe.wait_ge(s_x1, n + 1)
                        pe.wait_ge(s_xtl, n + 1)
                        for i in range(4):
                            t = pe.transpose(bank(4 + m % 2)[:, i * P:(i + 1) * P],
                                             x1b[m % 2][:, i * P:(i + 1) * P], id32[:])
                        t.then_inc(s_xt, 1)
                        if not (last and m >= 2):
                            product(n + 2, (m + 2) % 4, (c * 2048 + (m + 2) * 512, (b * CHUNKS + c) * 2 + (m + 2) // 2))
                        if m:
                            row_dft(c, m - 1, u)
                        elif not first:
                            row_dft(c - 1, 3, 1 - u)

                pe.wait_ge(s_folded, 2 * b + 2)
                for m in range(2):
                    product(b * 64 + m, m, (m * 512, b * 32))
                layer0_steps(0, 0, True, False)
                layer0_steps(1, 1, False, False)
                with pe.Fori(1, CHUNKS // 2 - 1) as c2:
                    for u in range(2):
                        layer0_steps(2 * c2 + u, u, False, False)
                layer0_steps(CHUNKS - 2, 0, False, False)
                layer0_steps(CHUNKS - 1, 1, False, True)
                row_dft(CHUNKS - 1, 3, 1)
                barrier(pe, b, 2)

                stats(1)
                for g in range(9):
                    if g < 8:
                        pe.wait_ge(s_atc, b * 8 + g + 1)
                        for i in range(4):
                            t = pe.transpose(bank(g % 2)[:, i * P:(i + 1) * P], AF[:, :, 4 * g + i], id32[:])
                        t.then_inc(s_at, 1)
                    if g == 0:
                        continue
                    pe.wait_ge(s_atc, b * 8 + g + 2)
                    for yy in range(2):
                        y = 2 * (g - 1) + yy
                        for part in range(2):
                            t = pe.matmul(bank(4 + y // 8)[:, (y % 8) * 64:(y % 8 + 1) * 64],
                                          aft[(g - 1) % 2][:, 2 * yy + part, :], dfh[:, ds(part, 2, 2), :],
                                          start=part == 0, stop=part == 1)
                    t.then_inc(s_fg, 1)
                pe.wait_ge(s_bd, b * 2 + 2)
                past(pe)
                sides = both_dft.rearrange("p (y q n) -> p y q n", q=2, n=32)
                for q in range(2):
                    t = pe.matmul(bank(2), fld[:, 2 * q:2 * q + 2, :], sides[:, :, q, :], start=q == 0, stop=q == 1)
                t.then_inc(s_ff, 1)
                pe.wait_ge(s_dv, b * 8 + 8)
                past(pe)
                for i in range(4):
                    for u in range(2):
                        pe.wait_ge(s_wl, b * 8 + 2 * i + u + 1)
                        for md in range(32):
                            k = (2 * i + u) * 32 + md
                            t = pe.matmul(bank(2 + k // 128)[:, 4 * (k % 128):4 * (k % 128) + 4], W16[u][:, md],
                                          DV16[:, :, k:k + 1], start=True, stop=True)
                        t.then_inc(s_om, 1)
                pe.wait_ge(s_oms, b * 4 + 4)
                past(pe)
                for s, src in enumerate((om, om2)):
                    for y in range(MODES):
                        t = pe.matmul(bank(4 + 2 * s + y // 8)[0:32, (y % 8) * C:(y % 8 + 1) * C],
                                      src[:, y, :, :], fld[:, 4, :], start=True, stop=True)
                t.then_inc(s_ot, 1)
                barrier(pe, b, 3)

                def rows_synthesis(z, g):
                    pe.wait_ge(s_zl, b * 32 + z * 8 + g + 1)
                    past(pe)
                    for o in range(8):
                        t = pe.matmul(bank(g % 2)[0:32, o * 64:(o + 1) * 64], OT[:, 8 * g + o],
                                      idh[:, 64 * z:64 * z + 64], start=True, stop=True)
                    t.then_inc(s_zp, 1)

                for g in range(8):
                    rows_synthesis(0, g)
                for z in range(4):
                    pe.wait_ge(s_zl, b * 32 + z * 8 + 10)
                    for m in range(16):
                        pe.wait_ge(s_x2, (b * 4 + z) * 16 + m + 1)
                        for i in range(2):
                            r = 2 * (2 * m + i)
                            t = pe.matmul(bank(2 + m % 4)[:, i * 256:(i + 1) * 256], Z[z % 2][:, r:r + 2, :],
                                          idw[:], start=True, stop=True)
                        t.then_inc(s_yp, 1)
                        if z < 3 and m % 2:
                            rows_synthesis(z + 1, m // 2)
                barrier(pe, b, 4)

                stats(2)

                def scores(n, u, h, fresh):
                    px, q, hh = h // 4, h // 2 % 2, h % 2
                    for t2 in range(2):
                        pix = slice(px * 512 + (2 * hh + t2) * P, px * 512 + (2 * hh + t2 + 1) * P)
                        dst = bank(2 * hh + t2)
                        if not fresh:
                            pe.wait_ge(s_oh, 2 * n - 4 + t2 + 1)
                        pe.matmul(dst, LQ[u][q][:, pix], code_low[:], start=True, stop=False)
                        pe.matmul(dst, HQ[u][q][0:C + 2, pix], code_top[0:C + 2, :], start=False,
                                  stop=True).then_inc(s_sc, 1)

                def layer2_chunks(i, first, last):
                    k0, unit0, quarter0 = (b * 16 + i) * 16, (b * 16 + i) * 8, (b * 16 + i) * 4

                    def look_up(k):
                        q, px = k // 2 % 2, k // 4 % 2
                        pe.wait_ge(s_oca, unit0 + k // 2 + 2)
                        pe.wait_ge(s_ocd, unit0 + k // 2 + 2)
                        if q == 0:
                            pe.wait_ge(s_x3, quarter0 + k // 4 + 1)
                        dst = bank(6 + px)[q * C:(q + 1) * C, :]
                        for blk in range(4):
                            pe.matmul(dst, code_hi[:, blk, :], OTs[q][:, blk, :], start=blk == 0, stop=False)
                            t = pe.matmul(dst, code_lo[:, blk, :], OTs[q][:, blk, :], start=False, stop=blk == 3)
                        t.then_inc(s_cd, 1)

                    for k in range(16):
                        n, h, hh = k0 + k, k % 8, k % 2
                        if not (last and k >= 14):
                            if h == 6:
                                pe.wait_ge(s_hl[1 - k // 8], 96 * (b * 16 + i + 1 + k // 8))
                            scores(n + 2, (k + 2) // 8 % 2, (h + 2) % 8, False)
                        else:
                            pe.wait_ge(s_oh, 2 * n + 2)
                        pe.wait_ge(s_oca if hh else s_ocd, unit0 + k // 2 + 1)
                        dst = bank(4 + hh).bitcast(F16).rearrange("p (k n) -> p k n", k=4)
                        for t2 in range(2):
                            for blk in range(4):
                                t = pe.transpose(dst[:, blk, t2 * P:(t2 + 1) * P],
                                                 OH[2 * hh + t2][:, blk * P:(blk + 1) * P], id16[:])
                        t.then_inc(s_oht, 1)
                        if hh and not (first and k == 1):
                            look_up(k - 3)
                    if last:
                        look_up(14)

                pe.wait_ge(s_hl[0], 96 * (b * 16 + 1))
                scores(b * 256, 0, 0, True)
                scores(b * 256 + 1, 0, 1, True)
                layer2_chunks(0, True, False)
                with pe.Fori(1, 15) as i:
                    layer2_chunks(i, False, False)
                layer2_chunks(15, False, True)
                barrier(pe, b, 5)

                stats(3)

                def conv_group(dst, u, kk0, count, j):
                    taps = [(tap, pr, w3, src) for tap in range(3) for pr in range(2)
                            for w3, src in ((conv_hi, NH), (conv_lo, NH), (conv_hi, NL))]
                    for i, (tap, pr, w3, src) in enumerate(taps):
                        col = j - (tap + 1)
                        jj = col % 2
                        p0 = 2 + (col - jj) // 2
                        t = pe.matmul(dst, w3[:, pr * 3 + tap, :], src[u][:, kk0 + pr:kk0 + pr + count, jj, p0:p0 + P],
                                      start=i == 0, stop=i == len(taps) - 1)
                    return t

                def turn(n, m):
                    pe.wait_ge(s_rs, n + 5)
                    pe.wait_ge(s_oc, n + 1)
                    for i in range(4):
                        t = pe.transpose(bank(4 + m % 2)[:, i * P:(i + 1) * P], res[m][:, i * P:(i + 1) * P], id32[:])
                    t.then_inc(s_ct, 1)

                with pe.Fori(0, 8) as i:
                    for u in range(2):
                        c = b * CHUNKS + 2 * i + u
                        pe.wait_ge(s_cp, b * 17 + 2 * i + u + 2)
                        for m in range(4):
                            pe.wait_ge(s_rs, c * 4 + m + 1)
                            conv_group(bank(m), u, 4 * (m // 2), 4, m % 2).then_inc(s_cv, 1)
                            if u or m:
                                turn(c * 4 + m - 1, (m - 1) % 4)
                    turn(c * 4 + 3, 3)
                pe.wait_ge(s_cp, b * 17 + 18)
                conv_group(bank(6)[:, 0:P], 0, 0, 1, 0)
                conv_group(bank(6)[:, P:2 * P], 0, 0, 1, 1).then_inc(s_e, 1)
                pe.wait_ge(s_e, b * 5 + 3)
                for j in range(2):
                    t = pe.transpose(bank(7)[:, j * P:(j + 1) * P], edge[:, j * P:(j + 1) * P], id32[:])
                t.then_inc(s_e, 1)
                barrier(pe, b, 6)

        @block.scalar
        def _(act):
            for free, count in ((s_xin, 2), (s_wb, 2), (s_mo, 2), (s_g, 4), (s_xst, 2), (s_atc, 2),
                                (s_oc, 2), (s_oca, 1)):
                act.sem_inc(free, count)
            act.wait_ge(s_const, 16 * len(CONSTS))
            with act.Fori(0, B) as b:
                def stats(layer):
                    base = st_base(b, layer)
                    act.wait_ge(s_st, base + 6)
                    act.activation(sd, var, ACT.Sqrt).then_inc(s_st, 1)

                with act.Fori(0, 8) as c2:
                    for u in range(2):
                        c = b * CHUNKS + 2 * c2 + u
                        for m in range(4):
                            act.wait_ge(s_tp, c * 4 + m + 1)
                            act.activation(X[:, ds((2 * c2 + u) * 2048 + m * 512, 512)], bank(m % 2),
                                           ACT.Copy).then_inc(s_xin, 1)
                        act.wait_ge(s_wa, 2 + c * 2 + 2)
                        act.activation(R1[:, ds((2 * c2 + u) * 512, 512)], bank(2 + u), ACT.Copy).then_inc(s_wb, 1)
                barrier(act, b, 0)
                stats(0)
                act.wait_ge(s_st, st_base(b, 0) + NST)
                act.wait_ge(s_folded, 2 * b + 1)

                def normalise_bands(n, u):
                    act.wait_ge(s_mt, n + 1)
                    src = bank(u).rearrange("p (m n) -> p m n", n=P)
                    act.activation(mbt[u][:, :, 0:C], src[:, :, 0:C], ACT.Identity, bias=nbl[:], scale=rs)
                    act.activation(mbt[u][:, :, C:P], src[:, :, C:P], ACT.Copy, scale=rs).then_inc(s_mb, 1)

                def store_bands(n, at, u):
                    act.wait_ge(s_mm, n + 1)
                    act.activation(R1[:, ds(at, 512)], bank(2 + u), ACT.Copy).then_inc(s_mo, 1)

                normalise_bands(b * 16, 0)
                with act.Fori(0, 7) as g:
                    for u in range(2):
                        n = b * 16 + 2 * g + u
                        normalise_bands(n + 1, 1 - u)
                        store_bands(n, (2 * g + u) * 512, u)
                normalise_bands(b * 16 + 15, 1)
                store_bands(b * 16 + 14, 14 * 512, 0)
                store_bands(b * 16 + 15, 15 * 512, 1)
                barrier(act, b, 1)

                def gelu(n, m):
                    act.wait_ge(s_l0, n + 1)
                    act.wait_ge(s_xt, n + 1)
                    act.wait_ge(s_x1n, n + 1)
                    act.wait_ge(s_xst, n + 1)
                    act.activation(x1b[m % 2], bank(m), ACT.Gelu_apprx_tanh, bias=fb).then_inc(s_g, 1)

                def rows_high(n, u):
                    act.wait_ge(s_si, n + 1)
                    act.activation(syn_hi[u], syn, ACT.Copy).then_inc(s_sh, 1)

                def copies(c, last):
                    for m in range(4):
                        n = (b * CHUNKS + c) * 4 + m
                        if not (last and m == 3):
                            gelu(n + 1, (m + 1) % 4)
                        if not last and m % 2:
                            rows_high((b * CHUNKS + c + 1) * 2 + m // 2, m // 2)
                        act.wait_ge(s_x1, n + 1)
                        past(act)
                        act.activation(X[:, ds(c * 2048 + m * 512, 512)], x1b[m % 2], ACT.Copy).then_inc(s_xst, 1)
                        act.wait_ge(s_xt, n + 3)
                        act.wait_ge(s_fa, n + 1)
                        act.activation(x1t_hi[m % 2], bank(4 + m % 2).rearrange("p (n m) -> p n m", m=P),
                                       ACT.Copy).then_inc(s_xth, 1)

                act.wait_ge(s_folded, 2 * b + 2)
                rows_high(b * 32, 0)
                rows_high(b * 32 + 1, 1)
                gelu(b * 64, 0)
                with act.Fori(0, CHUNKS // 2 - 1) as c2:
                    for u in range(2):
                        copies(2 * c2 + u, False)
                copies(CHUNKS - 2, False)
                copies(CHUNKS - 1, True)
                barrier(act, b, 2)

                stats(1)
                def weights_high(j):
                    i, u = j // 2, j % 2
                    act.wait_ge(s_wm[u], 16 * (b * 4 + i + 1))
                    if j >= 2:
                        act.wait_ge(s_om, b * 8 + j - 1)
                    act.activation(W16[u][:, :, 0, :], WM[u], ACT.Copy, scale=WSCALE).then_inc(s_wh, 1)

                def mixed_low(half):
                    act.activation(om_low[:, 8 * half:8 * half + 8], mixed(half)[:, :, :, 2:4], ACT.Copy,
                                   scale=1.0 / WSCALE).then_inc(s_ol, 1)

                for g in range(8):
                    act.wait_ge(s_at, b * 8 + g + 1)
                    act.wait_ge(s_fg, b * 8 + g + 1)
                    act.activation(aft[g % 2], bank(g % 2).rearrange("p (n m) -> p n m", m=P),
                                   ACT.Copy).then_inc(s_atc, 1)
                    if g in (3, 5):
                        weights_high((g - 3) // 2)
                for j in range(2, 6):
                    weights_high(j)
                act.wait_ge(s_om, b * 8 + 4)
                mixed_low(0)
                weights_high(6)
                weights_high(7)
                act.wait_ge(s_om, b * 8 + 8)
                mixed_low(1)
                act.wait_ge(s_oms, b * 4 + 2)
                act.activation(om2[:, :, :, 0], om[:, :, :, 1], ACT.Copy).then_inc(s_oms, 1)
                act.activation(om2[:, :, :, 1], om[:, :, :, 0], ACT.Copy, scale=-1.0).then_inc(s_oms, 1)
                act.wait_ge(s_ot, b + 1)
                for s in range(2):
                    for yh in range(2):
                        act.activation(modes_out(0, s, yh), modes_in(s, yh), ACT.Copy)
                        act.activation(modes_out(2, s, yh), modes_in(s, yh), ACT.Copy).then_inc(s_oth, 1)
                barrier(act, b, 3)
                for z in range(4):
                    for g in range(8):
                        act.wait_ge(s_zp, b * 32 + z * 8 + g + 1)
                        if g == 0 and z >= 2:
                            act.wait_ge(s_yp, (b * 4 + z - 1) * 16 + 1)
                        act.activation(block_out(z, 0, g), block_in(g), ACT.Copy)
                        act.activation(block_out(z, 2, g), block_in(g), ACT.Copy).then_inc(s_zc, 1)
                barrier(act, b, 4)
                stats(2)
                act.wait_ge(s_st, st_base(b, 2) + NST)

                def high(at, u):
                    act.activation(XH[u], X[:, ds(at, 1024)], ACT.Identity, bias=nb, scale=rs).then_inc(s_xh, 1)

                def one_hots(i, first, last):
                    k0, unit0 = (b * 16 + i) * 16, (b * 16 + i) * 8

                    def copy_odd(k):
                        q = k // 2 % 2
                        act.wait_ge(s_oht, 2 + k0 + k + 1)
                        act.wait_ge(s_cd, unit0 + k // 2 + 1)
                        act.activation(OTs[q][:, :, 256:512], bank(5).bitcast(F16).rearrange(
                            "p (k n) -> p k n", k=4), ACT.Copy).then_inc(s_oca, 1)

                    for k in range(16):
                        n, hh = k0 + k, k % 2
                        act.wait_ge(s_oht, n + 1)
                        for t2 in range(2):
                            act.wait_ge(s_mxs, 2 * n + t2 + 1)
                            act.activation(OH[2 * hh + t2], bank(2 * hh + t2), ACT.Exp,
                                           bias=negsharp[:, hh, t2:t2 + 1], scale=SHARP).then_inc(s_oh, 1)
                        if k % 2 == 0 and not (first and k == 0):
                            copy_odd(k - 1)
                        if k % 8 == 3 and not last:
                            u = k // 8
                            act.wait_ge(s_hl[u], 96 * (b * 16 + i + 1))
                            act.wait_ge(s_xl, b * 32 + 2 * i + u + 1)
                            high((2 * i + u + 2) * 1024, u)
                    if last:
                        copy_odd(15)

                high(0, 0)
                high(1024, 1)
                one_hots(0, True, False)
                with act.Fori(1, 15) as i:
                    one_hots(i, False, False)
                one_hots(15, False, True)
                barrier(act, b, 5)
                stats(3)
                act.wait_ge(s_st, st_base(b, 3) + NST)

                def conv_high(at, u):
                    act.activation(NH[u][:, 1:9, :, 2:130], X[:, ds(at, 2048)].rearrange(
                        "p (k j n) -> p k j n", j=2, n=P), ACT.Identity, bias=nb, scale=rs).then_inc(s_nh, 1)

                def out_copies(i, last):
                    for u in range(2):
                        c = b * CHUNKS + 2 * i + u
                        for m in range(4):
                            n = c * 4 + m
                            if m == 3 and not last:
                                act.wait_ge(s_cv, c * 4 + 8)
                                act.wait_ge(s_cp, b * 17 + 2 * i + u + 3)
                                conv_high((2 * i + u + 2) * 2048, u)
                            if m == 0:
                                act.wait_ge(s_out[u], 32 * (b * 8 + i + 1))
                            act.wait_ge(s_ct, n + 5)
                            src = bank(4 + m % 2).rearrange("p (k r o) -> p k r o", r=2, o=C)
                            dst = ost[u].rearrange("p (k r) j o -> p k r j o", r=2)[:, 4 * (m // 2):4 * (m // 2) + 4]
                            act.activation(dst[:, :, 1, m % 2, :], src[:, :, 0, :], ACT.Copy)
                            act.activation(dst[:, :, 0, m % 2, :], src[:, :, 1, :], ACT.Copy).then_inc(s_oc, 1)

                act.wait_ge(s_pad, 2 * b + 2)
                conv_high(0, 0)
                act.wait_ge(s_cp, b * 17 + 2)
                conv_high(2048, 1)
                with act.Fori(0, 7) as i:
                    out_copies(i, False)
                out_copies(7, True)
                act.wait_ge(s_e, b * 5 + 4)
                act.activation(edge_t.rearrange("p (j o) -> p j o", o=C),
                               bank(7)[:, 0:2 * P].rearrange("p (j r o) -> p j r o", r=2, o=C)[:, :, 0, :],
                               ACT.Copy).then_inc(s_e, 1)
                barrier(act, b, 6)

        @block.vector
        def _(dve):
            for free, count in ((s_x1n, 2), (s_xtl, 2), (s_fac, 2), (s_zl, 2), (s_x2, 4), (s_ocd, 1), (s_x3, 2), (s_rs, 4), (s_cp, 1)):
                dve.sem_inc(free, count)
            dve.memset(neghalf, -0.5 / CSCALE).then_inc(s_prep, 1)
            dve.wait_ge(s_const, 16 * len(CONSTS))
            dve.tensor_scalar(ct32, ct32, CSCALE, None, ALU.mult).then_inc(s_prep, 1)
            dve.tensor_scalar(c32, c32, CSCALE, None, ALU.mult).then_inc(s_prep, 1)
            dve.wait_ge(s_prep, 3)
            dve.tensor_copy(code_top[0:C, :], ct32[0:C, :])
            dve.tensor_copy(code_low[0:C, :], ct32[0:C, :]).then_inc(s_prep, 1)
            dve.tensor_copy(hi16, ct32).then_inc(s_prep, 1)
            dve.tensor_copy(code_hi[:], c32).then_inc(s_prep, 1)
            dve.tensor_copy(conv_hi[:], cv32).then_inc(s_prep, 1)
            dve.wait_ge(s_prep, 7)
            dve.tensor_tensor(code_low[C:P, :], ct32[C:P, :], hi16[C:P, :], ALU.subtract)
            dve.tensor_tensor(code_lo[:], c32, code_hi[:], ALU.subtract).then_inc(s_prep, 1)
            dve.tensor_tensor(conv_lo[:], cv32, conv_hi[:], ALU.subtract).then_inc(s_prep, 1)
            dve.tensor_tensor(sq, ct32[0:C, :], ct32[0:C, :], ALU.mult).then_inc(s_prep, 1)
            dve.wait_ge(s_prep, 11)
            dve.tensor_copy(bias_row, bank(0)[0:1, :]).then_inc(s_prep, 1)
            dve.wait_ge(s_prep, 12)
            dve.tensor_copy(row16[:, 0:NCODE], bias_row).then_inc(s_lf, 1)
            dve.tensor_copy(id16[:], id32[:])
            dve.memset(X[:, NPX:NPX + PAIR], 0.0)
            dve.memset(nbl[:], 0.0).then_inc(s_lf, 1)
            dve.wait_ge(s_lf, 2)
            dve.tensor_tensor(row16[:, NCODE:2 * NCODE], bias_row, row16[:, 0:NCODE], ALU.subtract).then_inc(s_prep, 1)

            with dve.Fori(0, B) as b:
                def stats(layer):
                    base = st_base(b, layer)
                    dve.bn_aggr(agg[:], bnst[:]).then_inc(s_st, 1)
                    dve.wait_ge(s_st, base + 2)
                    dve.tensor_tensor(dev, agg[:, 0:1], mg, ALU.subtract).then_inc(s_st, 1)
                    dve.wait_ge(s_st, base + 3)
                    dve.scalar_tensor_tensor(e2, dev, dev, agg[:, 1:2], ALU.mult, ALU.add).then_inc(s_st, 1)
                    dve.wait_ge(s_st, base + 5)
                    dve.tensor_scalar(var, bank(7)[:, 1:2], EPS, None, ALU.add).then_inc(s_st, 1)
                    dve.wait_ge(s_st, base + 7)
                    dve.reciprocal(y0, sd).then_inc(s_st, 1)
                    dve.wait_ge(s_st, base + 8)
                    dve.scalar_tensor_tensor(y2, y0, var, y0, ALU.mult, ALU.mult).then_inc(s_st, 1)
                    dve.wait_ge(s_st, base + 9)
                    dve.tensor_scalar(y3, y2, -0.5, 1.5, ALU.mult, ALU.add).then_inc(s_st, 1)
                    dve.wait_ge(s_st, base + 10)
                    dve.tensor_tensor(rs, y0, y3, ALU.mult).then_inc(s_st, 1)
                    dve.wait_ge(s_st, base + 11)
                    dve.scalar_tensor_tensor(nb, mg, -1.0, rs, ALU.mult, ALU.mult).then_inc(s_st, 1)
                    dve.wait_ge(s_st, base + 12)

                def measure(src, at):
                    return dve.bn_stats(bnst[:, at:at + 6] if isinstance(at, int) else bnst[:, ds(at, 6)], src)

                def pairs(k, count, parity):
                    both = R1[:, ds(k * 2 * C, count * 2 * C)].rearrange("p (k t c) -> p k t c", t=2, c=C)
                    return both[:, :, parity, :]

                def row(k, parity):
                    at = (2 * k + parity) * C
                    return R1[:, at:at + C]

                def lift_step(step, k, count, parity, factor):
                    dve.wait_ge(s_lf, 2 + b * LIFTS + step)
                    other = 1 - parity
                    near = k + 1 if parity else k - 1
                    dve.tensor_tensor(lift[:, 0:count, :], pairs(k, count, other), pairs(near, count, other),
                                      ALU.add).then_inc(s_lf, 1)
                    dve.wait_ge(s_lf, 2 + b * LIFTS + step + 1)
                    dst = pairs(k, count, parity)
                    dve.scalar_tensor_tensor(dst, lift[:, 0:count, :], factor, dst, ALU.mult, ALU.add).then_inc(s_lf, 1)

                def lift_row(step, k, parity, factor):
                    dve.wait_ge(s_lf, 2 + b * LIFTS + step)
                    other = 1 - parity
                    near = (k + 1 if parity else k - 1) % 64
                    dve.tensor_tensor(lift[:, 0, :], row(k, other), row(near, other), ALU.add).then_inc(s_lf, 1)
                    dve.wait_ge(s_lf, 2 + b * LIFTS + step + 1)
                    dve.scalar_tensor_tensor(row(k, parity), lift[:, 0, :], factor, row(k, parity),
                                             ALU.mult, ALU.add).then_inc(s_lf, 1)

                def load_steps(c2, first):
                    for u in range(2):
                        c = b * CHUNKS + 2 * c2 + u
                        for j in range(2):
                            n = c * 2 + j
                            dve.wait_ge(s_padd, (n + 1) * 2)
                            dve.scalar_tensor_tensor(ta[:, j], tb[:, j], -0.5, ta[:, j],
                                                     ALU.mult, ALU.add).then_inc(s_dl, 1)
                            dve.wait_ge(s_dl, n + 1)
                            dve.scalar_tensor_tensor(tb[:, j], T[u][:, j, 2:18:2, :], 3.0,
                                                     ta[:, j], ALU.mult, ALU.add).then_inc(s_s1, 1)
                        for m in range(4):
                            dve.wait_ge(s_xin, 2 + c * 4 + m + 1)
                            measure(X[:, ds((2 * c2 + u) * 2048 + m * 512, 512)], ((2 * c2 + u) * 4 + m) * 6)
                        if first and u == 0:
                            continue
                        dve.wait_ge(s_wb, 2 + c)
                        if first:
                            lift_step(0, 0, 3, 1, -0.5)
                            lift_step(2, 1, 2, 0, 0.25)
                        else:
                            lift_step((2 * c2 + u - 1) * 4, (2 * c2 + u - 1) * 4 - 1, 4, 1, -0.5)
                            lift_step((2 * c2 + u - 1) * 4 + 2, (2 * c2 + u - 1) * 4 - 1, 4, 0, 0.25)

                load_steps(0, True)
                with dve.Fori(1, 8) as c2:
                    load_steps(c2, False)
                dve.wait_ge(s_wb, 2 + b * CHUNKS + 16)
                lift_step(60, 59, 4, 1, -0.5)
                lift_step(62, 59, 4, 0, 0.25)
                lift_row(64, 63, 1, -0.5)
                lift_row(66, 63, 0, 0.25)
                lift_row(68, 0, 0, 0.25)
                barrier(dve, b, 0)
                stats(0)
                dve.tensor_copy(nbl[0:C, :], nb[0:C, :])
                dve.tensor_scalar(dnf[:], dn[:], rs, None, ALU.mult).then_inc(s_folded, 1)
                dve.wait_ge(s_mo, 2 + b * 16 + 1)
                lift_step(70, 1, 3, 0, -0.25)
                lift_step(72, 1, 2, 1, 0.5)
                with dve.Fori(1, 16) as g:
                    dve.wait_ge(s_mo, 2 + b * 16 + g + 1)
                    lift_step(70 + g * 4, g * 4, 4, 0, -0.25)
                    lift_step(72 + g * 4, g * 4 - 1, 4, 1, 0.5)
                lift_row(134, 0, 0, -0.25)
                lift_row(136, 63, 1, 0.5)
                lift_row(138, 0, 1, 0.5)
                dve.wait_ge(s_lf, 2 + b * LIFTS + 138)
                dve.tensor_copy(R1[:, P * C:P * C + C], R1[:, 0:C])
                dve.wait_ge(s_fold, b + 1)
                dve.tensor_tensor(fb, bank(7)[:, 2:3], dbias[:], ALU.add).then_inc(s_folded, 1)
                barrier(dve, b, 1)

                def store_dft(c, u, half):
                    part = bank(6 + u).rearrange("p (k s n) -> p k s n", s=2, n=32)[:, :, half, :]
                    dst = SCR[:, ds(c * 256, 256)].rearrange("p (k n) -> p k n", n=32)
                    if half == 0:
                        dve.wait_ge(s_fa, (b * CHUNKS + c) * 4 + 6)
                        dve.tensor_copy(dst, part).then_inc(s_fah, 1)
                    else:
                        dve.wait_ge(s_fah, b * CHUNKS + c + 1)
                        dve.tensor_tensor(dst, part, dst, ALU.add).then_inc(s_fac, 1)

                def transpose_low(n, m):
                    dve.wait_ge(s_xth, n + 1)
                    dve.tensor_tensor(x1t_lo[m % 2], bank(4 + m % 2).rearrange("p (n m) -> p n m", m=P),
                                      x1t_hi[m % 2], ALU.subtract).then_inc(s_xtl, 1)

                def layer0_sums(c, u, first):
                    for m in range(4):
                        n = (b * CHUNKS + c) * 4 + m
                        dve.wait_ge(s_g, 4 + n + 1)
                        dve.tensor_tensor(x1b[m % 2], x1b[m % 2], X[:, ds(c * 2048 + m * 512, 512)],
                                          ALU.add).then_inc(s_x1, 1)
                        if not (first and m == 0):
                            transpose_low(n - 1, m - 1)
                        dve.wait_ge(s_x1, n + 1)
                        measure(x1b[m % 2], (c * 4 + m) * 6).then_inc(s_x1n, 1)
                        if m in (1, 2) and not first:
                            store_dft(c - 1, 1 - u, m - 1)

                layer0_sums(0, 0, True)
                layer0_sums(1, 1, False)
                with dve.Fori(1, CHUNKS // 2) as c2:
                    for u in range(2):
                        layer0_sums(2 * c2 + u, u, False)
                transpose_low(b * 64 + 63, 3)
                store_dft(CHUNKS - 1, 1, 0)
                store_dft(CHUNKS - 1, 1, 1)
                barrier(dve, b, 2)

                stats(1)

                def weights_low(j):
                    dve.wait_ge(s_wh, b * 8 + j + 1)
                    dve.scalar_tensor_tensor(W16[j % 2][:, :, 1, :], WM[j % 2], WSCALE, W16[j % 2][:, :, 0, :],
                                             ALU.mult, ALU.subtract).then_inc(s_wl, 1)

                def store_image_dft(half):
                    dve.wait_ge(s_fg, 2 + b * 8 + 4 * half + 4)
                    dve.tensor_copy(both_dft[:, 512 * half:512 * half + 512], bank(4 + half)).then_inc(s_bd, 1)

                def mixed_sum(half):
                    dve.wait_ge(s_ol, b * 2 + half + 1)
                    dve.scalar_tensor_tensor(om[:, 8 * half:8 * half + 8], mixed(half)[:, :, :, 0:2], 1.0 / WSCALE,
                                             om_low[:, 8 * half:8 * half + 8], ALU.mult, ALU.add).then_inc(s_oms, 1)

                weights_low(0)
                store_image_dft(0)
                weights_low(1)
                store_image_dft(1)
                dve.wait_ge(s_ff, b + 1)
                F = bank(2).rearrange("p (y t n) -> p t y n", t=2, n=MODES)
                V = DV.rearrange("p t (y n) -> p t y n", n=MODES)
                lo, up = slice(0, C), slice(C, P)
                dve.tensor_scalar(V[lo, 0], F[lo, 0], rs[lo, :], None, ALU.mult).then_inc(s_dv, 1)
                dve.tensor_scalar(V[lo, 1], F[lo, 1], rs[lo, :], None, ALU.mult).then_inc(s_dv, 1)
                dve.tensor_scalar(V[up, 0], F[up, 1], rs[up, :], -1.0, ALU.mult, ALU.mult).then_inc(s_dv, 1)
                dve.tensor_scalar(V[up, 1], F[up, 0], rs[up, :], None, ALU.mult).then_inc(s_dv, 1)
                dve.wait_ge(s_dv, b * 8 + 4)
                dve.scalar_tensor_tensor(DV[lo, 0, 0:1], nb[lo, :], float(W), DV[lo, 0, 0:1], ALU.mult, ALU.add).then_inc(s_dv, 1)
                dve.scalar_tensor_tensor(DV[up, 1, 0:1], nb[up, :], float(W), DV[up, 1, 0:1], ALU.mult, ALU.add).then_inc(s_dv, 1)
                dve.wait_ge(s_dv, b * 8 + 6)
                dve.tensor_copy(DV16[:, 0:2, :], DV).then_inc(s_dv, 1)
                dve.wait_ge(s_dv, b * 8 + 7)
                dve.tensor_tensor(DV16[:, 2:4, :], DV, DV16[:, 0:2, :], ALU.subtract).then_inc(s_dv, 1)
                for j in range(2, 6):
                    weights_low(j)
                mixed_sum(0)
                weights_low(6)
                weights_low(7)
                mixed_sum(1)
                dve.wait_ge(s_ot, b + 1)
                for s in range(2):
                    for yh in range(2):
                        dve.wait_ge(s_oth, b * 4 + 2 * s + yh + 1)
                        dve.tensor_tensor(modes_out(1, s, yh), modes_in(s, yh), modes_out(0, s, yh), ALU.subtract)
                barrier(dve, b, 3)

                def low_modes(z, g):
                    dve.wait_ge(s_zc, b * 32 + z * 8 + g + 1)
                    dve.tensor_tensor(block_out(z, 1, g), block_in(g), block_out(z, 0, g), ALU.subtract).then_inc(s_zl, 1)

                def add_synthesis(z, m):
                    at = (z * 16 + m) * 512
                    dve.wait_ge(s_yp, (b * 4 + z) * 16 + m + 2)
                    dve.scalar_tensor_tensor(X[:, at:at + 512], bank(2 + m % 4), 1.0 / YSCALE, X[:, at:at + 512],
                                             ALU.mult, ALU.add).then_inc(s_x2, 1)

                def measure_x2(z, m):
                    dve.wait_ge(s_x2, 4 + (b * 4 + z) * 16 + m + 1)
                    at = z * 16 + m
                    measure(X[:, at * 512:(at + 1) * 512], at * 6)

                for g in range(8):
                    low_modes(0, g)
                for z in range(4):
                    for m in range(0, 16, 2):
                        add_synthesis(z, m)
                        add_synthesis(z, m + 1)
                        measure_x2(z, m)
                        if z < 3:
                            low_modes(z + 1, m // 2)
                        measure_x2(z, m + 1)
                barrier(dve, b, 4)

                stats(2)

                def maximum(n, hh, t2):
                    dve.wait_ge(s_sc, 2 * n + t2 + 1)
                    dve.tensor_reduce(negmax[:, hh, t2:t2 + 1], bank(2 * hh + t2), AX.X,
                                      ALU.max, negate=True).then_inc(s_mx, 1)

                def scale_maximum(n, hh, t2):
                    dve.wait_ge(s_mx, 2 * n + t2 + 1)
                    dve.tensor_scalar(negsharp[:, hh, t2:t2 + 1], negmax[:, hh, t2:t2 + 1], SHARP, None,
                                      ALU.mult).then_inc(s_mxs, 1)

                def vector_steps(i, first, last):
                    k0, unit0, quarter0 = (b * 16 + i) * 16, (b * 16 + i) * 8, (b * 16 + i) * 4

                    def add_codes(k):
                        dve.wait_ge(s_cd, 2 + unit0 + k // 2 + 1)
                        at = 2 * i * 1024 + (k // 4) * 512
                        dve.scalar_tensor_tensor(X[:, ds(at, 512)], bank(6 + k // 4 % 2), 1.0 / CSCALE,
                                                 X[:, ds(at, 512)], ALU.mult, ALU.add).then_inc(s_x3, 1)

                    def measure_codes(k):
                        dve.wait_ge(s_x3, 2 + quarter0 + k // 4 + 1)
                        measure(X[:, ds(2 * i * 1024 + (k // 4) * 512, 512)], (2 * i * 2 + k // 4) * 6)

                    for k in range(16):
                        hh, q = k % 2, k // 2 % 2
                        ahead = not (last and k >= 14)
                        if ahead:
                            maximum(k0 + k + 2, hh, 0)
                            maximum(k0 + k + 2, hh, 1)
                            scale_maximum(k0 + k + 2, hh, 0)
                        if hh == 0:
                            dve.wait_ge(s_oht, 2 + k0 + k + 1)
                            dve.wait_ge(s_cd, unit0 + k // 2 + 1)
                            dve.tensor_copy(OTs[q][:, :, 0:256],
                                            bank(4).bitcast(F16).rearrange("p (k n) -> p k n", k=4)).then_inc(s_ocd, 1)
                        elif k % 4 == 3 and not (first and k == 3):
                            add_codes(k - 4)
                        elif k % 4 == 1 and not (first and k <= 5):
                            measure_codes(k - 6)
                        if ahead:
                            scale_maximum(k0 + k + 2, hh, 1)
                    if last:
                        measure_codes(11)
                        add_codes(15)
                        measure_codes(15)

                for u in range(2):
                    dve.tensor_scalar(XN[u], X[:, u * 1024:u * 1024 + 1024], rs, nb, ALU.mult, ALU.add).then_inc(s_xn, 2)
                for u in range(2):
                    dve.wait_ge(s_xn, 2 * (b * 32 + u) + 2)
                    dve.wait_ge(s_xh, b * 32 + u + 1)
                    dve.tensor_tensor(XL[u], XN[u], XH[u], ALU.subtract).then_inc(s_xl, 1)
                for k in range(2):
                    for t2 in range(2):
                        maximum(b * 256 + k, k, t2)
                        scale_maximum(b * 256 + k, k, t2)
                vector_steps(0, True, False)
                with dve.Fori(1, 15) as i:
                    vector_steps(i, False, False)
                vector_steps(15, False, True)
                barrier(dve, b, 5)

                stats(3)

                def residuals(i, last):
                    for u in range(2):
                        c = b * CHUNKS + 2 * i + u
                        for m in range(4):
                            n = c * 4 + m
                            dve.wait_ge(s_cv, n + 5)
                            dve.wait_ge(s_ct, n + 1)
                            k0 = ((2 * i + u) * 8 + 4 * (m // 2)) * 2 + m % 2
                            X4 = X[:, :].rearrange("p (k n) -> p k n", n=P)
                            src = bank(m).rearrange("p (k n) -> p k n", n=P)
                            dst = res[m].rearrange("p (k n) -> p k n", n=P)
                            dve.scalar_tensor_tensor(dst[0:C], src[0:C], cbias[0:C, :],
                                                     X4[0:C, ds(k0 + 2, 4, 2), :], ALU.add, ALU.add)
                            dve.scalar_tensor_tensor(dst[C:P], src[C:P], cbias[C:P, :],
                                                     X4[C:P, ds(k0, 4, 2), :], ALU.add, ALU.add).then_inc(s_rs, 1)
                            if m == 1 and not last:
                                dve.wait_ge(s_nl, c + 2)
                                normalise((2 * i + u + 2) * 2048)

                def normalise(at):
                    dve.tensor_scalar(XM, X[:, ds(at, 2048)], rs, nb, ALU.mult, ALU.add).then_inc(s_nn, 1)

                normalise(0)
                dve.wait_ge(s_nn, b * CHUNKS + 1)
                dve.wait_ge(s_nh, b * CHUNKS + 1)
                dve.tensor_tensor(NL[0][:, 1:9, :, 2:130], XM.rearrange("p (k j n) -> p k j n", j=2, n=P),
                                  NH[0][:, 1:9, :, 2:130], ALU.subtract).then_inc(s_nl, 1)
                dve.wait_ge(s_nl, b * CHUNKS + 1)
                dve.wait_ge(s_pad, 2 * b + 2)
                past(dve)
                for buf in (NH, NL):
                    dve.tensor_copy(buf[0][:, 0, :, :], buf[1][:, 8, :, :])
                    t = dve.tensor_copy(buf[0][:, 1:9, 1, 0:1], buf[0][:, 1:9, 1, 129:130])
                t.then_inc(s_cp, 1)
                normalise(2048)
                with dve.Fori(0, 7) as i:
                    residuals(i, False)
                residuals(7, True)
                dve.wait_ge(s_cv, (b * CHUNKS + 16) * 4 + 4)
                dve.wait_ge(s_cp, b * 17 + 17)
                for buf in (NH, NL):
                    dve.tensor_copy(buf[0][:, 0, :, :], buf[1][:, 8, :, :])
                    t = dve.memset(buf[0][:, 1, :, :], 0.0)
                t.then_inc(s_cp, 1)
                dve.wait_ge(s_e, b * 5 + 1)
                dve.scalar_tensor_tensor(edge[0:C, :], bank(6)[0:C, 0:PAIR], cbias[0:C, :], X[0:C, 0:PAIR],
                                         ALU.add, ALU.add).then_inc(s_e, 1)
                dve.memset(edge[C:P, :], 0.0).then_inc(s_e, 1)
                barrier(dve, b, 6)

        @block.gpsimd
        def _(pool):
            pool.wait_ge(s_prep, 13)
            pool.wait_ge(s_const, 16 * (len(CONSTS) + 2))
            with pool.Fori(0, B) as b:
                with pool.Fori(0, 8) as c2:
                    for u in range(2):
                        c = b * CHUNKS + 2 * c2 + u
                        pool.wait_ge(s_tile[u], 96 * (b * 8 + c2 + 1))
                        for j in range(2):
                            pool.wait_ge(s_wa, c * 2 + j + 1)
                            pool.tensor_tensor(ta[:, j], T[u][:, j, 1:16:2, :], T[u][:, j, 3:18:2, :],
                                               ALU.add).then_inc(s_padd, 1)
                            pool.tensor_tensor(tb[:, j], T[u][:, j, 0:15:2, :], T[u][:, j, 4:19:2, :],
                                               ALU.add).then_inc(s_padd, 1)
                barrier(pool, b, 0)
                barrier(pool, b, 1)

                def interpolate(n, at, u):
                    a = R1[:, ds(at, 256)].rearrange("p (k o) -> p k o", o=C)
                    a1 = R1[:, ds(at + C, 256)].rearrange("p (k o) -> p k o", o=C)
                    pool.tensor_tensor(syn[:, :, 0, :], a, a, ALU.add)
                    pool.tensor_tensor(syn[:, :, 1, :], a, a1, ALU.add).then_inc(s_si, 1)
                    pool.wait_ge(s_sh, n + 1)
                    pool.tensor_tensor(syn_lo[u], syn, syn_hi[u], ALU.subtract).then_inc(s_sy, 1)
                    pool.wait_ge(s_sy, n + 1)
                    past(pool)

                interpolate(b * 32, 0, 0)
                interpolate(b * 32 + 1, 256, 1)
                with pool.Fori(0, CHUNKS - 1) as c:
                    for u in range(2):
                        interpolate((b * CHUNKS + c) * 2 + u + 2, c * 512 + 512 + 256 * u, u)
                barrier(pool, b, 2)
                barrier(pool, b, 3)
                barrier(pool, b, 4)
                for u in range(2):
                    for q in range(2):
                        t = pool.memset(HQ[u][q][C:C + 32, :], 1.0)
                t.then_inc(s_pad, 1)
                pool.wait_ge(s_pad, 2 * b + 1)
                pool.wait_ge(s_st, st_base(b, 2) + NST)
                past(pool)

                def low(n, at, u):
                    pool.tensor_tensor(XN[u], X[:, ds(at, 1024)], wide(rs, 1024), ALU.mult).then_inc(s_xn, 1)
                    pool.wait_ge(s_xn, 2 * n + 1)
                    past(pool)
                    pool.tensor_scalar(XN[u], XN[u], nb, None, ALU.add).then_inc(s_xn, 1)
                    pool.wait_ge(s_xn, 2 * n + 2)
                    pool.wait_ge(s_xh, n + 1)
                    pool.tensor_tensor(XL[u], XN[u], XH[u], ALU.subtract).then_inc(s_xl, 1)

                with pool.Fori(0, 15) as i:
                    for u in range(2):
                        pool.wait_ge(s_hl[u], 96 * (b * 16 + i + 1))
                        past(pool)
                        low(b * 32 + 2 * i + u + 2, (2 * i + u + 2) * 1024, u)
                barrier(pool, b, 5)
                for buf in (NH, NL):
                    for u in range(2):
                        pool.memset(buf[u][:, :, :, 0:2], 0.0)
                    t = pool.memset(buf[1][:, 8, :, 2:130], 0.0)
                t.then_inc(s_pad, 1)
                pool.wait_ge(s_pad, 2 * b + 2)

                def conv_low(n, u, edges):
                    pool.wait_ge(s_nn, n + 1)
                    pool.wait_ge(s_nh, n + 1)
                    pool.tensor_tensor(NL[u][:, 1:9, :, 2:130], XM.rearrange("p (k j n) -> p k j n", j=2, n=P),
                                       NH[u][:, 1:9, :, 2:130], ALU.subtract).then_inc(s_nl, 1)
                    pool.wait_ge(s_nl, n + 1)
                    pool.wait_ge(s_cp, edges)
                    past(pool)
                    for buf in (NH, NL):
                        pool.tensor_copy(buf[u][:, 0, :, :], buf[1 - u][:, 8, :, :])
                        t = pool.tensor_copy(buf[u][:, 1:9, 1, 0:1], buf[u][:, 1:9, 1, 129:130])
                    t.then_inc(s_cp, 1)

                conv_low(b * CHUNKS + 1, 1, b * 17 + 2)
                with pool.Fori(0, 7) as i:
                    for u in range(2):
                        conv_low(b * CHUNKS + 2 * i + u + 2, u, b * 17 + 2 * i + u + 3)
                barrier(pool, b, 6)

    return nc


def cdf53(n, level):
    cur = np.eye(n)
    for _ in range(level):
        e, o = cur[0::2], cur[1::2]
        d = o - 0.5 * (e + np.roll(e, -1, 0))
        s = e + 0.25 * (d + np.roll(d, 1, 0))
        cur, high = s, d
    return np.concatenate([cur, high])


def uncdf53(s, d):
    e = s - 0.25 * (d + np.roll(d, 1, 0))
    o = d + 0.5 * (e + np.roll(e, -1, 0))
    return np.stack([e, o], 1).reshape(2 * len(e), -1)


def shape_constants():
    f32 = np.float32
    a = cdf53(W, 2) / 4.0
    w_analysis = a.reshape(P, P, 2).transpose(1, 2, 0)
    low, high = np.eye(P)[:C], np.eye(P)[C:]
    s = uncdf53(low, high)
    s = uncdf53(s, np.zeros_like(s)) / 2.0
    w_synthesis = s.reshape(P, 2, P).transpose(2, 1, 0).reshape(P, 2 * P)
    k, m = np.arange(W), np.arange(MODES)
    ang = 2 * np.pi * np.outer(k, m) / W
    cos, sin = np.cos(ang), np.sin(ang)
    dft_w = np.stack([cos, -sin], 2).reshape(P, 2, 2 * MODES).astype(f32)
    high = dft_w.astype(np.float16)
    dft_w = np.concatenate([high, (dft_w - high).astype(np.float16)], 2)
    c2, s2 = cos.reshape(P, 2, MODES), sin.reshape(P, 2, MODES)
    dft_h = np.stack([np.concatenate([c2, -s2], 2), np.concatenate([s2, c2], 2)], 2).reshape(P, 4, 2 * MODES) / W
    idft_h = np.stack([cos, -sin], 2).reshape(W, 2 * MODES).T.astype(f32)
    high = idft_h.astype(np.float16)
    idft_h = np.concatenate([high, high, (idft_h - high).astype(np.float16)])
    twice = np.where(m == 0, 1.0, 2.0)[:, None] / W
    order = k.reshape(P, 2).T.reshape(-1)
    eye, none = np.eye(C), np.zeros((C, C))
    fold = np.stack([np.concatenate(v) for v in ((eye, none), (eye, none), (none, eye), (none, eye), (eye, eye))], 1)
    idft_w = (np.concatenate([cos.T * twice, -sin.T * twice])[:, order] * YSCALE).astype(f32)
    high = idft_w.astype(np.float16)
    idft_w = np.concatenate([high, high, (idft_w - high).astype(np.float16)])
    pair = np.arange(P) % C // 2
    group = (pair[:, None] == pair[None, :]) / 4.0
    return {"ident": np.eye(P, dtype=f32), "group": group.astype(f32), "fold": fold.astype(f32), "w_analysis": w_analysis.astype(f32),
            "w_synthesis": w_synthesis.astype(np.float16), "dft_w": dft_w, "dft_h": dft_h.astype(f32),
            "idft_h": idft_h, "idft_w": idft_w}


def two_blocks(a, b):
    out = np.zeros((2 * C, 2 * C), a.dtype)
    out[:C, :C] = a
    out[C:, C:] = b
    return out


def kernel(x, L0_conv_w_approx, L0_conv_w_detail, L0_conv_dense_kernel, L0_conv_dense_bias,
           L1_conv_weights_real, L1_conv_weights_imag, L2_conv_codebook, L3_conv_kernel, L3_conv_bias):
    import concourse.bacc as bacc
    from concourse.bass_utils import run_bass_kernel_spmd as run

    x = np.ascontiguousarray(x)
    det = np.asarray(L0_conv_w_detail)
    both = np.concatenate([np.asarray(L1_conv_weights_real), np.asarray(L1_conv_weights_imag)])
    modes = both.transpose(0, 3, 2, 1).reshape(P, MODES * MODES, C)
    book = np.asarray(L2_conv_codebook)
    taps = np.asarray(L3_conv_kernel).transpose(2, 3, 1, 0)
    conv = np.zeros((P, 6, P), np.float32)
    for half, row in ((0, 2), (1, 1)):
        for pr in range(2):
            for q in range(2):
                back = row - (2 * (pr - 1) + q)
                if 1 <= back <= 3:
                    for t in range(3):
                        conv[q * C:(q + 1) * C, pr * 3 + t, half * C:(half + 1) * C] = taps[back - 1, t]
    twice = lambda v: np.ascontiguousarray(np.concatenate([np.asarray(v).reshape(C, 1)] * 2))
    arrays = {
        "x": x,
        "dense": two_blocks(np.asarray(L0_conv_dense_kernel), np.asarray(L0_conv_dense_kernel)),
        "dense_bias": twice(L0_conv_dense_bias),
        "mix_low": two_blocks(np.asarray(L0_conv_w_approx)[:, :, 0, 0], det[..., 0]),
        "mix_high": two_blocks(det[..., 1], det[..., 2]),
        "modes": np.ascontiguousarray(modes),
        "codes": np.ascontiguousarray(book.reshape(4, P, C).transpose(1, 0, 2)),
        "codes_t": np.ascontiguousarray(np.concatenate([book.T, book.T])),
        "conv": conv,
        "conv_bias": twice(L3_conv_bias),
        **shape_constants(),
    }
    nc = bacc.Bacc("TRN2", target_bir_lowering=False, num_devices=1)
    args = {}
    for name, a in arrays.items():
        arrays[name] = a = np.ascontiguousarray(a)
        args[name] = nc.dram_tensor(name, a.shape, mybir.dt.from_np(a.dtype), kind="ExternalInput").ap()
    out = nc.dram_tensor("out", x.shape, F32, kind="ExternalOutput").ap()
    fused_layers(nc, out=out, **args)
    r = run(nc, [arrays], core_ids=[0])
    return r.results[0]["out"]
```
